# Optimizing a Trainium2 kernel written in Bass

```python
import numpy as np
import jax
import jax.numpy as jnp

def _softmax(x, axis=-1):
    return jax.nn.softmax(x, axis=axis)

def _gelu(x):
    return jax.nn.gelu(x, approximate=True)

def _silu(x):
    return jax.nn.silu(x)

def _sigmoid(x):
    return jax.nn.sigmoid(x)

def _layernorm(x, axis=-1, eps=1e-05):
    m = jnp.mean(x, axis=axis, keepdims=True)
    v = jnp.var(x, axis=axis, keepdims=True)
    return (x - m) / jnp.sqrt(v + eps)

def _scatter_add(tgt, idx, src, axis=0):
    return tgt.at[idx].add(src)

def _segment_sum(src, seg, n):
    return jax.ops.segment_sum(src, seg, n)
kernel_name = 'mk_flamingo_gated_d4_seqx_r8_df0997'

def setup_inputs(seed: int=0):
    np.random.seed(seed)
    _w = jnp.asarray

    def _rec_inputs():
        import jax
        import jax.numpy as jnp
        _rk = jax.random.key(seed)
        x = -0.0002928 + 1 * jax.random.normal(jax.random.fold_in(_rk, 1), (8, 256, 128), jnp.float32)
        _lenS = 256 - jax.random.randint(jax.random.fold_in(_rk, 7), (8,), 0, max(1, 256 // 4) + 1, jnp.int32)
        _lenS2 = 256 - jax.random.randint(jax.random.fold_in(_rk, 8), (8,), 0, max(1, 256 // 4) + 1, jnp.int32)
        _ctx_1024P = jax.random.normal(jax.random.fold_in(_rk, 11), (8, 16, 128), jnp.float32)
        _ctx_1024c = jax.random.dirichlet(jax.random.fold_in(_rk, 511), 0.3 * jnp.ones((16,), jnp.float32), (8, 256))
        _ctx_1024t = jnp.einsum('bsk,bkd->bsd', _ctx_1024c, _ctx_1024P)
        _ctx_1024t = _ctx_1024t * jax.lax.rsqrt(jnp.mean(jnp.square(_ctx_1024t)) + 1e-12) * 0.953939
        ctx_1024 = -1.39393e-06 + 0.999914 * (_ctx_1024t + 0.3 * jax.random.normal(jax.random.fold_in(_rk, 611), (8, 256, 128), jnp.float32))
        _g = jax.random.normal(jax.random.fold_in(_rk, 9001), (2, 4), jnp.float32)
        _g = jnp.sign(_g) * jnp.maximum(jnp.abs(_g), 1.0) + (_g == 0) * 1.0
        g_xattn = _g[0]
        g_ffn = _g[1]
        return (x, ctx_1024, g_xattn, g_ffn)
    x, ctx_1024, g_xattn, g_ffn = _rec_inputs()

    def _L0_xattn_setup():
        import jax, jax.numpy as jnp
        import numpy as np
        D_MODEL = 128
        N_HEADS = 16
        D_HEAD = D_MODEL // N_HEADS
        WINDOW = 128

        def _heads(x):
            B, S, _ = x.shape
            return x.reshape(B, S, N_HEADS, D_HEAD).transpose(0, 2, 1, 3)
        key = jax.random.key(seed)
        ks = jax.random.split(key, 11)
        B, S = (1, 512)
        s = 1.0 / np.sqrt(D_MODEL)
        return {'query': jax.random.normal(ks[0], (B, S, D_MODEL), jnp.float32), 'key': jax.random.normal(ks[1], (B, S, D_MODEL), jnp.float32), 'value': jax.random.normal(ks[2], (B, S, D_MODEL), jnp.float32), 'Wq': jax.random.normal(ks[3], (D_MODEL, D_MODEL), jnp.float32) * s, 'bq': jnp.zeros((D_MODEL,), jnp.float32), 'Wk': jax.random.normal(ks[4], (D_MODEL, D_MODEL), jnp.float32) * s, 'bk': jnp.zeros((D_MODEL,), jnp.float32), 'Wv': jax.random.normal(ks[5], (D_MODEL, D_MODEL), jnp.float32) * s, 'bv': jnp.zeros((D_MODEL,), jnp.float32), 'Wo': jax.random.normal(ks[6], (D_MODEL, D_MODEL), jnp.float32) * s, 'bo': jnp.zeros((D_MODEL,), jnp.float32)}
    _L0_xattn_all = _L0_xattn_setup()
    _L0_xattn_in = {k: v for k, v in _L0_xattn_all.items() if k in ('Wq', 'bq', 'Wk', 'bk', 'Wv', 'bv', 'Wo', 'bo')}
    del _L0_xattn_all

    def _L0_ffn_setup():
        import jax, jax.numpy as jnp
        import numpy as np
        B, S, H = (4, 256, 128)
        E = 8
        GS = 2
        NG = E // GS
        F = int(H * 4 * (2.0 / 3.0))
        key = jax.random.key(seed)
        ks = jax.random.split(key, 7)
        sc_h = 1.0 / np.sqrt(H)
        sc_f = 1.0 / np.sqrt(F)
        return {'x': jax.random.normal(ks[0], (B, S, H), dtype=jnp.float32), 'Wr': jax.random.normal(ks[1], (H, E), dtype=jnp.float32) * sc_h, 'br': jnp.zeros((E,), dtype=jnp.float32), 'W_up': jax.random.normal(ks[2], (NG, H, F), dtype=jnp.float32) * sc_h, 'b_up': jax.random.normal(ks[3], (NG, F), dtype=jnp.float32) * 0.01, 'W_down': jax.random.normal(ks[4], (E, F, H), dtype=jnp.float32) * sc_f, 'b_down': jax.random.normal(ks[5], (E, H), dtype=jnp.float32) * 0.01}
    _L0_ffn_all = _L0_ffn_setup()
    _L0_ffn_in = {k: v for k, v in _L0_ffn_all.items() if k in ('Wr', 'br', 'W_up', 'b_up', 'W_down', 'b_down')}
    del _L0_ffn_all

    def _L1_xattn_setup():
        import jax, jax.numpy as jnp
        import numpy as np
        DIM = 128
        NUM_HEADS = 16
        DIM_HEAD = 64
        INNER = NUM_HEADS * DIM_HEAD
        SCALE = DIM_HEAD ** (-0.5)

        def _layernorm(x, gamma, beta, eps=1e-05):
            mu = jnp.mean(x, axis=-1, keepdims=True)
            var = jnp.mean(jnp.square(x - mu), axis=-1, keepdims=True)
            return (x - mu) * jax.lax.rsqrt(var + eps) * gamma + beta
        key = jax.random.key(seed)
        ks = jax.random.split(key, 8)
        B, SQ, SK = (2, 256, 512)
        x = jax.random.normal(ks[0], (B, SQ, DIM), dtype=jnp.float32)
        context = jax.random.normal(ks[1], (B, SK, DIM), dtype=jnp.float32)
        ln_gamma = jnp.ones((DIM,), jnp.float32)
        ln_beta = jnp.zeros((DIM,), jnp.float32)
        w_q = jax.random.normal(ks[2], (DIM, INNER), dtype=jnp.float32) / np.sqrt(DIM)
        w_kv = jax.random.normal(ks[3], (DIM, 2 * INNER), dtype=jnp.float32) / np.sqrt(DIM)
        w_out = jax.random.normal(ks[4], (INNER, DIM), dtype=jnp.float32) / np.sqrt(INNER)
        b_out = jnp.zeros((DIM,), jnp.float32)
        gate = jnp.array([0.5], jnp.float32)
        return {'x': x, 'context': context, 'ln_gamma': ln_gamma, 'ln_beta': ln_beta, 'w_q': w_q, 'w_kv': w_kv, 'w_out': w_out, 'b_out': b_out, 'gate': gate}
    _L1_xattn_all = _L1_xattn_setup()
    _L1_xattn_in = {k: v for k, v in _L1_xattn_all.items() if k in ('ln_gamma', 'ln_beta', 'w_q', 'w_kv', 'w_out', 'b_out', 'gate')}
    del _L1_xattn_all

    def _L1_ffn_setup():
        import jax, jax.numpy as jnp
        import numpy as np
        EPS = 1e-06
        LN_EPS = 1e-05

        def _absmean_core(W):
            gamma = jnp.mean(jnp.abs(W)) + EPS
            Ws = W / gamma
            Wq = jnp.sign(Ws) * jnp.minimum(jnp.round(jnp.abs(Ws)), 1.0)
            return (Wq, gamma)

        @jax.custom_vjp
        def absmean(W):
            return _absmean_core(W)[0]

        def _absmean_fwd(W):
            Wq, gamma = _absmean_core(W)
            return (Wq, gamma)

        def _absmean_bwd(gamma, g):
            return (g / gamma,)
        absmean.defvjp(_absmean_fwd, _absmean_bwd)

        def layernorm(x, w, b, eps=LN_EPS):
            mu = jnp.mean(x, axis=-1, keepdims=True)
            var = jnp.mean((x - mu) ** 2, axis=-1, keepdims=True)
            return (x - mu) * jax.lax.rsqrt(var + eps) * w + b
        key = jax.random.key(seed)
        k1, k2, k3 = jax.random.split(key, 3)
        d, h = (128, 512)
        B, T = (8, 256)
        return {'x': jax.random.normal(k1, (B, T, d), jnp.float32), 'W_fc': jax.random.normal(k2, (h, d), jnp.float32), 'ln_w': jnp.ones((h,), jnp.float32), 'ln_b': jnp.zeros((h,), jnp.float32), 'W_proj': jax.random.normal(k3, (d, h), jnp.float32)}
    _L1_ffn_all = _L1_ffn_setup()
    _L1_ffn_in = {k: v for k, v in _L1_ffn_all.items() if k in ('W_fc', 'ln_w', 'ln_b', 'W_proj')}
    del _L1_ffn_all

    def _L2_xattn_setup():
        import jax, jax.numpy as jnp
        import numpy as np
        D_MODEL = 128
        N_HEADS = 16
        BATCH = 2
        SEQ = 256

        def _rope(x):
            d = x.shape[-1]
            half = d // 2
            seq = x.shape[-2]
            pos = jnp.arange(seq, dtype=jnp.float32)
            theta = 1.0 / 10000.0 ** (2.0 * jnp.arange(half, dtype=jnp.float32) / d)
            ang = pos[:, None] * theta[None, :]
            sin, cos = (jnp.sin(ang), jnp.cos(ang))
            x1 = x[..., 0::2]
            x2 = x[..., 1::2]
            r1 = x1 * cos - x2 * sin
            r2 = x1 * sin + x2 * cos
            return jnp.stack([r1, r2], axis=-1).reshape(x.shape)
        key = jax.random.key(seed)
        ks = jax.random.split(key, 8)
        s = 1.0 / np.sqrt(D_MODEL)
        return {'q': jax.random.normal(ks[0], (BATCH, SEQ, D_MODEL), jnp.float32), 'k': jax.random.normal(ks[1], (BATCH, SEQ, D_MODEL), jnp.float32), 'v': jax.random.normal(ks[2], (BATCH, SEQ, D_MODEL), jnp.float32), 'Wq': jax.random.normal(ks[3], (D_MODEL, D_MODEL), jnp.float32) * s, 'Wk': jax.random.normal(ks[4], (D_MODEL, D_MODEL), jnp.float32) * s, 'Wv': jax.random.normal(ks[5], (D_MODEL, D_MODEL), jnp.float32) * s, 'Wp': jax.random.normal(ks[6], (D_MODEL, D_MODEL), jnp.float32) * s, 'bp': jax.random.normal(ks[7], (D_MODEL,), jnp.float32) * s}
    _L2_xattn_all = _L2_xattn_setup()
    _L2_xattn_in = {k: v for k, v in _L2_xattn_all.items() if k in ('Wq', 'Wk', 'Wv', 'Wp', 'bp')}
    del _L2_xattn_all

    def _L2_ffn_setup():
        import jax, jax.numpy as jnp
        import numpy as np
        B, S, D, F, E = (4, 256, 128, 512, 8)
        key = jax.random.key(seed)
        ks = jax.random.split(key, 7)
        s1 = 1.0 / np.sqrt(D)
        s2 = 1.0 / np.sqrt(F)
        x = jax.random.normal(ks[0], (B, S, D), dtype=jnp.float32)
        W1 = jax.random.uniform(ks[1], (E, D, F), jnp.float32, -s1, s1)
        b1 = jax.random.uniform(ks[2], (E, F), jnp.float32, -s1, s1)
        W2 = jax.random.uniform(ks[3], (E, F, D), jnp.float32, -s2, s2)
        b2 = jax.random.uniform(ks[4], (E, D), jnp.float32, -s2, s2)
        Wr = jax.random.uniform(ks[5], (D, E), jnp.float32, -s1, s1)
        br = jax.random.uniform(ks[6], (E,), jnp.float32, -s1, s1)
        return {'x': x, 'W1': W1, 'b1': b1, 'W2': W2, 'b2': b2, 'Wr': Wr, 'br': br}
    _L2_ffn_all = _L2_ffn_setup()
    _L2_ffn_in = {k: v for k, v in _L2_ffn_all.items() if k in ('W1', 'b1', 'W2', 'b2', 'Wr', 'br')}
    del _L2_ffn_all

    def _L3_xattn_setup():
        import jax, jax.numpy as jnp
        import numpy as np
        B, T, N_EMBD, N_HEAD = (2, 256, 128, 16)
        HEAD = N_EMBD // N_HEAD
        WINDOW = 64
        key = jax.random.key(seed)
        kq, kk, kv, kw = jax.random.split(key, 4)
        q = jax.random.normal(kq, (B, T, N_EMBD), dtype=jnp.float32)
        k = jax.random.normal(kk, (B, T, N_EMBD), dtype=jnp.float32)
        v = jax.random.normal(kv, (B, T, N_EMBD), dtype=jnp.float32)
        W_proj = jax.random.normal(kw, (N_EMBD, N_EMBD), dtype=jnp.float32) * (1.0 / np.sqrt(N_EMBD))
        b_proj = jnp.zeros((N_EMBD,), dtype=jnp.float32)
        return {'q': q, 'k': k, 'v': v, 'W_proj': W_proj, 'b_proj': b_proj}
    _L3_xattn_all = _L3_xattn_setup()
    _L3_xattn_in = {k: v for k, v in _L3_xattn_all.items() if k in ('W_proj', 'b_proj')}
    del _L3_xattn_all

    def _L3_ffn_setup():
        import jax, jax.numpy as jnp
        import numpy as np
        B, S, D = (2, 512, 128)
        H = 512
        E = 8
        K = 4
        key = jax.random.key(seed)
        kx, kr, ku, kd = jax.random.split(key, 4)
        x = jax.random.normal(kx, (B, S, D), dtype=jnp.float32)
        router_w = jax.random.normal(kr, (D, E), dtype=jnp.float32) / np.sqrt(D)
        up_w = jax.random.normal(ku, (E, D, H), dtype=jnp.float32) / np.sqrt(D)
        down_w = jax.random.normal(kd, (E, H, D), dtype=jnp.float32) / np.sqrt(H)
        return {'x': x, 'router_w': router_w, 'up_w': up_w, 'down_w': down_w}
    _L3_ffn_all = _L3_ffn_setup()
    _L3_ffn_in = {k: v for k, v in _L3_ffn_all.items() if k in ('router_w', 'up_w', 'down_w')}
    del _L3_ffn_all
    return {'x': x, 'ctx_1024': ctx_1024, 'g_xattn': g_xattn, 'g_ffn': g_ffn, 'L0_xattn_Wq': _L0_xattn_in['Wq'], 'L0_xattn_bq': _L0_xattn_in['bq'], 'L0_xattn_Wk': _L0_xattn_in['Wk'], 'L0_xattn_bk': _L0_xattn_in['bk'], 'L0_xattn_Wv': _L0_xattn_in['Wv'], 'L0_xattn_bv': _L0_xattn_in['bv'], 'L0_xattn_Wo': _L0_xattn_in['Wo'], 'L0_xattn_bo': _L0_xattn_in['bo'], 'L0_ffn_Wr': _L0_ffn_in['Wr'], 'L0_ffn_br': _L0_ffn_in['br'], 'L0_ffn_W_up': _L0_ffn_in['W_up'], 'L0_ffn_b_up': _L0_ffn_in['b_up'], 'L0_ffn_W_down': _L0_ffn_in['W_down'], 'L0_ffn_b_down': _L0_ffn_in['b_down'], 'L1_xattn_ln_gamma': _L1_xattn_in['ln_gamma'], 'L1_xattn_ln_beta': _L1_xattn_in['ln_beta'], 'L1_xattn_w_q': _L1_xattn_in['w_q'], 'L1_xattn_w_kv': _L1_xattn_in['w_kv'], 'L1_xattn_w_out': _L1_xattn_in['w_out'], 'L1_xattn_b_out': _L1_xattn_in['b_out'], 'L1_xattn_gate': _L1_xattn_in['gate'], 'L1_ffn_W_fc': _L1_ffn_in['W_fc'], 'L1_ffn_ln_w': _L1_ffn_in['ln_w'], 'L1_ffn_ln_b': _L1_ffn_in['ln_b'], 'L1_ffn_W_proj': _L1_ffn_in['W_proj'], 'L2_xattn_Wq': _L2_xattn_in['Wq'], 'L2_xattn_Wk': _L2_xattn_in['Wk'], 'L2_xattn_Wv': _L2_xattn_in['Wv'], 'L2_xattn_Wp': _L2_xattn_in['Wp'], 'L2_xattn_bp': _L2_xattn_in['bp'], 'L2_ffn_W1': _L2_ffn_in['W1'], 'L2_ffn_b1': _L2_ffn_in['b1'], 'L2_ffn_W2': _L2_ffn_in['W2'], 'L2_ffn_b2': _L2_ffn_in['b2'], 'L2_ffn_Wr': _L2_ffn_in['Wr'], 'L2_ffn_br': _L2_ffn_in['br'], 'L3_xattn_W_proj': _L3_xattn_in['W_proj'], 'L3_xattn_b_proj': _L3_xattn_in['b_proj'], 'L3_ffn_router_w': _L3_ffn_in['router_w'], 'L3_ffn_up_w': _L3_ffn_in['up_w'], 'L3_ffn_down_w': _L3_ffn_in['down_w']}

def reference(x, ctx_1024, g_xattn, g_ffn, L0_xattn_Wq, L0_xattn_bq, L0_xattn_Wk, L0_xattn_bk, L0_xattn_Wv, L0_xattn_bv, L0_xattn_Wo, L0_xattn_bo, L0_ffn_Wr, L0_ffn_br, L0_ffn_W_up, L0_ffn_b_up, L0_ffn_W_down, L0_ffn_b_down, L1_xattn_ln_gamma, L1_xattn_ln_beta, L1_xattn_w_q, L1_xattn_w_kv, L1_xattn_w_out, L1_xattn_b_out, L1_xattn_gate, L1_ffn_W_fc, L1_ffn_ln_w, L1_ffn_ln_b, L1_ffn_W_proj, L2_xattn_Wq, L2_xattn_Wk, L2_xattn_Wv, L2_xattn_Wp, L2_xattn_bp, L2_ffn_W1, L2_ffn_b1, L2_ffn_W2, L2_ffn_b2, L2_ffn_Wr, L2_ffn_br, L3_xattn_W_proj, L3_xattn_b_proj, L3_ffn_router_w, L3_ffn_up_w, L3_ffn_down_w):
    import jax
    import jax.numpy as jnp

    def _L0_xattn_ref(query, key, value, Wq, bq, Wk, bk, Wv, bv, Wo, bo):
        import jax, jax.numpy as jnp
        import numpy as np
        D_MODEL = 128
        N_HEADS = 16
        D_HEAD = D_MODEL // N_HEADS
        WINDOW = 128

        def _heads(x):
            B, S, _ = x.shape
            return x.reshape(B, S, N_HEADS, D_HEAD).transpose(0, 2, 1, 3)
        B, S, _ = query.shape
        q = _heads(query @ Wq.T + bq)
        k = _heads(key @ Wk.T + bk)
        v = _heads(value @ Wv.T + bv)
        scores = jnp.einsum('bhqd,bhkd->bhqk', q, k) / np.sqrt(D_HEAD).astype(np.float32)
        idx = jnp.arange(S)
        local = jnp.abs(idx[:, None] - idx[None, :]) <= WINDOW // 2
        scores = jnp.where(local[None, None, :, :], scores, -jnp.inf)
        attn = jax.nn.softmax(scores, axis=-1)
        ctx = jnp.einsum('bhqk,bhkd->bhqd', attn, v)
        ctx = ctx.transpose(0, 2, 1, 3).reshape(B, S, D_MODEL)
        return ctx @ Wo.T + bo

    def _L0_ffn_ref(x, Wr, br, W_up, b_up, W_down, b_down):
        import jax, jax.numpy as jnp
        import numpy as np
        B, S, H = (4, 256, 128)
        E = 8
        GS = 2
        NG = E // GS
        F = int(H * 4 * (2.0 / 3.0))
        b, s, h = x.shape
        n_tok = b * s
        k = n_tok // E
        xf = x.reshape(n_tok, h)
        logits = xf @ Wr + br
        Sm = jax.nn.softmax(logits, axis=-1)
        G_t, idx_t = jax.lax.top_k(Sm.T, k)
        G = G_t.T
        idx = idx_t.T
        tokens = xf[idx]
        group = jnp.arange(E) // GS
        Wu = W_up[group]
        bu = b_up[group]
        mid = jax.nn.silu(jnp.einsum('keh,ehf->kef', tokens, Wu) + bu)
        out = jnp.einsum('kef,efh->keh', mid, W_down) + b_down
        y = jnp.zeros_like(xf).at[idx].add(G[..., None] * out)
        return y.reshape(b, s, h)

    def _L1_xattn_ref(x, context, ln_gamma, ln_beta, w_q, w_kv, w_out, b_out, gate):
        import jax, jax.numpy as jnp
        import numpy as np
        DIM = 128
        NUM_HEADS = 16
        DIM_HEAD = 64
        INNER = NUM_HEADS * DIM_HEAD
        SCALE = DIM_HEAD ** (-0.5)

        def _layernorm(x, gamma, beta, eps=1e-05):
            mu = jnp.mean(x, axis=-1, keepdims=True)
            var = jnp.mean(jnp.square(x - mu), axis=-1, keepdims=True)
            return (x - mu) * jax.lax.rsqrt(var + eps) * gamma + beta
        B, SQ, _ = x.shape
        SK = context.shape[1]
        xn = _layernorm(x, ln_gamma, ln_beta)
        q = (xn @ w_q).reshape(B, SQ, NUM_HEADS, DIM_HEAD)
        kv = context @ w_kv
        k, v = jnp.split(kv, 2, axis=-1)
        k = k.reshape(B, SK, NUM_HEADS, DIM_HEAD)
        v = v.reshape(B, SK, NUM_HEADS, DIM_HEAD)
        scores = jnp.einsum('bqhd,bkhd->bhqk', q * SCALE, k)
        attn = jax.nn.softmax(scores, axis=-1)
        out = jnp.einsum('bhqk,bkhd->bqhd', attn, v).reshape(B, SQ, INNER)
        out = out @ w_out + b_out
        return out * jnp.tanh(gate[0])

    def _L1_ffn_ref(x, W_fc, ln_w, ln_b, W_proj):
        import jax, jax.numpy as jnp
        import numpy as np
        EPS = 1e-06
        LN_EPS = 1e-05

        def _absmean_core(W):
            gamma = jnp.mean(jnp.abs(W)) + EPS
            Ws = W / gamma
            Wq = jnp.sign(Ws) * jnp.minimum(jnp.round(jnp.abs(Ws)), 1.0)
            return (Wq, gamma)

        @jax.custom_vjp
        def absmean(W):
            return _absmean_core(W)[0]

        def _absmean_fwd(W):
            Wq, gamma = _absmean_core(W)
            return (Wq, gamma)

        def _absmean_bwd(gamma, g):
            return (g / gamma,)
        absmean.defvjp(_absmean_fwd, _absmean_bwd)

        def layernorm(x, w, b, eps=LN_EPS):
            mu = jnp.mean(x, axis=-1, keepdims=True)
            var = jnp.mean((x - mu) ** 2, axis=-1, keepdims=True)
            return (x - mu) * jax.lax.rsqrt(var + eps) * w + b
        h = jnp.einsum('btd,hd->bth', x, absmean(W_fc))
        h = jax.nn.gelu(h, approximate=False)
        h = layernorm(h, ln_w, ln_b)
        return jnp.einsum('bth,dh->btd', h, absmean(W_proj))

    def _L2_xattn_ref(q, k, v, Wq, Wk, Wv, Wp, bp):
        import jax, jax.numpy as jnp
        import numpy as np
        D_MODEL = 128
        N_HEADS = 16
        BATCH = 2
        SEQ = 256

        def _rope(x):
            d = x.shape[-1]
            half = d // 2
            seq = x.shape[-2]
            pos = jnp.arange(seq, dtype=jnp.float32)
            theta = 1.0 / 10000.0 ** (2.0 * jnp.arange(half, dtype=jnp.float32) / d)
            ang = pos[:, None] * theta[None, :]
            sin, cos = (jnp.sin(ang), jnp.cos(ang))
            x1 = x[..., 0::2]
            x2 = x[..., 1::2]
            r1 = x1 * cos - x2 * sin
            r2 = x1 * sin + x2 * cos
            return jnp.stack([r1, r2], axis=-1).reshape(x.shape)
        h = N_HEADS
        b, s, d = q.shape
        dh = d // h
        qp = q @ Wq.T
        kp = k @ Wk.T
        vp = v @ Wv.T
        kp = _rope(kp)
        vp = _rope(vp)
        qh = qp.reshape(b, s, h, dh).transpose(0, 2, 1, 3)
        kh = kp.reshape(b, s, h, dh).transpose(0, 2, 1, 3)
        vh = vp.reshape(b, s, h, dh).transpose(0, 2, 1, 3)
        scores = jnp.einsum('bhqd,bhkd->bhqk', qh, kh) / jnp.sqrt(jnp.float32(dh))
        weights = jax.nn.softmax(scores, axis=-1)
        ctx = jnp.einsum('bhqk,bhkd->bhqd', weights, vh)
        ctx = ctx.transpose(0, 2, 1, 3).reshape(b, s, d)
        return ctx @ Wp.T + bp

    def _L2_ffn_ref(x, W1, b1, W2, b2, Wr, br):
        import jax, jax.numpy as jnp
        import numpy as np
        B, S, D, F, E = (4, 256, 128, 512, 8)
        b, s, d = x.shape
        e = Wr.shape[1]
        logits = x @ Wr + br
        idx = jnp.argmax(logits, axis=-1)
        probs = jax.nn.softmax(logits, axis=-1)
        gates = jnp.take_along_axis(probs, idx[..., None], axis=-1)[..., 0]
        xf = x.reshape(-1, d)
        idxf = idx.reshape(-1)
        gf = gates.reshape(-1)
        out = jnp.zeros_like(xf)
        for ei in range(e):
            h = jax.nn.gelu(xf @ W1[ei] + b1[ei], approximate=False)
            y = h @ W2[ei] + b2[ei]
            mask = (idxf == ei).astype(xf.dtype)
            out = out + y * (gf * mask)[:, None]
        return out.reshape(b, s, d)

    def _L3_xattn_ref(q, k, v, W_proj, b_proj):
        import jax, jax.numpy as jnp
        import numpy as np
        B, T, N_EMBD, N_HEAD = (2, 256, 128, 16)
        HEAD = N_EMBD // N_HEAD
        WINDOW = 64
        Bsz, Tlen, _ = q.shape
        qh = q.reshape(Bsz, Tlen, N_HEAD, HEAD).transpose(0, 2, 1, 3)
        kh = k.reshape(Bsz, Tlen, N_HEAD, HEAD).transpose(0, 2, 1, 3)
        vh = v.reshape(Bsz, Tlen, N_HEAD, HEAD).transpose(0, 2, 1, 3)
        scale = 1.0 / np.sqrt(HEAD)
        scores = jnp.einsum('bhqd,bhkd->bhqk', qh, kh) * scale
        idx = jnp.arange(Tlen)
        dist = jnp.abs(idx[None, :] - idx[:, None])
        scores = jnp.where(dist[None, None] > WINDOW, -jnp.inf, scores)
        attn = jax.nn.softmax(scores, axis=-1)
        y = jnp.einsum('bhqk,bhkd->bhqd', attn, vh)
        y = y.transpose(0, 2, 1, 3).reshape(Bsz, Tlen, N_EMBD)
        return y @ W_proj.T + b_proj

    def _L3_ffn_ref(x, router_w, up_w, down_w):
        import jax, jax.numpy as jnp
        import numpy as np
        B, S, D = (2, 512, 128)
        H = 512
        E = 8
        K = 4
        router_logits = jnp.einsum('bsd,de->bse', x, router_w)
        routing_weights = jax.nn.softmax(router_logits, axis=-1)
        topk_weights, topk_indices = jax.lax.top_k(routing_weights, K)
        topk_weights = topk_weights / jnp.sum(topk_weights, axis=-1, keepdims=True)
        h = jnp.einsum('bsd,edh->bseh', x, up_w)
        h = jax.nn.gelu(h)
        expert_outputs = jnp.einsum('bseh,ehd->bsed', h, down_w)
        gathered = jnp.take_along_axis(expert_outputs, topk_indices[:, :, :, None], axis=2)
        output = jnp.sum(topk_weights[:, :, :, None] * gathered, axis=2)
        return output
    x = x + jnp.tanh(g_xattn[0]) * _L0_xattn_ref(_layernorm(x, axis=-1), ctx_1024, ctx_1024, L0_xattn_Wq, L0_xattn_bq, L0_xattn_Wk, L0_xattn_bk, L0_xattn_Wv, L0_xattn_bv, L0_xattn_Wo, L0_xattn_bo)
    x = x + jnp.tanh(g_ffn[0]) * _L0_ffn_ref(_layernorm(x, axis=-1), L0_ffn_Wr, L0_ffn_br, L0_ffn_W_up, L0_ffn_b_up, L0_ffn_W_down, L0_ffn_b_down)
    x = x + jnp.tanh(g_xattn[1]) * _L1_xattn_ref(_layernorm(x, axis=-1), ctx_1024, L1_xattn_ln_gamma, L1_xattn_ln_beta, L1_xattn_w_q, L1_xattn_w_kv, L1_xattn_w_out, L1_xattn_b_out, L1_xattn_gate)
    x = x + jnp.tanh(g_ffn[1]) * _L1_ffn_ref(_layernorm(x, axis=-1), L1_ffn_W_fc, L1_ffn_ln_w, L1_ffn_ln_b, L1_ffn_W_proj)
    x = x + jnp.tanh(g_xattn[2]) * _L2_xattn_ref(_layernorm(x, axis=-1), ctx_1024, ctx_1024, L2_xattn_Wq, L2_xattn_Wk, L2_xattn_Wv, L2_xattn_Wp, L2_xattn_bp)
    x = x + jnp.tanh(g_ffn[2]) * _L2_ffn_ref(_layernorm(x, axis=-1), L2_ffn_W1, L2_ffn_b1, L2_ffn_W2, L2_ffn_b2, L2_ffn_Wr, L2_ffn_br)
    x = x + jnp.tanh(g_xattn[3]) * _L3_xattn_ref(_layernorm(x, axis=-1), ctx_1024, ctx_1024, L3_xattn_W_proj, L3_xattn_b_proj)
    x = x + jnp.tanh(g_ffn[3]) * _L3_ffn_ref(_layernorm(x, axis=-1), L3_ffn_router_w, L3_ffn_up_w, L3_ffn_down_w)
    return x

_drawn_inputs = setup_inputs


def setup_inputs(seed=0):
    import zlib

    import numpy as np

    out = dict(_drawn_inputs(seed))
    spreads = {'L0_xattn_bq': (0.0, 0.334),
     'L0_xattn_bk': (0.0, 2.0),
     'L0_xattn_bv': (0.0, 0.1),
     'L0_xattn_bo': (0.0, 0.1),
     'L0_ffn_br': (0.0, 0.1),
     'L1_xattn_ln_gamma': (1.0, 0.6),
     'L1_xattn_ln_beta': (0.0, 0.764),
     'L1_xattn_b_out': (0.0, 0.1),
     'L1_ffn_ln_w': (1.0, 0.2),
     'L1_ffn_ln_b': (0.0, 0.1),
     'L3_xattn_b_proj': (0.0, 0.8)}
    factors = {'L0_ffn_b_up': 8.0,
     'L0_ffn_b_down': 8.0,
     'L2_xattn_Wq': 6.811,
     'L2_xattn_Wk': 6.716,
     'L2_xattn_Wv': 3.339,
     'L2_xattn_Wp': 3.338,
     'L2_xattn_bp': 8.0,
     'L2_ffn_W1': 8.0,
     'L2_ffn_b1': 8.0,
     'L2_ffn_W2': 8.0,
     'L2_ffn_b2': 64.0,
     'L2_ffn_Wr': 8.0,
     'L2_ffn_br': 8.0,
     'L3_ffn_router_w': 3.586,
     'L3_ffn_up_w': 3.399,
     'L3_ffn_down_w': 3.043}
    for name, (base, spread) in spreads.items():
        noise = np.random.default_rng([zlib.crc32(name.encode()), seed]).standard_normal(out[name].shape)
        drawn = base * np.exp(spread * noise) if base else spread * noise
        out[name] = jnp.asarray(drawn.astype(out[name].dtype))
    for name, factor in factors.items():
        out[name] = (out[name] * factor).astype(out[name].dtype)
    return out
```

```python
import numpy as np
import concourse.bass as bass
from concourse import mybir
from contextlib import ExitStack

F32 = mybir.dt.float32
F32R = mybir.dt.float32r
BF16 = mybir.dt.bfloat16
I32 = mybir.dt.int32
ALU = mybir.AluOpType
ACT = mybir.ActivationFunctionType
AX = mybir.AxisListType

P = 128
B, S, D = 8, 256, 128
TPB = S // P
NT = B * TPB
H = 16
DH = D // H
HU = H // 2
RING = 4
PROBS = 6
NEG = -1e30
LN_EPS = 1e-5


class Chip:

    def __init__(self, nc, ctx, arrays):
        self.nc, self.ctx, self.a = nc, ctx, arrays
        self.sublayer_sems = []
        sb = self.sb
        self.x = sb("x_res", [P, NT, D])
        self.xnT = sb("xnT", [P, NT, P])
        self.ident = sb("ident", [P, P])
        self.identb = sb("identb", [P, P], BF16)
        self.ones = sb("ones", [P, P])
        self.zrow = sb("zrow", [2, S])
        self.mhalf = sb("mhalf", [P, NT])
        self.gates_t = sb("gates_t", [P, 8])
        self.banks = [ctx.enter_context(nc.psum_tensor(f"bank{i}", [P, 512], F32)) for i in range(8)]

    def sb(self, name, shape, dt=F32):
        return self.ctx.enter_context(self.nc.sbuf_tensor(name, shape, dt))

    def sem(self, name):
        return self.ctx.enter_context(self.nc.semaphore(name))

    def sublayer_sem(self, name):
        s = self.nc.alloc_semaphore(name)
        self.sublayer_sems.append(s)
        return s

    def end_sublayer(self):
        with self.nc.Block() as block:
            @block.gpsimd
            def _(g):
                for s in self.sublayer_sems:
                    g.sem_clear(s)
        for s in self.sublayer_sems:
            self.nc.release_semaphore(s)
        self.sublayer_sems = []


def need(eng, sem, value):
    if value > 0:
        eng.wait_ge(sem, value)


def row(v):
    return v.rearrange("(a n) -> a n", a=1)


def col(v):
    return v.rearrange("(n a) -> n a", a=1)


def start_block(c, weights):
    nc, a = c.nc, c.a
    x_in, const, gate_in, gate_t = (c.sem(s) for s in ("x_loaded", "consts_ready", "gates_loaded", "gates_ready"))
    stats, rstd_ready, xn_ready, xT_ready, xnT_ready = (
        c.sem(s) for s in ("ln0_stats", "ln0_rstd", "ln0_xn", "ln0_xT", "ln0_xnT"))
    with ExitStack() as own:
        sb = lambda n, s: own.enter_context(nc.sbuf_tensor(n, s, F32))
        st = sb("ln0_st", [P, NT, 6])
        mv = sb("ln0_mv", [P, NT, 2])
        rstd = sb("ln0_rstd_t", [P, NT])
        ve = sb("ln0_ve", [P, NT])
        xn = sb("ln0_xn_t", [P, 2, 4, D])
        with nc.Block() as block:
            @block.sync
            def _(sp):
                sp.dma_start(c.x[:], a["x"]).then_inc(x_in, 16)
                sp.dma_start(c.gates_t[:, 0:4], a["g_xattn"].partition_broadcast(P)).then_inc(gate_in, 16)
                sp.dma_start(c.gates_t[:, 4:8], a["g_ffn"].partition_broadcast(P)).then_inc(gate_in, 16)
                for sem, dst, src in weights:
                    sp.dma_start(dst, src).then_inc(sem, 16)

            @block.gpsimd
            def _(g):
                g.memset(c.ones[:], 1.0).then_inc(const, 1)
                g.memset(c.mhalf[:], -0.5).then_inc(const, 1)
                g.memset(c.zrow[:], 0.0).then_inc(const, 1)
                g.wait_ge(const, 3)
                g.affine_select(out=c.ident[:], in_=c.ones[:], compare_op=ALU.is_equal, fill=0.0, base=0,
                                pattern=[[-1, P]], channel_multiplier=1).then_inc(const, 1)
                g.wait_ge(const, 4)
                g.tensor_copy(c.identb[:], c.ident[:]).then_inc(const, 1)
                g.wait_ge(stats, 2 * NT)
                g.tensor_scalar(ve[:], mv[:, :, 1], LN_EPS, None, ALU.add).then_inc(rstd_ready, 1)
                g.wait_ge(rstd_ready, 1)
                g.tensor_tensor(rstd[:], ve[:], c.mhalf[:], ALU.pow).then_inc(rstd_ready, 1)

            @block.scalar
            def _(act):
                act.wait_ge(gate_in, 32)
                act.activation(c.gates_t[:], c.gates_t[:], ACT.Tanh).then_inc(gate_t, 1)
                for q in range(4):
                    act.wait_ge(xT_ready, q + 1)
                    act.copy(c.xnT[:, 4 * q:4 * q + 4, :], c.banks[q][:, :]).then_inc(xnT_ready, 1)

            @block.vector
            def _(v):
                v.wait_ge(x_in, 16)
                for t in range(NT):
                    v.bn_stats(st[:, t, :], c.x[:, t, :]).then_inc(stats, 1)
                v.wait_ge(stats, NT)
                for t in range(NT):
                    v.bn_aggr(mv[:, t, :], st[:, t, :]).then_inc(stats, 1)
                v.wait_ge(stats, 2 * NT)
                v.wait_ge(rstd_ready, 2)
                for t in range(NT):
                    if t >= 8:
                        v.wait_ge(xT_ready, t // 4 - 1)
                    v.tensor_scalar(xn[:, t // 4 % 2, t % 4, :], c.x[:, t, :], mv[:, t, 0:1], rstd[:, t:t + 1],
                                    ALU.subtract, ALU.mult).then_inc(xn_ready, 1)

            @block.tensor
            def _(pe):
                pe.wait_ge(const, 4)
                for q in range(4):
                    pe.wait_ge(xn_ready, 4 * q + 4)
                    for t in range(4):
                        m = pe.transpose(c.banks[q][:, t * P:(t + 1) * P], xn[:, q % 2, t, :], c.ident[:])
                    m.then_inc(xT_ready, 1)


def attention(c, L, w, gate, window=0, rope=False, next_loads=()):
    nc = c.nc
    W = P + window if window else S
    lo = [0, S - W]
    scale = float(1.0 / np.sqrt(DH))
    NPS, TPS, PA, PB, OPB, MISC = c.banks[0:2], c.banks[2:4], c.banks[4], c.banks[5], c.banks[6], c.banks[7]
    U = 2 * B
    pre = f"L{L}_"
    sem = lambda n: c.sublayer_sem(pre + n)
    (ct_in0, ct_in1, proj_q, proj_v, split_q, va_ready, stacked0, stacked1, n_ready, max_ready, shT_ready, sh_ready,
     shifted, t_ready, p_ready, pv_ready, o_ready, trT_ready, rc_ready, cn_ready, cnT_ready, cnT_copied,
     po_ready, resid, st_ready, mv_ready, rstd_ready, xn_ready, xT_ready, xnT_ready, zeroed, kf_ready, tmp_ready, tmp2) = (
        sem(n) for n in (
            "ctx_loaded0", "ctx_loaded1", "qk_projected", "v_projected", "qk_split", "v_ready", "stacked0",
            "stacked1", "scores_ready", "max_ready", "maxT_ready", "shift_ready", "shift_stacked",
            "scoresT_ready", "probs_ready", "pv_ready", "ctx_copied", "ctx_turned", "recip_ready", "ctx_normed",
            "ctxT_ready", "ctxT_copied", "out_ready", "resid_ready", "ln_stats", "ln_mv", "ln_rstd", "ln_xn",
            "ln_xT", "ln_xnT", "zeroed", "k_roped", "k_turned", "v_turned"))
    ct_in, stacked = [ct_in0, ct_in1], [stacked0, stacked1]
    with ExitStack() as own:
        sb = lambda n, s, d=F32: own.enter_context(nc.sbuf_tensor(pre + n, s, d))
        ct = sb("ct", [P, 2, S])
        parts = sb("parts", [P, 4, S], F32R)
        kf = sb("kf", [P, 3, S]) if rope else None
        vt = sb("vt", [P, 2, TPB, D]) if rope else None
        QS = sb("q_stack", [P, RING, HU, S], F32R)
        KS = sb("k_stack", [P, RING, HU, S], F32R)
        q_cleared, k_cleared = sem("q_stack_cleared"), sem("k_stack_cleared")
        va = sb("va", [P, 3, TPB, H, 32])
        mx = sb("mx", [P, 2, HU, TPB])
        sh = sb("sh", [HU, 2, 2, S], F32R)
        pt = sb("pt", [P, PROBS, TPB, S])
        os_ = sb("os", [P, 2, S])
        rc = sb("rc", [P, 2, TPB, 4])
        cn = sb("cn", [P, TPB, D])
        cnT = sb("cnT", [P, S])
        st = sb("st", [P, TPB, 6])
        mv = sb("mv", [P, TPB, 2])
        ve = sb("ve", [P, TPB])
        rstd = sb("rstd", [P, TPB])
        xn = sb("xn", [P, TPB, D])

        with nc.Block() as block:
            @block.sync
            def _(sp):
                def load_ctx(b):
                    if b >= 2:
                        sp.wait_ge(proj_v, b - 1)
                    sp.dma_start(ct[:, b % 2, :], c.a["ctxT"][:, b * S:(b + 1) * S]).then_inc(ct_in[b % 2], 16)

                def stack(u):
                    b, hf, r = u // 2, u % 2, u % RING
                    sp.wait_ge(split_q, 4 * (b + 1))
                    need(sp, t_ready, (u - RING + 1) * HU)
                    if u < RING:
                        sp.wait_ge(q_cleared, u + 1)
                        sp.wait_ge(k_cleared, u + 1)
                    for term, (qp, kp) in enumerate(((0, 2), (1, 2), (0, 3))):
                        for dst, part in ((QS, qp), (KS, kp)):
                            src = parts[hf * 64:hf * 64 + 64, part, :].bitcast(F32)
                            sp.dma_start(dst[DH * term:DH * (term + 1), r, :, :].bitcast(F32), src).then_inc(stacked[u % 2], 16)
                    sp.dma_start(QS[24:26, r, :, :].bitcast(F32), c.zrow[:].unsqueeze(1).broadcast_to([2, HU, S])).then_inc(stacked[u % 2], 16)

                def shift(u):
                    sp.wait_ge(sh_ready, 2 * (u + 1))
                    sp.wait_ge(n_ready, (u + 1) * HU)
                    for k in range(2):
                        sp.dma_start(QS[24 + k:25 + k, u % RING, :, :].bitcast(F32), sh[:, u % 2, k, :].bitcast(F32)).then_inc(shifted, 16)

                load_ctx(0)
                load_ctx(1)
                stack(0)
                stack(1)
                for t in range(U + 2):
                    if t % 2 == 0 and t // 2 + 2 < B:
                        load_ctx(t // 2 + 2)
                    if t == 0:
                        for s, dst, src in next_loads:
                            sp.dma_start(dst, src).then_inc(s, 16)
                    if t >= 1 and t + 1 < U:
                        stack(t + 1)
                    if t >= 1 and t - 1 < U:
                        shift(t - 1)

            @block.tensor
            def _(pe):
                def project(b):
                    xs = c.xnT[:, TPB * b:TPB * (b + 1), :].rearrange("p t n -> p (t n)")
                    need(pe, split_q, 4 * b)
                    if b >= 1:
                        pe.wait_ge(va_ready, b)
                    pe.wait_ge(ct_in[b % 2], 16 * (b // 2 + 1))
                    pe.matmul(PA[:, 0:S], w["WqT"], xs, start=True, stop=True)
                    m = pe.matmul(PA[:, S:2 * S], w["WkT"], ct[:, b % 2, :], start=True, stop=True)
                    if rope:
                        m = pe.matmul(PB[:, 0:S], w["WkTs"], ct[:, b % 2, :], start=True, stop=True)
                    m.then_inc(proj_q, 1)
                    if rope:
                        pe.wait_ge(tmp_ready, 2 * b + 2)
                    for t in range(TPB):
                        tok = ct[:, b % 2, t * P:(t + 1) * P]
                        m = pe.matmul(PB[:, t * D:(t + 1) * D], tok, w["WvT"], start=True, stop=True)
                        if rope:
                            m = pe.matmul(PB[:, (2 + t) * D:(3 + t) * D], tok, w["WvTs"], start=True, stop=True)
                    m.then_inc(proj_v, 1)

                def scores(u, h):
                    n, r = u * HU + h, u % RING
                    need(pe, max_ready, n - 1)
                    if h == 0:
                        pe.wait_ge(stacked[u % 2], 16 * 7 * (u // 2 + 1))
                    for t in range(TPB):
                        o = NPS[n % 2][:, t * W:(t + 1) * W]
                        m = pe.matmul(o, QS[:, r, h, t * P:(t + 1) * P], KS[:, r, h, lo[t]:lo[t] + W],
                                      start=True, stop=not window)
                        if window:
                            m = pe.matmul(o, c.identb[:], w["mask"][:, t, :], start=False, stop=True)
                    m.then_inc(n_ready, 1)

                def scores_t(u, h):
                    n, r = u * HU + h, u % RING
                    need(pe, p_ready, n - 1)
                    if h == 0:
                        pe.wait_ge(shifted, 32 * (u + 1))
                    for t in range(TPB):
                        o = TPS[n % 2][:, t * W:(t + 1) * W]
                        m = pe.matmul(o, KS[:, r, h, t * P:(t + 1) * P], QS[:, r, h, lo[t]:lo[t] + W],
                                      start=True, stop=not window)
                        if window:
                            m = pe.matmul(o, c.identb[:], w["mask"][:, t, :], start=False, stop=True)
                    m.then_inc(t_ready, 1)

                def pv(u, g):
                    G = 2 * u + g
                    pe.wait_ge(p_ready, 4 * (G + 1))
                    need(pe, o_ready, G)
                    pe.wait_ge(va_ready, u // 2 + 1)
                    for t in range(TPB):
                        for j in range(4):
                            n = 4 * G + j
                            h = n % H
                            m = pe.matmul(OPB[32 * j:32 * j + 32, lo[t]:lo[t] + W], va[:, u // 2 % 3, t, h, :],
                                          pt[:, n % PROBS, t, 0:W], start=(t == 0), stop=(t == 1),
                                          skip_group_check=bool(window))
                    m.then_inc(pv_ready, 1)

                def turn_max(u):
                    pe.wait_ge(max_ready, (u + 1) * HU)
                    need(pe, cn_ready, 2 * (u - 2) + 1)
                    for t in range(TPB):
                        m = pe.transpose(MISC[0:HU, t * P:(t + 1) * P], mx[:, u % 2, :, t], c.ident[:])
                    m.then_inc(shT_ready, 1)

                def turn_ctx(u, g):
                    G = 2 * u + g
                    pe.wait_ge(o_ready, G + 1)
                    need(pe, cn_ready, G)
                    for t in range(TPB):
                        m = pe.transpose(MISC[:, t * P:(t + 1) * P], os_[:, G % 2, t * P:(t + 1) * P], c.ident[:])
                    m.then_inc(trT_ready, 1)

                def turn_normed(b):
                    pe.wait_ge(cn_ready, 4 * (b + 1))
                    for t in range(TPB):
                        m = pe.transpose(MISC[:, t * P:(t + 1) * P], cn[:, t, :], c.ident[:])
                    m.then_inc(cnT_ready, 1)

                def out(b):
                    pe.wait_ge(cnT_copied, b + 1)
                    for t in range(TPB):
                        pe.matmul(MISC[:, t * D:(t + 1) * D], cnT[:, t * P:(t + 1) * P], w["WoT"],
                                  start=True, stop=False)
                        m = pe.matmul(MISC[:, t * D:(t + 1) * D], c.ones[0:1, :], w["bo"], start=False, stop=True)
                    m.then_inc(po_ready, 1)

                def turn_ln(b):
                    pe.wait_ge(xn_ready, 2 * (b + 1))
                    for t in range(TPB):
                        m = pe.transpose(MISC[:, t * P:(t + 1) * P], xn[:, t, :], c.ident[:])
                    m.then_inc(xT_ready, 1)

                for s, all_loads in w["loaded"]:
                    pe.wait_ge(s, all_loads)
                project(0)
                for t in range(U + 6):
                    N, T, T3 = t < U, 0 <= t - 2 < U, 0 <= t - 3 < U
                    b4, b5 = (t - 4) // 2, (t - 5) // 2
                    for h in range(HU):
                        if N:
                            scores(t, h)
                        if T:
                            scores_t(t - 2, h)
                        if h == 1:
                            if T3:
                                pv(t - 3, 1)
                            if 0 <= t - 1 < U:
                                turn_max(t - 1)
                        if h == 2 and t % 2 == 1 and 0 <= b5 < B:
                            need(pe, sh_ready, 2 * min(t, U))
                            turn_ln(b5)
                        if h == 3 and T3:
                            need(pe, sh_ready, 2 * min(t, U))
                            if t % 2 == 1 and b5 >= 0:
                                pe.wait_ge(xnT_ready, b5 + 1)
                            turn_ctx(t - 3, 1)
                        if h == 4 and t % 2 == 0 and 0 <= b4 < B:
                            turn_normed(b4)
                        if h == 5 and T:
                            pv(t - 2, 0)
                        if h == 5 and t % 2 == 0 and t // 2 + 1 < B:
                            project(t // 2 + 1)
                        if h == 6 and t % 2 == 0 and 0 <= b4 < B:
                            out(b4)
                        if h == 7 and T:
                            if t % 2 == 0 and b4 >= 0:
                                pe.wait_ge(resid, b4 + 1)
                            if t % 2 == 1:
                                need(pe, cn_ready, 2 * (t - 3) + 2)
                            need(pe, sh_ready, 2 * min(t, U))
                            turn_ctx(t - 2, 0)

            @block.scalar
            def _(act):
                def split(b):
                    act.wait_ge(proj_q, b + 1)
                    if b >= 1:
                        act.wait_ge(stacked[0], 16 * 7 * b)
                        act.wait_ge(stacked[1], 16 * 7 * b)
                    act.activation(parts[:, 0, :], PA[:, 0:S], ACT.Identity, bias=w["bq"]).then_inc(split_q, 1)
                    if rope:
                        act.wait_ge(kf_ready, b + 1)
                        act.copy(parts[:, 2, :], kf[:, 2, :]).then_inc(split_q, 1)
                    else:
                        act.activation(parts[:, 2, :], PA[:, S:2 * S], ACT.Identity, bias=w["bk"]).then_inc(split_q, 1)

                def exps(u, h):
                    n = u * HU + h
                    act.wait_ge(t_ready, n + 1)
                    need(act, pv_ready, (n - PROBS) // 4 + 1)
                    src = TPS[n % 2][:, 0:TPB * W]
                    if window:
                        src = src.rearrange("p (t n) -> p t n", t=TPB)
                    else:
                        src = src.rearrange("p (t n) -> p t n", t=TPB)
                    act.activation(pt[:, n % PROBS, :, 0:W], src, ACT.Exp, scale=scale).then_inc(p_ready, 1)

                def copy_ctx(u, g):
                    G = 2 * u + g
                    act.wait_ge(pv_ready, G + 1)
                    need(act, trT_ready, G - 1)
                    act.copy(os_[:, G % 2, :], OPB[:, 0:S]).then_inc(o_ready, 1)

                def copy_normed(b):
                    act.wait_ge(cnT_ready, b + 1)
                    need(act, po_ready, b)
                    act.copy(cnT[:], MISC[:, 0:S]).then_inc(cnT_copied, 1)

                def copy_ln(b):
                    act.wait_ge(xT_ready, b + 1)
                    act.copy(c.xnT[:, TPB * b:TPB * (b + 1), :].rearrange("p t n -> p (t n)"),
                             MISC[:, 0:S]).then_inc(xnT_ready, 1)

                for s, all_loads in w["loaded"]:
                    act.wait_ge(s, all_loads)
                split(0)
                for t in range(U + 6):
                    T, T3 = 0 <= t - 2 < U, 0 <= t - 3 < U
                    b4, b5 = (t - 4) // 2, (t - 5) // 2
                    for h in range(HU):
                        if T:
                            exps(t - 2, h)
                        if h == 1 and T3:
                            copy_ctx(t - 3, 1)
                        if h == 2 and t % 2 == 1 and 0 <= b5 < B:
                            copy_ln(b5)
                        if h == 4 and t % 2 == 0 and 0 <= b4 < B:
                            copy_normed(b4)
                        if h == 5 and t % 2 == 0 and t // 2 + 1 < B:
                            split(t // 2 + 1)
                        if h == 5 and T:
                            copy_ctx(t - 2, 0)

            @block.gpsimd
            def _(g):
                g.memset(QS[:, 0].bitcast(F32), 0.0).then_inc(q_cleared, 1)
                g.memset(va[:], 1.0).then_inc(zeroed, 1)
                for r in range(1, RING):
                    g.memset(QS[:, r].bitcast(F32), 0.0).then_inc(q_cleared, 1)
                for b in range(B):
                    g.wait_ge(mv_ready, 2 * (b + 1))
                    g.tensor_scalar(ve[:], mv[:, :, 1], LN_EPS, None, ALU.add).then_inc(rstd_ready, 1)
                    g.wait_ge(rstd_ready, 2 * b + 1)
                    g.tensor_tensor(rstd[:], ve[:], c.mhalf[:, 0:TPB], ALU.pow).then_inc(rstd_ready, 1)

            @block.vector
            def _(v):
                v3 = lambda ap: ap.rearrange("p (t h d) -> p t h d", t=TPB, h=H)

                def split(b):
                    v.wait_ge(proj_q, b + 1)
                    if rope:
                        v.wait_ge(split_q, 4 * b + 1)
                        v.tensor_tensor(kf[:, 0, :], PA[:, S:2 * S], w["cosT"], ALU.mult).then_inc(tmp_ready, 1)
                        v.tensor_tensor(kf[:, 1, :], PB[:, 0:S], w["sinT"], ALU.mult).then_inc(tmp_ready, 1)
                        v.wait_ge(tmp_ready, 2 * b + 2)
                        if b >= 1:
                            v.wait_ge(split_q, 4 * b)
                        v.tensor_tensor(kf[:, 2, :], kf[:, 0, :], kf[:, 1, :], ALU.add).then_inc(kf_ready, 1)
                    v.wait_ge(split_q, 4 * b + 2)
                    v.scalar_tensor_tensor(parts[:, 1, :], PA[:, 0:S], w["bq"], parts[:, 0, :].bitcast(F32),
                                           ALU.add, ALU.subtract).then_inc(split_q, 1)
                    if rope:
                        v.wait_ge(kf_ready, b + 1)
                        v.tensor_tensor(parts[:, 3, :], kf[:, 2, :], parts[:, 2, :].bitcast(F32),
                                        ALU.subtract).then_inc(split_q, 1)
                    else:
                        v.scalar_tensor_tensor(parts[:, 3, :], PA[:, S:2 * S], w["bk"],
                                               parts[:, 2, :].bitcast(F32), ALU.add, ALU.subtract).then_inc(split_q, 1)
                    v.wait_ge(proj_v, b + 1)
                    if b == 0:
                        v.wait_ge(zeroed, 1)
                    need(v, pv_ready, 4 * (b - 2))
                    dst = va[:, b % 3, :, :, 0:DH]
                    if rope:
                        src = PB[:, :].rearrange("p (s t d) -> p s t d", s=2, t=TPB)
                        for s in range(2):
                            v.tensor_tensor(vt[:, s], src[:, s], w["cs"][:, s], ALU.mult).then_inc(tmp2, 1)
                        v.wait_ge(tmp2, 2 * b + 2)
                        x3 = lambda s: vt[:, s].rearrange("p t (h d) -> p t h d", h=H)
                        for t in range(TPB):
                            i = v.tensor_tensor(dst[:, t], x3(0)[:, t], x3(1)[:, t], ALU.add)
                        i.then_inc(va_ready, 1)
                    else:
                        for t in range(TPB):
                            if w["bv"] is None:
                                i = v.tensor_copy(dst[:, t], v3(PB[:, 0:S])[:, t])
                            else:
                                i = v.tensor_tensor(dst[:, t], v3(PB[:, 0:S])[:, t],
                                                    w["bv"].rearrange("p (h d) -> p h d", h=H), ALU.add)
                        i.then_inc(va_ready, 1)

                def maxima(u, h):
                    n = u * HU + h
                    v.wait_ge(n_ready, n + 1)
                    if h == 0:
                        need(v, shT_ready, u - 1)
                    v.tensor_reduce(mx[:, u % 2, h, :], NPS[n % 2][:, 0:TPB * W].rearrange("p (t n) -> p t n", t=TPB),
                                    AX.X, ALU.max).then_inc(max_ready, 1)

                def shift(u):
                    v.wait_ge(shT_ready, u + 1)
                    need(v, shifted, 32 * (u - 1))
                    v.tensor_scalar(sh[:, u % 2, 0, :], MISC[0:HU, 0:S], -1.0, None, ALU.mult).then_inc(sh_ready, 1)
                    v.wait_ge(sh_ready, 2 * u + 1)
                    v.scalar_tensor_tensor(sh[:, u % 2, 1, :], MISC[0:HU, 0:S], -1.0,
                                           sh[:, u % 2, 0, :].bitcast(F32), ALU.mult, ALU.subtract).then_inc(sh_ready, 1)

                def norm_ctx(u, g):
                    G = 2 * u + g
                    v.wait_ge(trT_ready, G + 1)
                    o4 = MISC[:, 0:S].rearrange("p (t j k) -> p t j k", t=TPB, j=4)
                    need(v, cn_ready, G - 1)
                    v.reciprocal(rc[:, G % 2], o4[:, :, :, DH]).then_inc(rc_ready, 1)
                    v.wait_ge(rc_ready, G + 1)
                    if G % 4 == 0:
                        need(v, cnT_ready, G // 4)
                    h0 = 4 * G % H
                    for t in range(TPB):
                        i = v.tensor_tensor(cn[:, t, h0 * DH:(h0 + 4) * DH].rearrange("p (j d) -> p j d", j=4),
                                            o4[:, t, :, 0:DH],
                                            rc[:, G % 2, t, :].rearrange("p (j a) -> p j a", a=1).broadcast_to([P, 4, DH]),
                                            ALU.mult)
                    i.then_inc(cn_ready, 1)

                def finish(b):
                    v.wait_ge(po_ready, b + 1)
                    xs = c.x[:, TPB * b:TPB * (b + 1), :].rearrange("p t n -> p (t n)")
                    v.scalar_tensor_tensor(xs, MISC[:, 0:S], gate, xs, ALU.mult, ALU.add).then_inc(resid, 1)
                    v.wait_ge(resid, b + 1)
                    for t in range(TPB):
                        v.bn_stats(st[:, t, :], c.x[:, TPB * b + t, :]).then_inc(st_ready, 1)
                    v.wait_ge(st_ready, 2 * (b + 1))
                    for t in range(TPB):
                        v.bn_aggr(mv[:, t, :], st[:, t, :]).then_inc(mv_ready, 1)

                def normalise(b):
                    v.wait_ge(mv_ready, 2 * (b + 1))
                    v.wait_ge(rstd_ready, 2 * (b + 1))
                    need(v, xT_ready, b)
                    for t in range(TPB):
                        v.tensor_scalar(xn[:, t, :], c.x[:, TPB * b + t, :], mv[:, t, 0:1], rstd[:, t:t + 1],
                                        ALU.subtract, ALU.mult).then_inc(xn_ready, 1)

                v.memset(KS[:, 0].bitcast(F32), 1.0).then_inc(k_cleared, 1)
                for s, all_loads in w["loaded"]:
                    v.wait_ge(s, all_loads)
                split(0)
                for r in range(1, RING):
                    v.memset(KS[:, r].bitcast(F32), 1.0).then_inc(k_cleared, 1)
                for t in range(U + 6):
                    N, T, T3 = t < U, 0 <= t - 2 < U, 0 <= t - 3 < U
                    b4, b5 = (t - 4) // 2, (t - 5) // 2
                    for h in range(HU):
                        if h == 0 and t % 2 == 1 and 0 <= b5 < B:
                            normalise(b5)
                        if h == 1 and 0 <= t - 1 < U:
                            shift(t - 1)
                        if N:
                            maxima(t, h)
                        if h == 3 and T3:
                            norm_ctx(t - 3, 1)
                        if h == 5 and t % 2 == 0 and t // 2 + 1 < B:
                            split(t // 2 + 1)
                        if h == 6 and t % 2 == 0 and 0 <= b4 < B:
                            finish(b4)
                        if h == 7 and T:
                            norm_ctx(t - 2, 0)


def layer_norm_tail(c, own, pre, double=None):
    nc = c.nc
    sb = lambda n, s, d=F32: own.enter_context(nc.sbuf_tensor(pre + n, s, d))
    return dict(st=sb("st", [P, 4, 6]), mv=sb("mv", [P, 4, 2]), ve=sb("ve", [P, 4]), rstd=sb("rstd", [P, 4]),
                xn=sb("xn", [P, 4, D]))


def ffn(c, L, w, tgate, E, per_group, act_f, rule, double=None):
    nc = c.nc
    F = w["F"]
    FT = (F + P - 1) // P
    FP = FT * P
    AHEAD = 10 if rule == "experts" else 1
    HR = AHEAD + 1
    CH = 4
    NC = NT // CH
    groups = E // per_group
    K = [(q, g) for q in range(NC) for g in range(groups)]
    UB, YB, GB, LB = c.banks[0:4], c.banks[4:6], c.banks[6], c.banks[7]
    pre = f"F{L}_"
    sem = lambda n: c.sublayer_sem(pre + n)
    (stepg2, xn1_ready) = (sem("gate_zeroed"), sem("ln_xn1"))
    (wh_ready, wl_ready, xh_ready, xl_ready) = (sem(n) for n in ("w1_high", "w1_low", "x_high", "x_low"))
    (lg_ready, step, stepg, stepa, stepp, gates_ready, up_ready, h_ready, y_ready, added, gT_ready, gT_copied, bias_ready,
     bias_added, st_ready, mv_ready, rstd_ready, xn_ready, xT_ready, xnT_ready) = (sem(n) for n in (
         "logits_ready", "gate_step", "gate_pool", "gate_exp", "gate_pe", "gates_ready", "up_ready", "hidden_ready",
         "down_ready", "added", "gatesT_ready", "gatesT_copied", "bias_ready", "bias_added", "ln_stats", "ln_mv",
         "ln_rstd", "ln_xn", "ln_xT", "ln_xnT"))
    with ExitStack() as own:
        sb = lambda n, s, d=F32: own.enter_context(nc.sbuf_tensor(pre + n, s, d))
        lg = sb("lg", [P, NT, E])
        pr = sb("pr", [P, NT, E])
        m1 = sb("m1", [P, NT])
        gates = sb("gates", [P, NT, E])
        gT = sb("gT", [E, NT, P])
        ht = sb("ht", [P, HR, FT, CH * P])
        wh = sb("wh", [P, groups * FP], F32R)
        wl = sb("wl", [P, groups * FP], F32R)
        xh = sb("xh", [P, NC, CH * P], F32R)
        xl = sb("xl", [P, NC, CH * P], F32R)
        ln = layer_norm_tail(c, own, pre)
        st, mv, ve, rstd, xn = (ln[k] for k in ("st", "mv", "ve", "rstd", "xn"))
        if rule == "experts":
            pT = sb("pT", [P, P])
            msk = sb("msk", [P, P])
            eq = sb("eq", [P, P])
            cum = sb("cum", [P, P])
            zero = sb("zero", [P, P])
            cand = sb("cand", [P, 1], I32)
            low = sb("low", [P, 1], I32)
            take = sb("take", [P, 1], I32)
            cnt = sb("cnt", [P, 1])
            left = sb("left", [P, 1])
            prf = sb("prf", [P, 1])
        else:
            cmp1 = sb("cmp1", [P, NT, E, E])
            cmp2 = sb("cmp2", [P, NT, E, E])
            rank = sb("rank", [P, NT, E])

        b8 = lambda ap: ap.rearrange("p (t a) -> p t a", a=1).broadcast_to([P, NT, E])
        other = lambda ap: ap.rearrange("p t (a e) -> p t a e", a=1).broadcast_to([P, NT, E, E])
        mine = lambda ap: ap.rearrange("p t (e a) -> p t e a", a=1).broadcast_to([P, NT, E, E])
        BITS = 30

        with nc.Block() as block:
            @block.tensor
            def _(pe):
                def up(k, f):
                    q, g = K[k]
                    n = k * FT + f
                    if f == 0:
                        pe.wait_ge(wh_ready, g + 1)
                        pe.wait_ge(wl_ready, g + 1)
                        pe.wait_ge(xh_ready, q + 1)
                        pe.wait_ge(xl_ready, q + 1)
                    need(pe, h_ready, n - 3)
                    cols = slice(g * FP + f * P, g * FP + (f + 1) * P)
                    pe.matmul(UB[n % 4][:, :], wh[:, cols], xh[:, q, :], start=True, stop=False)
                    pe.matmul(UB[n % 4][:, :], wh[:, cols], xl[:, q, :], start=False, stop=False)
                    pe.matmul(UB[n % 4][:, :], wl[:, cols], xh[:, q, :], start=False, stop=True).then_inc(up_ready, 1)

                for s, all_loads in w["loaded"]:
                    pe.wait_ge(s, all_loads)
                for t in range(NT):
                    m = pe.matmul(GB[:, t * E:(t + 1) * E], c.xnT[:, t, :], w["Wr"], start=True, stop=True)
                m.then_inc(lg_ready, 1)
                if rule == "experts":
                    pe.wait_ge(step, w["steps_to_probs"])
                    pe.transpose(GB[:, 0:P], pr[:].rearrange("p t e -> p (t e)"), c.ident[:]).then_inc(stepp, 1)
                    for k in range(BITS + 1):
                        pe.wait_ge(stepg, 2 * k + 1)
                        pe.matmul(LB[:, 0:1], w["same_expert"], cnt[:], start=True, stop=True).then_inc(stepp, 1)
                        if k < AHEAD * FT:
                            up(k // FT, k % FT)
                    pe.wait_ge(stepg, 2 * BITS + 3)
                    pe.matmul(LB[:, 0:1], w["earlier_tile"], cum[:, P - 1:P], start=True, stop=True).then_inc(stepp, 1)
                    pe.wait_ge(stepg, 2 * BITS + 4)
                    pe.transpose(GB[:, 0:P], msk[:], c.ident[:]).then_inc(stepp, 1)

                def down(k, e):
                    q, g = K[k]
                    n = k * per_group + e
                    x = g * per_group + e
                    if e == 0:
                        pe.wait_ge(h_ready, (k + 1) * FT)
                    need(pe, added, 4 * (n - 1))
                    for t in range(CH):
                        for f in range(FT):
                            m = pe.matmul(YB[n % 2][:, t * D:(t + 1) * D], ht[:, k % HR, f, t * P:(t + 1) * P],
                                          w["W2"][:, (x * FT + f) * D:(x * FT + f + 1) * D],
                                          start=(f == 0), stop=(f == FT - 1))
                    m.then_inc(y_ready, 1)

                def biases(q):
                    if q == 0:
                        pe.wait_ge(gates_ready, 1)
                    for t in range(CH):
                        need(pe, gT_copied, CH * q + t)
                        pe.transpose(GB[0:E, 0:P], gates[:, CH * q + t, :], c.ident[:]).then_inc(gT_ready, 1)
                    pe.wait_ge(gT_copied, CH * (q + 1))
                    need(pe, bias_added, q)
                    for t in range(CH):
                        m = pe.matmul(LB[:, t * D:(t + 1) * D], gT[:, CH * q + t, :], w["b2"], start=True, stop=True)
                    m.then_inc(bias_ready, 1)

                def turn_ln(q):
                    pe.wait_ge(xn_ready, CH * (q + 1))
                    if w["b2"] is not None:
                        pe.wait_ge(bias_added, NC)
                    need(pe, xnT_ready, q)
                    for t in range(CH):
                        m = pe.transpose(LB[:, t * P:(t + 1) * P], xn[:, t, :], c.ident[:])
                    m.then_inc(xT_ready, 1)

                if rule != "experts":
                    for f in range(FT):
                        up(0, f)
                for k in range(len(K)):
                    q, g = K[k]
                    if k + AHEAD < len(K):
                        for f in range(FT):
                            up(k + AHEAD, f)
                    for e in range(per_group):
                        down(k, e)
                        if (k + 1) * per_group == 2 and e == per_group - 1 and w["b2"] is not None:
                            for n in range(NC):
                                biases(n)
                    if g == groups - 2 and q > 0:
                        turn_ln(q - 1)
                turn_ln(NC - 1)

            @block.scalar
            def _(act):
                for s, all_loads in w["loaded"]:
                    act.wait_ge(s, all_loads)
                for g in range(groups):
                    act.copy(wh[:, g * FP:(g + 1) * FP], w["W1"][:, g * FP:(g + 1) * FP]).then_inc(wh_ready, 1)
                    if g < NC:
                        act.copy(xh[:, g, :],
                                 c.xnT[:, CH * g:CH * (g + 1), :].rearrange("p t n -> p (t n)")).then_inc(xh_ready, 1)
                act.wait_ge(step, 3)
                act.activation(pr[:], pr[:], ACT.Exp).then_inc(stepa, 1)

                def hidden(k):
                    q, g = K[k]
                    need(act, y_ready, (k - HR + 1) * per_group)
                    for f in range(FT):
                        n = k * FT + f
                        act.wait_ge(up_ready, n + 1)
                        b = w["b1"][:, g * FT + f:g * FT + f + 1] if w["b1"] is not None else 0.0
                        act.activation(ht[:, k % HR, f, :], UB[n % 4][:, :], act_f, bias=b).then_inc(h_ready, 1)

                for k in range(AHEAD):
                    hidden(k)
                for k in range(len(K)):
                    q, g = K[k]
                    if k + AHEAD < len(K):
                        hidden(k + AHEAD)
                    if g == groups - 1 and q > 0:
                        copy_ln(c, act, q - 1, xT_ready, xnT_ready, LB, double)
                copy_ln(c, act, NC - 1, xT_ready, xnT_ready, LB, double)

            @block.gpsimd
            def _(g):
                if rule == "experts":
                    g.memset(zero[:], 0.0).then_inc(stepg2, 1)
                    g.memset(low[:], 0).then_inc(stepg2, 1)
                for q in range(NC):
                    g.wait_ge(xh_ready, q + 1)
                    g.tensor_tensor(xl[:, q, :], c.xnT[:, CH * q:CH * (q + 1), :].rearrange("p t n -> p (t n)"),
                                    xh[:, q, :].bitcast(F32), ALU.subtract).then_inc(xl_ready, 1)
                rounds = 2 if double else 1
                for n in range(NC * rounds):
                    g.wait_ge(mv_ready, 4 * (n + 1))
                    g.tensor_scalar(ve[:], mv[:, :, 1], LN_EPS, None, ALU.add).then_inc(rstd_ready, 1)
                    g.wait_ge(rstd_ready, 2 * n + 1)
                    g.tensor_tensor(rstd[:], ve[:], c.mhalf[:, 0:4], ALU.pow).then_inc(rstd_ready, 1)

            @block.vector
            def _(v):
                count = [0]

                def chain(i):
                    count[0] += 1
                    i.then_inc(step, 1)
                    v.wait_ge(step, count[0])

                for s, all_loads in w["loaded"]:
                    v.wait_ge(s, all_loads)
                for g in range(groups):
                    v.wait_ge(wh_ready, g + 1)
                    v.tensor_tensor(wl[:, g * FP:(g + 1) * FP], w["W1"][:, g * FP:(g + 1) * FP],
                                    wh[:, g * FP:(g + 1) * FP].bitcast(F32), ALU.subtract).then_inc(wl_ready, 1)
                v.wait_ge(lg_ready, 1)
                l3 = GB[:, 0:NT * E].rearrange("p (t e) -> p t e", e=E)
                if w["br"] is not None:
                    chain(v.tensor_tensor(lg[:], l3, w["br"].rearrange("p (a e) -> p a e", a=1).broadcast_to([P, NT, E]),
                                          ALU.add))
                else:
                    chain(v.tensor_copy(lg[:], l3))
                chain(v.tensor_reduce(m1[:], lg[:], AX.X, ALU.max))
                chain(v.tensor_tensor(pr[:], lg[:], b8(m1[:]), ALU.subtract))
                v.wait_ge(stepa, 1)
                chain(v.tensor_reduce(m1[:], pr[:], AX.X, ALU.add))
                chain(v.reciprocal(m1[:], m1[:]))
                chain(v.tensor_tensor(pr[:], pr[:], b8(m1[:]), ALU.mult))
                if rule == "experts":
                    assert count[0] == w["steps_to_probs"]
                    v.wait_ge(stepp, 1)
                    chain(v.tensor_copy(pT[:], GB[:, 0:P]))
                    v.wait_ge(stepg2, 2)
                    for k in range(BITS):
                        chain(v.tensor_single_scalar(cand[:], low[:], 1 << (BITS - 1 - k), ALU.bitwise_or))
                        v.tensor_scalar(msk[:], pT[:], cand[:].bitcast(F32), 0.0, ALU.is_ge, ALU.add,
                                        accum_out=cnt[:]).then_inc(stepg, 1)
                        v.wait_ge(stepp, k + 2)
                        chain(v.tensor_single_scalar(take[:], LB[:, 0:1], float(w["capacity"]), ALU.is_ge))
                        v.scalar_tensor_tensor(low[:], take[:], BITS - 1 - k, low[:], ALU.logical_shift_left,
                                               ALU.bitwise_or).then_inc(stepg, 1)
                        v.wait_ge(stepg, 2 * k + 2)
                    v.tensor_scalar(msk[:], pT[:], low[:].bitcast(F32), 0.0, ALU.is_gt, ALU.add,
                                    accum_out=cnt[:]).then_inc(stepg, 1)
                    v.wait_ge(stepg, 2 * BITS + 1)
                    v.tensor_scalar(eq[:], pT[:], low[:].bitcast(F32), None, ALU.is_equal).then_inc(stepg, 1)
                    v.wait_ge(stepg, 2 * BITS + 2)
                    v.tensor_tensor_scan(cum[:], eq[:], zero[:], 0.0, ALU.add, ALU.add)
                    v.wait_ge(stepp, BITS + 2)
                    chain(v.tensor_scalar(left[:], LB[:, 0:1], -1.0, float(w["capacity"]), ALU.mult, ALU.add))
                    v.drain().then_inc(stepg, 1)
                    v.wait_ge(stepp, BITS + 3)
                    chain(v.tensor_copy(prf[:], LB[:, 0:1]))
                    chain(v.tensor_scalar(cum[:], cum[:], prf[:], left[:], ALU.add, ALU.is_le))
                    chain(v.tensor_tensor(eq[:], eq[:], cum[:], ALU.mult))
                    chain(v.tensor_tensor(msk[:], msk[:], eq[:], ALU.add))
                    v.tensor_tensor(msk[:], msk[:], pT[:], ALU.mult).then_inc(stepg, 1)
                    v.wait_ge(stepp, BITS + 4)
                    v.tensor_scalar(gates[:].rearrange("p t e -> p (t e)"), GB[:, 0:P], tgate, None,
                                    ALU.mult).then_inc(gates_ready, 1)
                else:
                    of = lg if rule == "first" else pr
                    v.tensor_tensor(cmp1[:], other(of[:]), mine(of[:]), ALU.is_gt)
                    chain(v.tensor_tensor(cmp2[:], other(of[:]), mine(of[:]), ALU.is_equal))
                    chain(v.tensor_tensor(cmp2[:].rearrange("p t e f -> p t (e f)"),
                                          cmp2[:].rearrange("p t e f -> p t (e f)"),
                                          w["before"].rearrange("p (a n) -> p a n", a=1).broadcast_to([P, NT, E * E]), ALU.mult))
                    chain(v.tensor_tensor(cmp1[:], cmp1[:], cmp2[:], ALU.add))
                    chain(v.tensor_reduce(rank[:], cmp1[:], AX.X, ALU.add))
                    top = 1.0 if rule == "first" else 4.0
                    chain(v.tensor_single_scalar(rank[:], rank[:], top, ALU.is_lt))
                    chain(v.tensor_tensor(pr[:], pr[:], rank[:], ALU.mult))
                    if rule == "four":
                        chain(v.tensor_reduce(m1[:], pr[:], AX.X, ALU.add))
                        chain(v.reciprocal(m1[:], m1[:]))
                        chain(v.tensor_tensor(pr[:], pr[:], b8(m1[:]), ALU.mult))
                    v.tensor_scalar(gates[:], pr[:], tgate, None, ALU.mult).then_inc(gates_ready, 1)
                v.wait_ge(gates_ready, 1)

                def biases(q):
                    for t in range(CH):
                        v.wait_ge(gT_ready, CH * q + t + 1)
                        v.tensor_copy(gT[:, CH * q + t, :], GB[0:E, 0:P]).then_inc(gT_copied, 1)
                    v.wait_ge(bias_ready, q + 1)
                    xs = c.x[:, CH * q:CH * (q + 1), :].rearrange("p t n -> p (t n)")
                    v.tensor_tensor(xs, LB[:, :], xs, ALU.add).then_inc(bias_added, 1)
                    v.wait_ge(bias_added, q + 1)

                def stats(q, n, src):
                    for t in range(CH):
                        v.bn_stats(st[:, t, :], src(t)).then_inc(st_ready, 1)
                    v.wait_ge(st_ready, CH * (n + 1))
                    for t in range(CH):
                        v.bn_aggr(mv[:, t, :], st[:, t, :]).then_inc(mv_ready, 1)

                def normalise(q, n, src):
                    v.wait_ge(mv_ready, CH * (n + 1))
                    v.wait_ge(rstd_ready, 2 * (n + 1))
                    need(v, xT_ready, q)
                    for t in range(CH):
                        v.tensor_scalar(xn[:, t, :], src(t), mv[:, t, 0:1], rstd[:, t:t + 1], ALU.subtract,
                                        ALU.mult).then_inc(norm_sem(n), 1)

                def norm_sem(n):
                    return xn_ready if not double or n % 2 else xn1_ready

                def ln_step(q, i):
                    x1 = lambda t: c.x[:, CH * q + t, :]
                    x2 = lambda t: xn[:, t, :]
                    n = 2 * q if double else q
                    if i == 0:
                        stats(q, n, x1)
                    elif i == 1:
                        normalise(q, n, x1)
                        if double:
                            v.wait_ge(xn1_ready, CH * (q + 1))
                            stats(q, n + 1, x2)
                    elif double:
                        normalise(q, n + 1, x2)

                if w["b2"] is not None:
                    for q in range(NC):
                        biases(q)
                for k in range(len(K)):
                    q, g = K[k]
                    for e in range(per_group):
                        n = k * per_group + e
                        x = g * per_group + e
                        v.wait_ge(y_ready, n + 1)
                        if g == 0 and e == 0:
                            need(v, st_ready, 0)
                        need(v, added, 4 * n)
                        for t in range(CH):
                            xt = c.x[:, CH * q + t, :]
                            v.scalar_tensor_tensor(xt, YB[n % 2][:, t * D:(t + 1) * D], gates[:, CH * q + t, x:x + 1],
                                                   xt, ALU.mult, ALU.add).then_inc(added, 1)
                    if g == groups - 1:
                        v.wait_ge(added, 4 * (k + 1) * per_group)
                        ln_step(q, 0)
                    elif g < 2 and q > 0:
                        ln_step(q - 1, g + 1)
                ln_step(NC - 1, 1)
                ln_step(NC - 1, 2)


def copy_ln(c, act, q, xT_ready, xnT_ready, bank, double):
    act.wait_ge(xT_ready, q + 1)
    dst = c.xnT[:, 4 * q:4 * (q + 1), :].rearrange("p t n -> p (t n)")
    if double:
        act.activation(dst, bank[:, :], ACT.Identity, bias=double[1], scale=double[0]).then_inc(xnT_ready, 1)
    else:
        act.copy(dst, bank[:, :]).then_inc(xnT_ready, 1)


def ternary_ffn(c, w, tgate):
    nc = c.nc
    F = 512
    FT = F // P
    CH = 4
    NC = NT // CH
    eps = 1e-6
    pre = "F1_"
    sem = lambda n: c.sublayer_sem(pre + n)
    xh_all = sem("x_high")
    (prep, prep_pe, xs_ready, up_ready, g_ready, st_ready, mv_ready, rs_ready, hn_ready, hT_ready, hh_ready, hl_ready,
     y_ready, y_copied, yT_ready, added, st2_ready, mv2_ready, rs2_ready, xn_ready, xT_ready, xnT_ready) = (
        sem(n) for n in (
            "weights_step", "weights_sums", "x_split", "up_ready", "gelu_ready", "h_stats", "h_mv", "h_rstd", "h_normed",
            "hT_ready", "h_high", "h_low", "down_ready", "down_copied", "down_turned", "added", "ln_stats", "ln_mv",
            "ln_rstd", "ln_xn", "ln_xT", "ln_xnT"))
    UB, HB, YB, TB, LB = c.banks[0:2], c.banks[2:4], c.banks[4], c.banks[5], c.banks[6]
    with ExitStack() as own:
        sb = lambda n, s, d=F32: own.enter_context(nc.sbuf_tensor(pre + n, s, d))
        tmp = sb("tmp", [P, 2, F])
        wf = sb("wf", [P, F], F32R)
        wp = sb("wp", [P, FT, D], F32R)
        sums = sb("sums", [P, 2])
        thr = sb("thr", [P, 2, 2])
        lnb = sb("lnb", [P, FT, P])
        bt = sb("bt", [P, D])
        xh = sb("xh", [P, NT, P], F32R)
        xl = sb("xl", [P, NT, P], F32R)
        hg = sb("hg", [P, 2, F])
        hn = sb("hn", [P, 2, F])
        hh = sb("hh", [P, 2, FT, CH, P], F32R)
        hl = sb("hl", [P, 2, FT, CH, P], F32R)
        yT = sb("yT", [P, F])
        st1 = sb("st1", [P, 6])
        mv1 = sb("mv1", [P, 2, 2])
        ve1 = sb("ve1", [P, 1])
        rs1 = sb("rs1", [P, 2, 1])
        ln = layer_norm_tail(c, own, pre)
        st, mv, ve, rstd, xn = (ln[k] for k in ("st", "mv", "ve", "rstd", "xn"))
        WF, WP = w["WfT"], w["WpT"].rearrange("p (j d) -> p j d", j=FT)

        with nc.Block() as block:
            @block.tensor
            def _(pe):
                for s, all_loads in w["loaded"]:
                    pe.wait_ge(s, all_loads)
                pe.wait_ge(prep, 2)
                pe.matmul(LB[:, 0:2], c.ones[:], sums[:], start=True, stop=True).then_inc(prep_pe, 1)
                pe.wait_ge(prep, 9)
                for j in range(FT):
                    m = pe.matmul(TB[:, 0:D], lnb[:, j, :], wp[:, j, :].bitcast(F32), start=(j == 0), stop=(j == FT - 1))
                m.then_inc(prep_pe, 1)

                def up(t):
                    if t % CH == 0:
                        pe.wait_ge(xs_ready, 2 * (t // CH + 1))
                    need(pe, g_ready, t - 1)
                    pe.matmul(UB[t % 2][:, :], xh[:, t, :], wf[:], start=True, stop=False)
                    pe.matmul(UB[t % 2][:, :], xl[:, t, :], wf[:], start=False, stop=True).then_inc(up_ready, 1)

                def turn(t):
                    pe.wait_ge(hn_ready, t + 1)
                    need(pe, hl_ready, t - 1)
                    for j in range(FT):
                        m = pe.transpose(HB[t % 2][:, j * P:(j + 1) * P], hn[:, t % 2, j * P:(j + 1) * P], c.ident[:])
                    m.then_inc(hT_ready, 1)

                def down(q):
                    pe.wait_ge(hl_ready, CH * (q + 1))
                    need(pe, y_copied, q)
                    n = 0
                    for part in (hh, hl):
                        for j in range(FT):
                            m = pe.matmul(YB[:, :], wp[:, j, :], part[:, q % 2, j].rearrange("p t n -> p (t n)"),
                                          start=(n == 0), stop=(n == 2 * FT - 1))
                            n += 1
                    m.then_inc(y_ready, 1)

                def turn_y(q):
                    pe.wait_ge(y_copied, q + 1)
                    need(pe, added, q)
                    if q == 0:
                        pe.wait_ge(prep, 11)
                    for t in range(CH):
                        m = pe.transpose(TB[:, t * P:(t + 1) * P], yT[:, t * P:(t + 1) * P], c.ident[:])
                    m.then_inc(yT_ready, 1)

                def turn_ln(q):
                    pe.wait_ge(xn_ready, CH * (q + 1))
                    need(pe, xnT_ready, q)
                    for t in range(CH):
                        m = pe.transpose(LB[:, t * P:(t + 1) * P], xn[:, t, :], c.ident[:])
                    m.then_inc(xT_ready, 1)

                LAG = 2
                for t in range(NT + 12):
                    if t < NT:
                        up(t)
                    if 0 <= t - LAG < NT:
                        turn(t - LAG)
                    if t - 4 >= 0 and (t - 4) % CH == CH - 1 and (t - 4) // CH < NC:
                        down((t - 4) // CH)
                    if t - 6 >= 0 and (t - 6) % CH == CH - 1 and (t - 6) // CH < NC:
                        turn_y((t - 6) // CH)
                    if t - 8 >= 0 and (t - 8) % CH == CH - 1 and (t - 8) // CH < NC:
                        turn_ln((t - 8) // CH)

            @block.scalar
            def _(act):
                for s, all_loads in w["loaded"]:
                    act.wait_ge(s, all_loads)
                act.copy(xh[:], c.xnT[:]).then_inc(xh_all, 1)
                for t in range(NT + 12):
                    if t < NT:
                        act.wait_ge(up_ready, t + 1)
                        need(act, hn_ready, t - 1)
                        act.activation(hg[:, t % 2, :], UB[t % 2][:, :], ACT.Gelu).then_inc(g_ready, 1)
                    if 0 <= t - 2 < NT:
                        n = t - 2
                        act.wait_ge(hT_ready, n + 1)
                        need(act, y_ready, n // CH - 1)
                        for j in range(FT):
                            i = act.activation(hh[:, n // CH % 2, j, n % CH, :], HB[n % 2][:, j * P:(j + 1) * P],
                                               ACT.Copy, scale=w["lnw"][:, j:j + 1])
                        i.then_inc(hh_ready, 1)
                    if t - 4 >= 0 and (t - 4) % CH == CH - 1 and (t - 4) // CH < NC:
                        q = (t - 4) // CH
                        act.wait_ge(y_ready, q + 1)
                        need(act, yT_ready, q)
                        act.copy(yT[:], YB[:, :]).then_inc(y_copied, 1)
                    if t - 8 >= 0 and (t - 8) % CH == CH - 1 and (t - 8) // CH < NC:
                        copy_ln(c, act, (t - 8) // CH, xT_ready, xnT_ready, LB, None)

            @block.gpsimd
            def _(g):
                a, b = 0, 0
                for t in range(NT + 12):
                    if t < NT:
                        g.wait_ge(mv_ready, t + 1)
                        need(g, rs_ready, 2 * t)
                        g.tensor_scalar(ve1[:], mv1[:, t % 2, 1:2], LN_EPS, None, ALU.add).then_inc(rs_ready, 1)
                        g.wait_ge(rs_ready, 2 * t + 1)
                        g.tensor_tensor(rs1[:, t % 2], ve1[:], c.mhalf[:, 0:1], ALU.pow).then_inc(rs_ready, 1)
                    if t - 7 >= 0 and (t - 7) % CH == CH - 1 and (t - 7) // CH < NC:
                        q = (t - 7) // CH
                        g.wait_ge(mv2_ready, CH * (q + 1))
                        g.tensor_scalar(ve[:], mv[:, :, 1], LN_EPS, None, ALU.add).then_inc(rs2_ready, 1)
                        g.wait_ge(rs2_ready, 2 * q + 1)
                        g.tensor_tensor(rstd[:], ve[:], c.mhalf[:, 0:4], ALU.pow).then_inc(rs2_ready, 1)

            @block.vector
            def _(v):
                count = [0]

                def chain(i):
                    count[0] += 1
                    i.then_inc(prep, 1)
                    v.wait_ge(prep, count[0])

                for s, all_loads in w["loaded"]:
                    v.wait_ge(s, all_loads)
                chain(v.tensor_reduce(sums[:, 0:1], WF, AX.X, ALU.add, apply_absolute_value=True))
                chain(v.tensor_reduce(sums[:, 1:2], w["WpT"], AX.X, ALU.add, apply_absolute_value=True))
                v.wait_ge(prep_pe, 1)
                half = 0.5 / (D * F)
                chain(v.tensor_scalar(thr[:, 0], LB[:, 0:2], half, 0.5 * eps, ALU.mult, ALU.add))
                chain(v.tensor_scalar(thr[:, 1], thr[:, 0], -1.0, None, ALU.mult))
                chain(v.tensor_scalar(tmp[:, 0, :], WF, thr[:, 1, 0:1], None, ALU.is_lt))
                chain(v.scalar_tensor_tensor(wf[:], WF, thr[:, 0, 0:1], tmp[:, 0, :], ALU.is_gt, ALU.subtract))
                chain(v.tensor_scalar(tmp[:, 1, :], w["WpT"], thr[:, 1, 1:2], None, ALU.is_lt))
                chain(v.scalar_tensor_tensor(wp[:].rearrange("p j d -> p (j d)"), w["WpT"], thr[:, 0, 1:2], tmp[:, 1, :],
                                             ALU.is_gt, ALU.subtract))
                for j in range(FT):
                    i = v.tensor_scalar(lnb[:, j, :], c.ones[:], w["lnb"][:, j:j + 1], None, ALU.mult)
                chain(i)
                v.wait_ge(prep_pe, 2)
                chain(v.tensor_scalar(bt[:], TB[:, 0:D], tgate, None, ALU.mult))
                chain(v.tensor_tensor(c.x[:], c.x[:], bt[:].rearrange("p (a d) -> p a d", a=1).broadcast_to([P, NT, D]),
                                      ALU.add))
                v.wait_ge(xh_all, 1)
                for q in range(NC):
                    s = slice(CH * q, CH * (q + 1))
                    v.tensor_tensor(xl[:, s, :], c.xnT[:, s, :], xh[:, s, :].bitcast(F32),
                                    ALU.subtract).then_inc(xs_ready, 2)

                def low(n):
                    v.wait_ge(hh_ready, n + 1)
                    for j in range(FT):
                        i = v.scalar_tensor_tensor(hl[:, n // CH % 2, j, n % CH, :], HB[n % 2][:, j * P:(j + 1) * P],
                                                   w["lnw"][:, j:j + 1], hh[:, n // CH % 2, j, n % CH, :].bitcast(F32),
                                                   ALU.mult, ALU.subtract)
                    i.then_inc(hl_ready, 1)

                for t in range(NT + 12):
                    if t < NT:
                        v.wait_ge(g_ready, t + 1)
                        need(v, mv_ready, t)
                        v.bn_stats(st1[:], hg[:, t % 2, :]).then_inc(st_ready, 1)
                        v.wait_ge(st_ready, t + 1)
                        need(v, rs_ready, 2 * (t - 1) + 1)
                        v.bn_aggr(mv1[:, t % 2, :], st1[:]).then_inc(mv_ready, 1)
                    if 0 <= t - 1 < NT:
                        n = t - 1
                        v.wait_ge(rs_ready, 2 * n + 2)
                        need(v, hT_ready, n - 1)
                        v.tensor_scalar(hn[:, n % 2, :], hg[:, n % 2, :], mv1[:, n % 2, 0:1], rs1[:, n % 2, 0:1],
                                        ALU.subtract, ALU.mult).then_inc(hn_ready, 1)
                    if 0 <= t - 2 < NT:
                        low(t - 2)
                    if t - 6 >= 0 and (t - 6) % CH == CH - 1 and (t - 6) // CH < NC:
                        q = (t - 6) // CH
                        v.wait_ge(yT_ready, q + 1)
                        xs = c.x[:, CH * q:CH * (q + 1), :].rearrange("p t n -> p (t n)")
                        v.scalar_tensor_tensor(xs, TB[:, :], tgate, xs, ALU.mult, ALU.add).then_inc(added, 1)
                        v.wait_ge(added, q + 1)
                        for k in range(CH):
                            v.bn_stats(st[:, k, :], c.x[:, CH * q + k, :]).then_inc(st2_ready, 1)
                        v.wait_ge(st2_ready, CH * (q + 1))
                        for k in range(CH):
                            v.bn_aggr(mv[:, k, :], st[:, k, :]).then_inc(mv2_ready, 1)
                    if t - 8 >= 0 and (t - 8) % CH == CH - 1 and (t - 8) // CH < NC:
                        q = (t - 8) // CH
                        v.wait_ge(mv2_ready, CH * (q + 1))
                        v.wait_ge(rs2_ready, 2 * (q + 1))
                        need(v, xT_ready, q)
                        for k in range(CH):
                            v.tensor_scalar(xn[:, k, :], c.x[:, CH * q + k, :], mv[:, k, 0:1], rstd[:, k:k + 1],
                                            ALU.subtract, ALU.mult).then_inc(xn_ready, 1)


def wide_attention(c, w, next_loads, gate):
    nc = c.nc
    W64 = 64
    NP = H // 2
    M = B * NP
    SC = 0.125
    NPS, TRS, QKB, VB, OB, MISC = c.banks[0:2], c.banks[2:4], c.banks[4], c.banks[5], c.banks[6], c.banks[7]
    pre = "L1_"
    sem = lambda n: c.sublayer_sem(pre + n)
    (ct0, ct1, zeroed, gate_ready, qk_ready, hi_ready, lo_ready, n_ready, max_ready, p_ready, rc_ready, norm0_ready, norm1_ready,
     tr_ready, pt_even, pt_odd, pv_ready, o_ready, vp_ready, v_ready, po_ready, resid, st_ready, mv_ready, rstd_ready,
     xn_ready, xT_ready, xnT_ready) = (sem(n) for n in (
         "ctx_loaded0", "ctx_loaded1", "zeroed", "gate_ready", "qk_projected", "split_high", "split_low",
         "scores_ready", "max_ready", "exp_ready", "recip_ready", "probs_normed0", "probs_normed1", "probs_turned", "probsT_even", "probsT_odd",
         "pv_ready", "ctx_copied", "v_projected", "v_ready", "out_ready", "resid_ready", "ln_stats", "ln_mv",
         "ln_rstd", "ln_xn", "ln_xT", "ln_xnT"))
    ct_in = [ct0, ct1]
    with ExitStack() as own:
        sb = lambda n, s, d=F32: own.enter_context(nc.sbuf_tensor(pre + n, s, d))
        ct = sb("ct", [P, 2, S])
        qh = sb("qh", [P, 2, 2, S], F32R)
        ql = sb("ql", [P, 2, 2, S], F32R)
        kh = sb("kh", [P, 2, S], F32R)
        kl = sb("kl", [P, 2, S], F32R)
        nm = sb("nm", [P, 4, TPB])
        sm = sb("sm", [P, 4, TPB])
        rs = sb("rs", [P, 4, TPB])
        pn = sb("pn", [P, 4, TPB, S])
        pt = sb("pt", [P, 4, TPB, S])
        vv = sb("vv", [P, 2, TPB, H * W64])
        oT = sb("oT", [P, 2, NP, S])
        g2 = sb("g2", [P, 1])
        st = sb("st", [P, TPB, 6])
        mv = sb("mv", [P, TPB, 2])
        ve = sb("ve", [P, TPB])
        rstd = sb("rstd", [P, TPB])
        xn = sb("xn", [P, TPB, D])

        with nc.Block() as block:
            @block.sync
            def _(sp):
                for b in range(B):
                    if b >= 2:
                        sp.wait_ge(qk_ready, NP * (b - 1))
                        sp.wait_ge(vp_ready, 4 * (b - 1))
                    sp.dma_start(ct[:, b % 2, :], c.a["ctxT"][:, b * S:(b + 1) * S]).then_inc(ct_in[b % 2], 16)
                    if b == 1:
                        for s, dst, src in next_loads:
                            sp.dma_start(dst, src).then_inc(s, 16)

            @block.tensor
            def _(pe):
                def project(m):
                    b, p = divmod(m, NP)
                    need(pe, lo_ready, 3 * m)
                    pe.wait_ge(ct_in[b % 2], 16 * (b // 2 + 1))
                    xs = c.xnT[:, TPB * b:TPB * (b + 1), :].rearrange("p t n -> p (t n)")
                    pe.matmul(QKB[:, 0:S], w["Wq"][:, p * P:(p + 1) * P], xs, start=True, stop=True)
                    pe.matmul(QKB[:, S:2 * S], w["Wk"][:, p * P:(p + 1) * P], ct[:, b % 2, :],
                              start=True, stop=True).then_inc(qk_ready, 1)

                def project_v(b, i):
                    t, half = divmod(i, 2)
                    need(pe, v_ready, 4 * b + i)
                    pe.wait_ge(ct_in[b % 2], 16 * (b // 2 + 1))
                    pe.matmul(VB[:, :], ct[:, b % 2, t * P:(t + 1) * P], w["Wv"][:, half * 512:(half + 1) * 512],
                              start=True, stop=True).then_inc(vp_ready, 1)

                def scores(n):
                    m, s = divmod(n, 2)
                    if s == 0:
                        pe.wait_ge(lo_ready, 3 * (m + 1))
                    need(pe, p_ready, 2 * (n - 1))
                    for t in range(TPB):
                        o = NPS[n % 2][:, t * S:(t + 1) * S]
                        q = slice(t * P, (t + 1) * P)
                        pe.matmul(o, qh[:, m % 2, s, q], kh[:, m % 2, :], start=True, stop=False)
                        pe.matmul(o, qh[:, m % 2, s, q], kl[:, m % 2, :], start=False, stop=False)
                        i = pe.matmul(o, ql[:, m % 2, s, q], kh[:, m % 2, :], start=False, stop=True)
                    i.then_inc(n_ready, 1)

                def turn(n):
                    pe.wait_ge(norm0_ready, n + 1)
                    pe.wait_ge(norm1_ready, n + 1)
                    need(pe, (pt_even, pt_odd)[n % 2], n // 2)
                    for k in range(TPB):
                        for t in range(TPB):
                            i = pe.transpose(TRS[n % 2][:, k * S + t * P:k * S + (t + 1) * P],
                                             pn[:, n % 4, t, k * P:(k + 1) * P], c.ident[:])
                    i.then_inc(tr_ready, 1)

                def pv(m):
                    b, p = divmod(m, NP)
                    pe.wait_ge(pt_even, m + 1)
                    pe.wait_ge(pt_odd, m + 1)
                    need(pe, o_ready, m)
                    pe.wait_ge(v_ready, 4 * (b + 1))
                    for k in range(TPB):
                        for s in range(2):
                            h = 2 * p + s
                            i = pe.matmul(OB[W64 * s:W64 * (s + 1), 0:S], vv[:, b % 2, k, h * W64:(h + 1) * W64],
                                          pt[:, (2 * m + s) % 4, k, :], start=(k == 0), stop=(k == 1))
                    i.then_inc(pv_ready, 1)

                def out(b):
                    pe.wait_ge(o_ready, NP * (b + 1))
                    need(pe, xnT_ready, b)
                    for t in range(TPB):
                        o = MISC[:, t * D:(t + 1) * D]
                        for p in range(NP):
                            pe.matmul(o, oT[:, b % 2, p, t * P:(t + 1) * P], w["Wo"][:, p * D:(p + 1) * D],
                                      start=(p == 0), stop=False)
                        i = pe.matmul(o, c.ones[0:1, :], w["bo"], start=False, stop=True)
                    i.then_inc(po_ready, 1)

                def turn_ln(b):
                    pe.wait_ge(xn_ready, 2 * (b + 1))
                    for t in range(TPB):
                        i = pe.transpose(MISC[:, t * P:(t + 1) * P], xn[:, t, :], c.ident[:])
                    i.then_inc(xT_ready, 1)

                for s, all_loads in w["loaded"]:
                    pe.wait_ge(s, all_loads)
                project(0)
                for m in range(M + 8):
                    b, p = divmod(m, NP)
                    for s in range(2):
                        n = 2 * m + s
                        if m < M:
                            scores(n)
                        if s == 0 and m + 1 < M:
                            project(m + 1)
                        if m == 0 and s == 0:
                            for i in range(4):
                                project_v(0, i)
                        if 0 <= n - 3 < 2 * M:
                            turn(n - 3)
                        if s == 0 and 0 <= m - 3 < M:
                            pv(m - 3)
                    if 3 <= p < 7 and b + 1 < B:
                        project_v(b + 1, p - 3)
                    if m >= 12 and (m - 12) % NP == 0 and (m - 12) // NP < B:
                        out((m - 12) // NP)
                    if m >= 15 and (m - 15) % NP == 0 and (m - 15) // NP < B:
                        turn_ln((m - 15) // NP)

            @block.scalar
            def _(act):
                def split(m):
                    act.wait_ge(qk_ready, m + 1)
                    need(act, n_ready, 2 * (m - 1))
                    for s in range(2):
                        r = slice(W64 * s, W64 * (s + 1))
                        act.activation(qh[r, m % 2, s, :], QKB[r, 0:S], ACT.Copy, scale=SC).then_inc(hi_ready, 1)
                    act.copy(kh[:, m % 2, :], QKB[:, S:2 * S]).then_inc(hi_ready, 1)

                def copy_v(b, i):
                    t, half = divmod(i, 2)
                    act.wait_ge(vp_ready, 4 * b + i + 1)
                    need(act, pv_ready, NP * (b - 1))
                    act.copy(vv[:, b % 2, t, half * 512:(half + 1) * 512], VB[:, :]).then_inc(v_ready, 1)

                for s, all_loads in w["loaded"]:
                    act.wait_ge(s, all_loads)
                act.activation(g2[:], w["gate"], ACT.Tanh).then_inc(gate_ready, 1)
                act.wait_ge(gate_ready, 1)
                act.activation(g2[:], g2[:], ACT.Copy, scale=gate).then_inc(gate_ready, 1)
                act.wait_ge(zeroed, 2)
                split(0)
                for m in range(M + 8):
                    b, p = divmod(m, NP)
                    for s in range(2):
                        n = 2 * m + s
                        if s == 0 and m + 1 < M:
                            split(m + 1)
                        if s == 1 and 0 <= n - 4 < 2 * M:
                            k = n - 4
                            act.wait_ge(tr_ready, k + 1)
                            need(act, pv_ready, k // 2 - 1)
                            act.copy(pt[:, k % 4].rearrange("p t n -> p (t n)"), TRS[k % 2][:, :]).then_inc(pt_odd, 1)
                        if m < M:
                            act.wait_ge(max_ready, n + 1)
                            need(act, tr_ready, n - 3)
                            for t in range(TPB):
                                act.activation(pn[:, n % 4, t, :], NPS[n % 2][:, t * S:(t + 1) * S], ACT.Exp,
                                               bias=nm[:, n % 4, t:t + 1],
                                               accum_out=sm[:, n % 4, t:t + 1]).then_inc(p_ready, 1)
                        if m == 0 and s == 0:
                            for i in range(4):
                                copy_v(0, i)
                        if s == 0 and 0 <= m - 3 < M:
                            k = m - 3
                            act.wait_ge(pv_ready, k + 1)
                            if k % NP == 0:
                                need(act, po_ready, k // NP - 1)
                            act.copy(oT[:, k // NP % 2, k % NP, :], OB[:, 0:S]).then_inc(o_ready, 1)
                    if 3 <= p < 7 and b + 1 < B:
                        copy_v(b + 1, p - 3)
                    if m >= 15 and (m - 15) % NP == 0 and (m - 15) // NP < B:
                        k = (m - 15) // NP
                        act.wait_ge(xT_ready, k + 1)
                        act.copy(c.xnT[:, TPB * k:TPB * (k + 1), :].rearrange("p t n -> p (t n)"),
                                 MISC[:, 0:S]).then_inc(xnT_ready, 1)

            @block.gpsimd
            def _(g):
                g.memset(ql[:].bitcast(F32), 0.0).then_inc(zeroed, 1)
                for m in range(M + 8):
                    for s in range(2):
                        n = 2 * m + s
                        if m < M:
                            g.wait_ge(rc_ready, n + 1)
                            g.tensor_scalar(pn[:, n % 4, 0, :], pn[:, n % 4, 0, :], rs[:, n % 4, 0:1], None,
                                            ALU.mult).then_inc(norm0_ready, 1)
                    if m >= 13 and (m - 13) % NP == 0 and (m - 13) // NP < B:
                        k = (m - 13) // NP
                        g.wait_ge(mv_ready, 2 * (k + 1))
                        g.tensor_scalar(ve[:], mv[:, :, 1], LN_EPS, None, ALU.add).then_inc(rstd_ready, 1)
                        g.wait_ge(rstd_ready, 2 * k + 1)
                        g.tensor_tensor(rstd[:], ve[:], c.mhalf[:, 0:TPB], ALU.pow).then_inc(rstd_ready, 1)

            @block.vector
            def _(v):
                def split(m):
                    v.wait_ge(hi_ready, 3 * (m + 1))
                    for s in range(2):
                        r = slice(W64 * s, W64 * (s + 1))
                        v.scalar_tensor_tensor(ql[r, m % 2, s, :], QKB[r, 0:S], SC, qh[r, m % 2, s, :].bitcast(F32),
                                               ALU.mult, ALU.subtract).then_inc(lo_ready, 1)
                    v.tensor_tensor(kl[:, m % 2, :], QKB[:, S:2 * S], kh[:, m % 2, :].bitcast(F32),
                                    ALU.subtract).then_inc(lo_ready, 1)

                def recip(n):
                    v.wait_ge(p_ready, 2 * (n + 1))
                    v.reciprocal(rs[:, n % 4, :], sm[:, n % 4, :]).then_inc(rc_ready, 1)

                v.memset(qh[:].bitcast(F32), 0.0).then_inc(zeroed, 1)
                for s, all_loads in w["loaded"]:
                    v.wait_ge(s, all_loads)
                v.wait_ge(zeroed, 2)
                split(0)
                for m in range(M + 8):
                    for s in range(2):
                        n = 2 * m + s
                        if m < M:
                            v.wait_ge(n_ready, n + 1)
                            v.tensor_reduce(nm[:, n % 4, :], NPS[n % 2][:, :].rearrange("p (t n) -> p t n", t=TPB),
                                            AX.X, ALU.max, negate=True).then_inc(max_ready, 1)
                        if 0 <= n - 1 < 2 * M:
                            recip(n - 1)
                        if 0 <= n - 1 < 2 * M:
                            k = n - 1
                            v.wait_ge(rc_ready, k + 1)
                            v.tensor_scalar(pn[:, k % 4, 1, :], pn[:, k % 4, 1, :], rs[:, k % 4, 1:2], None,
                                            ALU.mult).then_inc(norm1_ready, 1)
                        if s == 0 and 0 <= n - 4 < 2 * M:
                            k = n - 4
                            v.wait_ge(tr_ready, k + 1)
                            need(v, pv_ready, k // 2 - 1)
                            v.tensor_copy(pt[:, k % 4].rearrange("p t n -> p (t n)"), TRS[k % 2][:, :]).then_inc(pt_even, 1)
                        if s == 0 and m + 1 < M:
                            split(m + 1)
                    if m >= 12 and (m - 12) % NP == 0 and (m - 12) // NP < B:
                        k = (m - 12) // NP
                        v.wait_ge(po_ready, k + 1)
                        if k == 0:
                            v.wait_ge(gate_ready, 2)
                        xs = c.x[:, TPB * k:TPB * (k + 1), :].rearrange("p t n -> p (t n)")
                        v.scalar_tensor_tensor(xs, MISC[:, 0:S], g2[:, 0:1], xs, ALU.mult, ALU.add).then_inc(resid, 1)
                        v.wait_ge(resid, k + 1)
                        for t in range(TPB):
                            v.bn_stats(st[:, t, :], c.x[:, TPB * k + t, :]).then_inc(st_ready, 1)
                        v.wait_ge(st_ready, 2 * (k + 1))
                        for t in range(TPB):
                            v.bn_aggr(mv[:, t, :], st[:, t, :]).then_inc(mv_ready, 1)
                    if m >= 14 and (m - 14) % NP == 0 and (m - 14) // NP < B:
                        k = (m - 14) // NP
                        v.wait_ge(mv_ready, 2 * (k + 1))
                        v.wait_ge(rstd_ready, 2 * (k + 1))
                        need(v, xT_ready, k)
                        for t in range(TPB):
                            v.tensor_scalar(xn[:, t, :], c.x[:, TPB * k + t, :], mv[:, t, 0:1], rstd[:, t:t + 1],
                                            ALU.subtract, ALU.mult).then_inc(xn_ready, 1)


def window_mask(c, name, window):
    W = P + window
    m = c.sb(name, [P, TPB, W], BF16)
    return m, window


def build_masks(c, masks):
    nc = c.nc
    made = c.sem("masks_made")
    with nc.Block() as block:
        @block.gpsimd
        def _(g):
            n = 0
            for m, window in masks:
                g.memset(m[:], 0.0).then_inc(made, 1)
                n += 1
                g.wait_ge(made, n)
                W = P + window
                for t in range(TPB):
                    off = window * t
                    g.affine_select(out=m[:, t, :], in_=m[:, t, :], compare_op=ALU.is_ge, fill=NEG,
                                    base=off + window, pattern=[[-1, W]], channel_multiplier=1).then_inc(made, 1)
                    n += 1
                    g.wait_ge(made, n)
                    g.affine_select(out=m[:, t, :], in_=m[:, t, :], compare_op=ALU.is_ge, fill=NEG,
                                    base=window - off, pattern=[[1, W]], channel_multiplier=-1).then_inc(made, 1)
                    n += 1
                    g.wait_ge(made, n)


def program(nc, a, out, stages=range(8)):
    with ExitStack() as ctx:
        c = Chip(nc, ctx, a)
        stored = c.sem("stored")
        weights = []

        def load(name, shape, src, sems, place=None, after=None):
            t = c.sb("w_" + name, shape, F32)[:] if place is None else place
            if not sems:
                sems.append([c.sem("ld_" + name), 0])
            sems[0][1] += 16
            (weights if after is None or after + 1 not in stages else late[after]).append((sems[0][0], t, src))
            return t

        late = {1: [], 3: []}
        early, middle = c.sb("place_early", [P, 8192], F32), c.sb("place_middle", [P, 8192], F32)

        masks = []
        W = {}
        if 0 in stages:
            l = []
            w = {k: load("L0" + k, [P, P], a["L0_" + k], l) for k in ("WqT", "WkT", "WvT", "WoT")}
            w["bq"] = load("L0bq", [P, 1], col(a["L0_bq"]), l)
            w["bk"] = load("L0bk", [P, 1], col(a["L0_bk"]), l)
            w["bv"] = load("L0bv", [P, D], a["L0_bv"].partition_broadcast(P), l)
            w["bo"] = load("L0bo", [1, D], row(a["L0_bo"]), l)
            m = window_mask(c, "mask64", 64)
            masks.append(m)
            w["mask"] = m[0]
            w["loaded"] = l
            W[0] = w
        def cst(key, shape, l):
            return load(key, shape, a[key], l)

        if 1 in stages:
            l = []
            w = dict(F=341, capacity=256, steps_to_probs=6)
            w["Wr"] = load("F0Wr", [P, 8], a["F0_Wr"], l)
            w["br"] = load("F0br", [P, 8], a["F0_br"].partition_broadcast(P), l)
            w["W1"] = load("F0W1", None, a["F0_W1"], l, early[:, 0:1536])
            w["b1"] = load("F0b1", [P, 12], a["F0_b1"], l)
            w["W2"] = load("F0W2", None, a["F0_W2"], l, early[:, 1536:1536 + 24 * D])
            w["b2"] = load("F0b2", [8, D], a["F0_b2"], l)
            w["same_expert"] = cst("same_expert", [P, P], l)
            w["earlier_tile"] = cst("earlier_tile", [P, P], l)
            w["ln1"] = load("ln1", [P, 2], a["L1_ln"], l)
            w["loaded"] = l
            W[1] = w
        if 2 in stages:
            l = []
            W[2] = dict(Wq=load("L1Wq", None, a["L1_Wq"], l, middle[:, 0:1024]), Wk=load("L1Wk", None, a["L1_Wkv"][:, 0:1024], l, middle[:, 1024:2048]),
                        Wv=load("L1Wv", None, a["L1_Wkv"][:, 1024:2048], l, middle[:, 2048:3072]), Wo=load("L1Wo", None, a["L1_Wo"], l, middle[:, 3072:4096]),
                        bo=load("L1bo", [1, D], row(a["L1_bo"]), l),
                        gate=load("L1gate", [P, 1], a["L1_gate"].partition_broadcast(P), l), loaded=l)
        if 3 in stages:
            l = []
            W[3] = dict(WfT=load("F1Wf", None, a["F1_WfT"], l, middle[:, 4096:4608]), WpT=load("F1Wp", None, a["F1_WpT"], l, middle[:, 4608:5120]),
                        lnw=load("F1lnw", [P, 4], a["F1_lnw"], l), lnb=load("F1lnb", [P, 4], a["F1_lnb"], l), loaded=l)
        if 4 in stages:
            l = []
            w = {k: load("L2" + k, [P, P], a["L2_" + k], l) for k in ("WqT", "WkT", "WkTs", "WoT", "WvT", "WvTs")}
            w["bo"] = load("L2bo", [1, D], row(a["L2_bo"]), l)
            w["cosT"] = load("cosT", [P, S], a["rope_cosT"], l)
            w["sinT"] = load("sinT", [P, S], a["rope_sinT"], l)
            w["cs"] = load("rope_cs", [P, 2, TPB, D], a["rope_cs"], l)
            w["bq"] = 0.0
            w["loaded"] = l
            W[4] = w
        if 6 in stages:
            l = []
            w = {k: load("L3" + k, [P, P], a["L3_" + k], l) for k in ("WqT", "WvT", "WoT")}
            w["WkT"] = w["WqT"]
            w["bo"] = load("L3bo", [1, D], row(a["L3_bo"]), l)
            w["bq"] = w["bk"] = 0.0
            w["bv"] = None
            m = window_mask(c, "mask64b", 64) if 0 not in stages else (W[0]["mask"],)
            if 0 not in stages:
                masks.append(m)
            w["mask"] = m[0]
            w["loaded"] = l
            W[6] = w
        before_l = []
        if 5 in stages or 7 in stages:
            before = load("before", [P, 64], a["before"].partition_broadcast(P), before_l)

        if 5 in stages:
            l = []
            w = dict(F=512, before=before)
            w["Wr"] = load("F2Wr", [P, 8], a["F2_Wr"], l)
            w["br"] = load("F2br", [P, 8], a["F2_br"].partition_broadcast(P), l)
            w["W1"] = load("F2W1", None, a["F2_W1"], l, middle[:, 0:4096], 3)
            w["b1"] = load("F2b1", [P, 32], a["F2_b1"], l)
            w["W2"] = load("F2W2", None, a["F2_W2"], l, middle[:, 4096:8192], 3)
            w["b2"] = load("F2b2", [8, D], a["F2_b2"], l)
            w["loaded"] = l + before_l
            W[5] = w
        if 7 in stages:
            l = []
            w = dict(F=512, before=before, br=None, b1=None, b2=None)
            w["Wr"] = load("F3Wr", [P, 8], a["F3_Wr"], l)
            w["W1"] = load("F3W1", None, a["F3_W1"], l, early[:, 0:4096], 1)
            w["W2"] = load("F3W2", None, a["F3_W2"], l, early[:, 4096:8192], 1)
            w["loaded"] = l + before_l
            W[7] = w
        start_block(c, weights)
        build_masks(c, masks)
        if 0 in stages:
            attention(c, 0, W[0], c.gates_t[:, 0:1], window=64)
            c.end_sublayer()
        if 1 in stages:
            w = W[1]
            ffn(c, 0, w, c.gates_t[:, 4:5], 8, 2, ACT.Silu, "experts", double=(w["ln1"][:, 0:1], w["ln1"][:, 1:2]))
            c.end_sublayer()
        if 2 in stages:
            wide_attention(c, W[2], late[1], c.gates_t[:, 1:2])
            c.end_sublayer()
        if 3 in stages:
            ternary_ffn(c, W[3], c.gates_t[:, 5:6])
            c.end_sublayer()
        if 4 in stages:
            attention(c, 2, W[4], c.gates_t[:, 2:3], rope=True, next_loads=late[3])
            c.end_sublayer()
        if 5 in stages:
            ffn(c, 2, W[5], c.gates_t[:, 6:7], 8, 1, ACT.Gelu, "first")
            c.end_sublayer()
        if 6 in stages:
            attention(c, 3, W[6], c.gates_t[:, 3:4], window=64)
            c.end_sublayer()
        if 7 in stages:
            ffn(c, 3, W[7], c.gates_t[:, 7:8], 8, 1, ACT.Gelu_apprx_tanh, "four")
            c.end_sublayer()
        with nc.Block() as block:
            @block.sync
            def _(sp):
                sp.dma_start(out, c.x[:]).then_inc(stored, 16)
                sp.wait_ge(stored, 16)


def feature_first(w):
    return w.reshape(*w.shape[:-1], 2, HU, DH).swapaxes(-1, -2).reshape(w.shape)


def layout(i):
    o = {}
    tiles = lambda x: np.ascontiguousarray(x.reshape(NT, P, D).transpose(1, 0, 2))
    o["x"] = tiles(i["x"])
    o["ctxT"] = i["ctx_1024"].reshape(B * S, D).T
    o["g_xattn"], o["g_ffn"] = i["g_xattn"], i["g_ffn"]
    o["L0_WqT"] = feature_first(i["L0_xattn_Wq"].T)
    o["L0_WkT"] = feature_first(i["L0_xattn_Wk"].T)
    o["L0_WvT"] = i["L0_xattn_Wv"].T
    o["L0_WoT"] = i["L0_xattn_Wo"].T
    o["L0_bq"] = feature_first(i["L0_xattn_bq"])
    o["L0_bk"] = feature_first(i["L0_xattn_bk"])
    o["L0_bv"], o["L0_bo"] = i["L0_xattn_bv"], i["L0_xattn_bo"]
    f_tiles = lambda v, F: np.pad(v, [(0, 0), (0, -F % P)] + [(0, 0)] * (v.ndim - 2))
    for L, p, F in ((0, "L0_ffn_", 341), (2, "L2_ffn_", 512), (3, "L3_ffn_", 512)):
        n = {0: ("Wr", "W_up", "W_down"), 2: ("Wr", "W1", "W2"), 3: ("router_w", "up_w", "down_w")}[L]
        wr, w1, w2 = (i[p + k] for k in n)
        o[f"F{L}_Wr"] = wr
        o[f"F{L}_W1"] = np.pad(w1.transpose(1, 0, 2), [(0, 0), (0, 0), (0, -F % P)]).reshape(D, -1)
        w2 = f_tiles(w2, F)
        o[f"F{L}_W2"] = w2.reshape(8, -1, P, D).transpose(2, 0, 1, 3).reshape(P, -1)
    for L, p, F, br, b1, b2 in ((0, "L0_ffn_", 341, "br", "b_up", "b_down"), (2, "L2_ffn_", 512, "br", "b1", "b2")):
        o[f"F{L}_br"] = i[p + br]
        o[f"F{L}_b1"] = f_tiles(i[p + b1], F).reshape(-1, P).T
        o[f"F{L}_b2"] = i[p + b2]
    o["L1_Wq"], o["L1_Wkv"] = i["L1_xattn_w_q"], i["L1_xattn_w_kv"]
    o["L1_Wo"] = i["L1_xattn_w_out"].reshape(8, P, D).transpose(1, 0, 2).reshape(P, -1)
    o["L1_bo"], o["L1_gate"] = i["L1_xattn_b_out"], i["L1_xattn_gate"]
    o["F1_WfT"] = i["L1_ffn_W_fc"].T
    o["F1_WpT"] = i["L1_ffn_W_proj"].T.reshape(4, P, D).transpose(1, 0, 2).reshape(P, -1)
    o["F1_lnw"] = i["L1_ffn_ln_w"].reshape(4, P).T
    o["F1_lnb"] = i["L1_ffn_ln_b"].reshape(4, P).T
    turned = lambda w: np.stack([w[..., 1::2], w[..., 0::2]], -1).reshape(w.shape)
    o["L2_WqT"] = feature_first(i["L2_xattn_Wq"].T)
    o["L2_WkT"] = feature_first(i["L2_xattn_Wk"].T)
    o["L2_WkTs"] = feature_first(turned(i["L2_xattn_Wk"].T))
    o["L2_WvT"] = i["L2_xattn_Wv"].T
    o["L2_WvTs"] = turned(i["L2_xattn_Wv"].T)
    o["L2_WoT"], o["L2_bo"] = i["L2_xattn_Wp"].T, i["L2_xattn_bp"]
    half = D // 2
    theta = (1.0 / np.float32(10000.0) ** (np.float32(2.0) * np.arange(half, dtype=np.float32) / np.float32(D))).astype(np.float32)
    ang = np.arange(S, dtype=np.float32)[:, None] * theta[None, :]
    cos, sin = (np.repeat(f(ang), 2, axis=1).astype(np.float32) for f in (np.cos, np.sin))
    sin[:, 0::2] *= np.float32(-1.0)
    o["rope_cosT"], o["rope_sinT"] = feature_first(cos).T, feature_first(sin).T
    o["rope_cs"] = np.stack([cos, sin]).reshape(2, TPB, P, D).transpose(2, 0, 1, 3)
    eye = np.eye(P, dtype=np.float32)
    o["L3_WqT"], o["L3_WvT"] = feature_first(eye), eye
    o["L3_WoT"], o["L3_bo"] = i["L3_xattn_W_proj"].T, i["L3_xattn_b_proj"]
    e = np.arange(P) % 8
    t = np.arange(P) // 8
    o["same_expert"] = (e[:, None] == e[None, :]).astype(np.float32)
    o["earlier_tile"] = ((e[:, None] == e[None, :]) & (t[:, None] < t[None, :])).astype(np.float32)
    o["before"] = (np.arange(8)[None, :] < np.arange(8)[:, None]).astype(np.float32).reshape(-1)
    o["L1_ln"] = np.stack([i["L1_xattn_ln_gamma"], i["L1_xattn_ln_beta"]], 1)
    return {k: np.ascontiguousarray(v) for k, v in o.items()}


def kernel(**inputs):
    import concourse.bacc as bacc
    from concourse.bass_utils import run_bass_kernel_spmd

    arrays = layout({k: np.asarray(v) for k, v in inputs.items()})
    nc = bacc.Bacc("TRN2", target_bir_lowering=False, num_devices=1)
    aps = {k: nc.dram_tensor("in_" + k, v.shape, F32, kind="ExternalInput").ap() for k, v in arrays.items()}
    out = nc.dram_tensor("out", (P, NT, D), F32, kind="ExternalOutput").ap()
    program(nc, aps, out)
    r = run_bass_kernel_spmd(nc, [{"in_" + k: v for k, v in arrays.items()}], core_ids=[0])
    y = r.results[0]["out"]
    return np.ascontiguousarray(y.transpose(1, 0, 2)).reshape(B, S, D)
```

```python
import numpy as np
import concourse.bass as bass
from concourse import mybir
from contextlib import ExitStack

F32 = mybir.dt.float32
F32R = mybir.dt.float32r
BF16 = mybir.dt.bfloat16
I32 = mybir.dt.int32
ALU = mybir.AluOpType
ACT = mybir.ActivationFunctionType
AX = mybir.AxisListType

P = 128
B, S, D = 8, 256, 128
TPB = S // P
NT = B * TPB
H = 16
DH = D // H
HU = H // 2
RING = 4
PROBS = 6
NEG = -1e30
LN_EPS = 1e-5


class Chip:

    def __init__(self, nc, ctx, arrays):
        self.nc, self.ctx, self.a = nc, ctx, arrays
        self.sublayer_sems, self.spent_sems = [], []
        sb = self.sb
        self.x = sb("x_res", [P, NT, D])
        self.xnT = sb("xnT", [P, NT, P])
        self.ident = sb("ident", [P, P])
        self.identb = sb("identb", [P, P], BF16)
        self.ones = sb("ones", [P, P])
        self.zrow = sb("zrow", [2, S])
        self.mhalf = sb("mhalf", [P, NT])
        self.gates_t = sb("gates_t", [P, 8])
        self.banks = [ctx.enter_context(nc.psum_tensor(f"bank{i}", [P, 512], F32)) for i in range(8)]

    def sb(self, name, shape, dt=F32):
        return self.ctx.enter_context(self.nc.sbuf_tensor(name, shape, dt))

    def sem(self, name):
        return self.ctx.enter_context(self.nc.semaphore(name))

    def sublayer_sem(self, name):
        s = self.nc.alloc_semaphore(name)
        self.sublayer_sems.append(s)
        return s

    def end_sublayer(self):
        for s in self.spent_sems:
            self.nc.release_semaphore(s)
        self.spent_sems, self.sublayer_sems = self.sublayer_sems, []

    def clear_spent(self, g):
        for s in self.spent_sems:
            g.sem_clear(s)


def need(eng, sem, value):
    if value > 0:
        eng.wait_ge(sem, value)


def row(v):
    return v.rearrange("(a n) -> a n", a=1)


def col(v):
    return v.rearrange("(n a) -> n a", a=1)


def start_block(c, weights, masks):
    nc, a = c.nc, c.a
    CH = 4
    NC = NT // CH
    x_in = [c.sem(f"x_loaded{q}") for q in range(NC)]
    const, gate_in, gate_t, made = (c.sem(s) for s in ("consts_ready", "gates_loaded", "gates_ready", "masks_made"))
    stats, rstd_ready, xn_ready, xT_ready, xnT_ready = (
        c.sem(s) for s in ("ln0_stats", "ln0_rstd", "ln0_xn", "ln0_xT", "ln0_xnT"))
    with ExitStack() as own:
        sb = lambda n, s: own.enter_context(nc.sbuf_tensor(n, s, F32))
        st = sb("ln0_st", [P, NT, 6])
        mv = sb("ln0_mv", [P, NT, 2])
        rstd = sb("ln0_rstd_t", [P, NT])
        ve = sb("ln0_ve", [P, NT])
        xn = sb("ln0_xn_t", [P, 2, 4, D])
        with nc.Block() as block:
            @block.sync
            def _(sp):
                for q in range(NC):
                    sp.dma_start(c.x[:, CH * q:CH * (q + 1), :], a["x"][:, CH * q:CH * (q + 1), :]).then_inc(x_in[q], 16)
                sp.dma_start(c.gates_t[:, 0:4], a["g_xattn"].partition_broadcast(P)).then_inc(gate_in, 16)
                sp.dma_start(c.gates_t[:, 4:8], a["g_ffn"].partition_broadcast(P)).then_inc(gate_in, 16)
                for sem, dst, src in weights:
                    sp.dma_start(dst, src).then_inc(sem, 16)

            @block.gpsimd
            def _(g):
                g.memset(c.ones[:], 1.0).then_inc(const, 1)
                g.memset(c.mhalf[:], -0.5).then_inc(const, 1)
                g.memset(c.zrow[:], 0.0).then_inc(const, 1)
                g.wait_ge(const, 3)
                g.affine_select(out=c.ident[:], in_=c.ones[:], compare_op=ALU.is_equal, fill=0.0, base=0,
                                pattern=[[-1, P]], channel_multiplier=1).then_inc(const, 1)
                g.wait_ge(const, 4)
                g.tensor_copy(c.identb[:], c.ident[:]).then_inc(const, 1)
                for q in range(NC):
                    part = slice(CH * q, CH * (q + 1))
                    g.wait_ge(stats, 2 * CH * (q + 1))
                    g.tensor_scalar(ve[:, part], mv[:, part, 1], LN_EPS, None, ALU.add).then_inc(rstd_ready, 1)
                    g.wait_ge(rstd_ready, 2 * q + 1)
                    g.tensor_tensor(rstd[:, part], ve[:, part], c.mhalf[:, part], ALU.pow).then_inc(rstd_ready, 1)
                    if q == 1:
                        draw_masks(g, masks, made)

            @block.scalar
            def _(act):
                act.wait_ge(gate_in, 32)
                act.activation(c.gates_t[:], c.gates_t[:], ACT.Tanh).then_inc(gate_t, 1)
                for q in range(4):
                    act.wait_ge(xT_ready, q + 1)
                    act.copy(c.xnT[:, 4 * q:4 * q + 4, :], c.banks[q][:, :]).then_inc(xnT_ready, 1)

            @block.vector
            def _(v):
                def statistics(q):
                    v.wait_ge(x_in[q], 16)
                    for t in range(CH * q, CH * (q + 1)):
                        v.bn_stats(st[:, t, :], c.x[:, t, :]).then_inc(stats, 1)
                    v.wait_ge(stats, CH * (2 * q + 1))
                    for t in range(CH * q, CH * (q + 1)):
                        v.bn_aggr(mv[:, t, :], st[:, t, :]).then_inc(stats, 1)

                def normalise(q):
                    v.wait_ge(stats, 2 * CH * (q + 1))
                    v.wait_ge(rstd_ready, 2 * (q + 1))
                    if q >= 2:
                        v.wait_ge(xT_ready, q - 1)
                    for t in range(CH * q, CH * (q + 1)):
                        v.tensor_scalar(xn[:, q % 2, t % CH, :], c.x[:, t, :], mv[:, t, 0:1], rstd[:, t:t + 1],
                                        ALU.subtract, ALU.mult).then_inc(xn_ready, 1)

                for q in range(NC + 1):
                    if q < NC:
                        statistics(q)
                    if q >= 1:
                        normalise(q - 1)

            @block.tensor
            def _(pe):
                pe.wait_ge(const, 4)
                for q in range(4):
                    pe.wait_ge(xn_ready, 4 * q + 4)
                    for t in range(4):
                        m = pe.transpose(c.banks[q][:, t * P:(t + 1) * P], xn[:, q % 2, t, :], c.ident[:])
                    m.then_inc(xT_ready, 1)


def attention(c, L, w, gate, window=0, rope=False, next_loads=()):
    nc = c.nc
    W = P + window if window else S
    lo = [0, S - W]
    scale = float(1.0 / np.sqrt(DH))
    NPS, TPS, PA, PB, OPB, MISC = c.banks[0:2], c.banks[2:4], c.banks[4], c.banks[5], c.banks[6], c.banks[7]
    U = 2 * B
    pre = f"L{L}_"
    sem = lambda n: c.sublayer_sem(pre + n)
    (ct_in0, ct_in1, proj_q, proj_v, split_q, va_ready, stacked0, stacked1, n_ready, max_ready, shT_ready, sh_ready,
     shifted, t_ready, p_ready, pv_ready, o_ready, trT_ready, rc_ready, cn_ready, cnT_ready, cnT_copied,
     po_ready, resid, st_ready, mv_ready, rstd_ready, xn_ready, xT_ready, xnT_ready, zeroed, kf_ready, tmp_ready, tmp2) = (
        sem(n) for n in (
            "ctx_loaded0", "ctx_loaded1", "qk_projected", "v_projected", "qk_split", "v_ready", "stacked0",
            "stacked1", "scores_ready", "max_ready", "maxT_ready", "shift_ready", "shift_stacked",
            "scoresT_ready", "probs_ready", "pv_ready", "ctx_copied", "ctx_turned", "recip_ready", "ctx_normed",
            "ctxT_ready", "ctxT_copied", "out_ready", "resid_ready", "ln_stats", "ln_mv", "ln_rstd", "ln_xn",
            "ln_xT", "ln_xnT", "zeroed", "k_roped", "k_turned", "v_turned"))
    ct_in, stacked = [ct_in0, ct_in1], [stacked0, stacked1]
    with ExitStack() as own:
        sb = lambda n, s, d=F32: own.enter_context(nc.sbuf_tensor(pre + n, s, d))
        ct = sb("ct", [P, 2, S])
        parts = sb("parts", [P, 4, S], F32R)
        kf = sb("kf", [P, 3, S]) if rope else None
        vt = sb("vt", [P, 2, TPB, D]) if rope else None
        QS = sb("q_stack", [P, RING, HU, S], F32R)
        KS = sb("k_stack", [P, RING, HU, S], F32R)
        q_cleared, k_cleared = sem("q_stack_cleared"), sem("k_stack_cleared")
        va = sb("va", [P, 3, TPB, H, 32])
        mx = sb("mx", [P, 2, HU, TPB])
        sh = sb("sh", [HU, 2, 2, S], F32R)
        pt = sb("pt", [P, PROBS, TPB, S])
        os_ = sb("os", [P, 2, S])
        rc = sb("rc", [P, 2, TPB, 4])
        cn = sb("cn", [P, TPB, D])
        cnT = sb("cnT", [P, S])
        st = sb("st", [P, TPB, 6])
        mv = sb("mv", [P, TPB, 2])
        ve = sb("ve", [P, TPB])
        rstd = sb("rstd", [P, TPB])
        xn = sb("xn", [P, TPB, D])

        with nc.Block() as block:
            @block.sync
            def _(sp):
                def load_ctx(b):
                    if b >= 2:
                        sp.wait_ge(proj_v, b - 1)
                    sp.dma_start(ct[:, b % 2, :], c.a["ctxT"][:, b * S:(b + 1) * S]).then_inc(ct_in[b % 2], 16)

                def stack(u):
                    b, hf, r = u // 2, u % 2, u % RING
                    sp.wait_ge(split_q, 4 * (b + 1))
                    need(sp, t_ready, (u - RING + 1) * HU)
                    if u < RING:
                        sp.wait_ge(q_cleared, u + 1)
                        sp.wait_ge(k_cleared, u + 1)
                    for term, (qp, kp) in enumerate(((0, 2), (1, 2), (0, 3))):
                        for dst, part in ((QS, qp), (KS, kp)):
                            src = parts[hf * 64:hf * 64 + 64, part, :].bitcast(F32)
                            sp.dma_start(dst[DH * term:DH * (term + 1), r, :, :].bitcast(F32), src).then_inc(stacked[u % 2], 16)
                    sp.dma_start(QS[24:26, r, :, :].bitcast(F32), c.zrow[:].unsqueeze(1).broadcast_to([2, HU, S])).then_inc(stacked[u % 2], 16)

                def shift(u):
                    sp.wait_ge(sh_ready, 2 * (u + 1))
                    sp.wait_ge(n_ready, (u + 1) * HU)
                    for k in range(2):
                        sp.dma_start(QS[24 + k:25 + k, u % RING, :, :].bitcast(F32), sh[:, u % 2, k, :].bitcast(F32)).then_inc(shifted, 16)

                load_ctx(0)
                load_ctx(1)
                stack(0)
                stack(1)
                for t in range(U + 2):
                    if t % 2 == 0 and t // 2 + 2 < B:
                        load_ctx(t // 2 + 2)
                    if t == 0:
                        for s, dst, src in next_loads:
                            sp.dma_start(dst, src).then_inc(s, 16)
                    if t >= 1 and t + 1 < U:
                        stack(t + 1)
                    if t >= 1 and t - 1 < U:
                        shift(t - 1)

            @block.tensor
            def _(pe):
                def project_qk(b):
                    xs = c.xnT[:, TPB * b:TPB * (b + 1), :].rearrange("p t n -> p (t n)")
                    need(pe, split_q, 4 * b)
                    need(pe, sh_ready, 4 * (b - 1))
                    if b >= 1:
                        pe.wait_ge(va_ready, b)
                    pe.wait_ge(ct_in[b % 2], 16 * (b // 2 + 1))
                    pe.matmul(PA[:, 0:S], w["WqT"], xs, start=True, stop=True)
                    m = pe.matmul(PA[:, S:2 * S], w["WkT"], ct[:, b % 2, :], start=True, stop=True)
                    if rope:
                        m = pe.matmul(PB[:, 0:S], w["WkTs"], ct[:, b % 2, :], start=True, stop=True)
                    m.then_inc(proj_q, 1)

                def project_v(b):
                    if rope:
                        pe.wait_ge(tmp_ready, 2 * b + 2)
                    for t in range(TPB):
                        tok = ct[:, b % 2, t * P:(t + 1) * P]
                        m = pe.matmul(PB[:, t * D:(t + 1) * D], tok, w["WvT"], start=True, stop=True)
                        if rope:
                            m = pe.matmul(PB[:, (2 + t) * D:(3 + t) * D], tok, w["WvTs"], start=True, stop=True)
                    m.then_inc(proj_v, 1)

                def put_mask(bank):
                    pe.matmul(bank[:, 0:TPB * W], c.identb[:], w["mask"][:].rearrange("p t n -> p (t n)"),
                              start=True, stop=False, skip_group_check=True)

                def scores(u, h):
                    n, r = u * HU + h, u % RING
                    need(pe, max_ready, n - 1)
                    if h == 0:
                        pe.wait_ge(stacked[u % 2], 16 * 7 * (u // 2 + 1))
                    if window:
                        put_mask(NPS[n % 2])
                    for t in range(TPB):
                        m = pe.matmul(NPS[n % 2][:, t * W:(t + 1) * W], QS[:, r, h, t * P:(t + 1) * P],
                                      KS[:, r, h, lo[t]:lo[t] + W], start=not window, stop=True,
                                      skip_group_check=bool(window))
                    m.then_inc(n_ready, 1)

                def scores_t(u, h):
                    n, r = u * HU + h, u % RING
                    need(pe, p_ready, n - 1)
                    if h == 0:
                        pe.wait_ge(shifted, 32 * (u + 1))
                    if window:
                        put_mask(TPS[n % 2])
                    for t in range(TPB):
                        m = pe.matmul(TPS[n % 2][:, t * W:(t + 1) * W], KS[:, r, h, t * P:(t + 1) * P],
                                      QS[:, r, h, lo[t]:lo[t] + W], start=not window, stop=True,
                                      skip_group_check=bool(window))
                    m.then_inc(t_ready, 1)

                def pv(u, g):
                    G = 2 * u + g
                    pe.wait_ge(p_ready, 4 * (G + 1))
                    need(pe, o_ready, G)
                    pe.wait_ge(va_ready, u // 2 + 1)
                    for t in range(TPB):
                        for j in range(4):
                            n = 4 * G + j
                            h = n % H
                            m = pe.matmul(OPB[32 * j:32 * j + 32, lo[t]:lo[t] + W], va[:, u // 2 % 3, t, h, :],
                                          pt[:, n % PROBS, t, 0:W], start=(t == 0), stop=(t == 1),
                                          skip_group_check=bool(window))
                    m.then_inc(pv_ready, 1)

                def turn_max(u):
                    pe.wait_ge(max_ready, (u + 1) * HU)
                    pe.wait_ge(va_ready, min(B, (u + 1) // 2 + 1 + (u + 1) % 2))
                    for t in range(TPB):
                        m = pe.transpose(PB[0:HU, t * P:(t + 1) * P], mx[:, u % 2, :, t], c.ident[:])
                    m.then_inc(shT_ready, 1)

                def turn_ctx(u, g):
                    G = 2 * u + g
                    pe.wait_ge(o_ready, G + 1)
                    need(pe, cn_ready, G)
                    for t in range(TPB):
                        m = pe.transpose(MISC[:, t * P:(t + 1) * P], os_[:, G % 2, t * P:(t + 1) * P], c.ident[:])
                    m.then_inc(trT_ready, 1)

                def turn_normed(b):
                    pe.wait_ge(cn_ready, 4 * (b + 1))
                    for t in range(TPB):
                        m = pe.transpose(MISC[:, t * P:(t + 1) * P], cn[:, t, :], c.ident[:])
                    m.then_inc(cnT_ready, 1)

                def out(b):
                    pe.wait_ge(cnT_copied, b + 1)
                    for t in range(TPB):
                        pe.matmul(MISC[:, t * D:(t + 1) * D], cnT[:, t * P:(t + 1) * P], w["WoT"],
                                  start=True, stop=False)
                        m = pe.matmul(MISC[:, t * D:(t + 1) * D], c.ones[0:1, :], w["bo"], start=False, stop=True)
                    m.then_inc(po_ready, 1)

                def turn_ln(b):
                    pe.wait_ge(xn_ready, 2 * (b + 1))
                    for t in range(TPB):
                        m = pe.transpose(MISC[:, t * P:(t + 1) * P], xn[:, t, :], c.ident[:])
                    m.then_inc(xT_ready, 1)

                for s, all_loads in w["loaded"]:
                    pe.wait_ge(s, all_loads)
                project_qk(0)
                project_v(0)
                for t in range(U + 6):
                    N, T, T3 = t < U, 0 <= t - 2 < U, 0 <= t - 3 < U
                    b4, b5 = (t - 4) // 2, (t - 5) // 2
                    for h in range(HU):
                        if N:
                            scores(t, h)
                        if T:
                            scores_t(t - 2, h)
                        if h == 1:
                            if 0 <= t - 1 < U:
                                turn_max(t - 1)
                            if T3:
                                pv(t - 3, 1)
                        if h == 2 and t % 2 == 1 and 0 <= b5 < B:
                            pe.wait_ge(cn_ready, min(2 * t - 5, 2 * U))
                            turn_ln(b5)
                        if h == 3 and T3:
                            if t % 2 == 1 and b5 >= 0:
                                pe.wait_ge(xnT_ready, b5 + 1)
                            turn_ctx(t - 3, 1)
                        if h == 4 and t % 2 == 0 and 0 <= b4 < B:
                            turn_normed(b4)
                        if h == 5 and T:
                            pv(t - 2, 0)
                        if h == 5 and t % 2 == 0 and t // 2 + 1 < B:
                            project_qk(t // 2 + 1)
                        if h == 6 and t % 2 == 0 and 0 <= b4 < B:
                            out(b4)
                        if h == 7 and t % 2 == 0 and t // 2 + 1 < B:
                            project_v(t // 2 + 1)
                        if h == 7 and T:
                            if t % 2 == 0 and b4 >= 0:
                                pe.wait_ge(resid, b4 + 1)
                            if t % 2 == 1:
                                need(pe, cn_ready, 2 * (t - 3) + 2)
                            turn_ctx(t - 2, 0)

            @block.scalar
            def _(act):
                def split_q_high(b):
                    act.wait_ge(proj_q, b + 1)
                    if b >= 1:
                        act.wait_ge(stacked[0], 16 * 7 * b)
                        act.wait_ge(stacked[1], 16 * 7 * b)
                    act.activation(parts[:, 0, :], PA[:, 0:S], ACT.Identity, bias=w["bq"]).then_inc(split_q, 1)

                def split_k_high(b):
                    if rope:
                        act.wait_ge(kf_ready, b + 1)
                        act.copy(parts[:, 2, :], kf[:, 2, :]).then_inc(split_q, 1)
                    else:
                        act.activation(parts[:, 2, :], PA[:, S:2 * S], ACT.Identity, bias=w["bk"]).then_inc(split_q, 1)

                def exps(u, h):
                    n = u * HU + h
                    act.wait_ge(t_ready, n + 1)
                    need(act, pv_ready, (n - PROBS) // 4 + 1)
                    src = TPS[n % 2][:, 0:TPB * W]
                    if window:
                        src = src.rearrange("p (t n) -> p t n", t=TPB)
                    else:
                        src = src.rearrange("p (t n) -> p t n", t=TPB)
                    act.activation(pt[:, n % PROBS, :, 0:W], src, ACT.Exp, scale=scale).then_inc(p_ready, 1)

                def copy_ctx(u, g):
                    G = 2 * u + g
                    act.wait_ge(pv_ready, G + 1)
                    need(act, trT_ready, G - 1)
                    act.copy(os_[:, G % 2, :], OPB[:, 0:S]).then_inc(o_ready, 1)

                def copy_normed(b):
                    act.wait_ge(cnT_ready, b + 1)
                    need(act, po_ready, b)
                    act.copy(cnT[:], MISC[:, 0:S]).then_inc(cnT_copied, 1)

                def copy_ln(b):
                    act.wait_ge(xT_ready, b + 1)
                    act.copy(c.xnT[:, TPB * b:TPB * (b + 1), :].rearrange("p t n -> p (t n)"),
                             MISC[:, 0:S]).then_inc(xnT_ready, 1)

                for s, all_loads in w["loaded"]:
                    act.wait_ge(s, all_loads)
                split_q_high(0)
                split_k_high(0)
                for t in range(U + 6):
                    T, T3 = 0 <= t - 2 < U, 0 <= t - 3 < U
                    b4, b5 = (t - 4) // 2, (t - 5) // 2
                    for h in range(HU):
                        if T:
                            exps(t - 2, h)
                        if h == 1 and T3:
                            copy_ctx(t - 3, 1)
                        if h == 2 and t % 2 == 1 and 0 <= b5 < B:
                            copy_ln(b5)
                        if h == 4 and t % 2 == 0 and 0 <= b4 < B:
                            copy_normed(b4)
                        if h == 5 and t % 2 == 0 and t // 2 + 1 < B:
                            split_q_high(t // 2 + 1)
                        if h == 6 and t % 2 == 0 and t // 2 + 1 < B:
                            split_k_high(t // 2 + 1)
                        if h == 5 and T:
                            copy_ctx(t - 2, 0)

            @block.gpsimd
            def _(g):
                c.clear_spent(g)
                g.memset(QS[:, 0].bitcast(F32), 0.0).then_inc(q_cleared, 1)
                g.memset(va[:], 1.0).then_inc(zeroed, 1)
                for r in range(1, RING):
                    g.memset(QS[:, r].bitcast(F32), 0.0).then_inc(q_cleared, 1)
                for b in range(B):
                    g.wait_ge(mv_ready, 2 * (b + 1))
                    g.tensor_scalar(ve[:], mv[:, :, 1], LN_EPS, None, ALU.add).then_inc(rstd_ready, 1)
                    g.wait_ge(rstd_ready, 2 * b + 1)
                    g.tensor_tensor(rstd[:], ve[:], c.mhalf[:, 0:TPB], ALU.pow).then_inc(rstd_ready, 1)

            @block.vector
            def _(v):
                v3 = lambda ap: ap.rearrange("p (t h d) -> p t h d", t=TPB, h=H)

                def split_low(b):
                    v.wait_ge(proj_q, b + 1)
                    if rope:
                        v.wait_ge(split_q, 4 * b + 1)
                        v.tensor_tensor(kf[:, 0, :], PA[:, S:2 * S], w["cosT"], ALU.mult).then_inc(tmp_ready, 1)
                        v.tensor_tensor(kf[:, 1, :], PB[:, 0:S], w["sinT"], ALU.mult).then_inc(tmp_ready, 1)
                        v.wait_ge(tmp_ready, 2 * b + 2)
                        if b >= 1:
                            v.wait_ge(split_q, 4 * b)
                        v.tensor_tensor(kf[:, 2, :], kf[:, 0, :], kf[:, 1, :], ALU.add).then_inc(kf_ready, 1)
                    v.wait_ge(split_q, 4 * b + 2)
                    v.scalar_tensor_tensor(parts[:, 1, :], PA[:, 0:S], w["bq"], parts[:, 0, :].bitcast(F32),
                                           ALU.add, ALU.subtract).then_inc(split_q, 1)
                    if rope:
                        v.wait_ge(kf_ready, b + 1)
                        v.tensor_tensor(parts[:, 3, :], kf[:, 2, :], parts[:, 2, :].bitcast(F32),
                                        ALU.subtract).then_inc(split_q, 1)
                    else:
                        v.scalar_tensor_tensor(parts[:, 3, :], PA[:, S:2 * S], w["bk"],
                                               parts[:, 2, :].bitcast(F32), ALU.add, ALU.subtract).then_inc(split_q, 1)

                def place_v(b):
                    v.wait_ge(proj_v, b + 1)
                    if b == 0:
                        v.wait_ge(zeroed, 1)
                    need(v, pv_ready, 4 * (b - 2))
                    dst = va[:, b % 3, :, :, 0:DH]
                    if rope:
                        src = PB[:, :].rearrange("p (s t d) -> p s t d", s=2, t=TPB)
                        for s in range(2):
                            v.tensor_tensor(vt[:, s], src[:, s], w["cs"][:, s], ALU.mult).then_inc(tmp2, 1)
                        v.wait_ge(tmp2, 2 * b + 2)
                        x3 = lambda s: vt[:, s].rearrange("p t (h d) -> p t h d", h=H)
                        for t in range(TPB):
                            i = v.tensor_tensor(dst[:, t], x3(0)[:, t], x3(1)[:, t], ALU.add)
                        i.then_inc(va_ready, 1)
                    else:
                        for t in range(TPB):
                            if w["bv"] is None:
                                i = v.tensor_copy(dst[:, t], v3(PB[:, 0:S])[:, t])
                            else:
                                i = v.tensor_tensor(dst[:, t], v3(PB[:, 0:S])[:, t],
                                                    w["bv"].rearrange("p (h d) -> p h d", h=H), ALU.add)
                        i.then_inc(va_ready, 1)

                def maxima(u, h):
                    n = u * HU + h
                    v.wait_ge(n_ready, n + 1)
                    if h == 0:
                        need(v, shT_ready, u - 1)
                    v.tensor_reduce(mx[:, u % 2, h, :], NPS[n % 2][:, 0:TPB * W].rearrange("p (t n) -> p t n", t=TPB),
                                    AX.X, ALU.max).then_inc(max_ready, 1)

                def shift(u):
                    v.wait_ge(shT_ready, u + 1)
                    need(v, shifted, 32 * (u - 1))
                    v.tensor_scalar(sh[:, u % 2, 0, :], PB[0:HU, 0:S], -1.0, None, ALU.mult).then_inc(sh_ready, 1)
                    v.wait_ge(sh_ready, 2 * u + 1)
                    v.scalar_tensor_tensor(sh[:, u % 2, 1, :], PB[0:HU, 0:S], -1.0,
                                           sh[:, u % 2, 0, :].bitcast(F32), ALU.mult, ALU.subtract).then_inc(sh_ready, 1)

                def norm_ctx(u, g):
                    G = 2 * u + g
                    v.wait_ge(trT_ready, G + 1)
                    o4 = MISC[:, 0:S].rearrange("p (t j k) -> p t j k", t=TPB, j=4)
                    need(v, cn_ready, G - 1)
                    v.reciprocal(rc[:, G % 2], o4[:, :, :, DH]).then_inc(rc_ready, 1)
                    v.wait_ge(rc_ready, G + 1)
                    if G % 4 == 0:
                        need(v, cnT_ready, G // 4)
                    h0 = 4 * G % H
                    for t in range(TPB):
                        i = v.tensor_tensor(cn[:, t, h0 * DH:(h0 + 4) * DH].rearrange("p (j d) -> p j d", j=4),
                                            o4[:, t, :, 0:DH],
                                            rc[:, G % 2, t, :].rearrange("p (j a) -> p j a", a=1).broadcast_to([P, 4, DH]),
                                            ALU.mult)
                    i.then_inc(cn_ready, 1)

                def finish(b):
                    v.wait_ge(po_ready, b + 1)
                    xs = c.x[:, TPB * b:TPB * (b + 1), :].rearrange("p t n -> p (t n)")
                    v.scalar_tensor_tensor(xs, MISC[:, 0:S], gate, xs, ALU.mult, ALU.add).then_inc(resid, 1)
                    v.wait_ge(resid, b + 1)
                    for t in range(TPB):
                        v.bn_stats(st[:, t, :], c.x[:, TPB * b + t, :]).then_inc(st_ready, 1)
                    v.wait_ge(st_ready, 2 * (b + 1))
                    for t in range(TPB):
                        v.bn_aggr(mv[:, t, :], st[:, t, :]).then_inc(mv_ready, 1)

                def normalise(b):
                    v.wait_ge(mv_ready, 2 * (b + 1))
                    v.wait_ge(rstd_ready, 2 * (b + 1))
                    need(v, xT_ready, b)
                    for t in range(TPB):
                        v.tensor_scalar(xn[:, t, :], c.x[:, TPB * b + t, :], mv[:, t, 0:1], rstd[:, t:t + 1],
                                        ALU.subtract, ALU.mult).then_inc(xn_ready, 1)

                v.memset(KS[:, 0].bitcast(F32), 1.0).then_inc(k_cleared, 1)
                for s, all_loads in w["loaded"]:
                    v.wait_ge(s, all_loads)
                split_low(0)
                place_v(0)
                for r in range(1, RING):
                    v.memset(KS[:, r].bitcast(F32), 1.0).then_inc(k_cleared, 1)
                for t in range(U + 6):
                    N, T, T3 = t < U, 0 <= t - 2 < U, 0 <= t - 3 < U
                    b4, b5 = (t - 4) // 2, (t - 5) // 2
                    for h in range(HU):
                        if h == 0 and t % 2 == 1 and 0 <= b5 < B:
                            normalise(b5)
                        if N:
                            maxima(t, h)
                        if h == 1 and 0 <= t - 1 < U:
                            shift(t - 1)
                        if h == 3 and T3:
                            norm_ctx(t - 3, 1)
                        if h == 6 and t % 2 == 0 and t // 2 + 1 < B:
                            split_low(t // 2 + 1)
                        if h == 7 and t % 2 == 0 and t // 2 + 1 < B:
                            place_v(t // 2 + 1)
                        if h == 6 and t % 2 == 0 and 0 <= b4 < B:
                            finish(b4)
                        if h == 7 and T:
                            norm_ctx(t - 2, 0)


def layer_norm_tail(c, own, pre, double=None):
    nc = c.nc
    sb = lambda n, s, d=F32: own.enter_context(nc.sbuf_tensor(pre + n, s, d))
    return dict(st=sb("st", [P, 4, 6]), mv=sb("mv", [P, 4, 2]), ve=sb("ve", [P, 4]), rstd=sb("rstd", [P, 4]),
                xn=sb("xn", [P, 4, D]))


def ffn(c, L, w, tgate, E, per_group, act_f, rule, double=None, store=None):
    nc = c.nc
    F = w["F"]
    FT = (F + P - 1) // P
    FP = FT * P
    AHEAD = 10 if rule == "experts" else 1
    HR = AHEAD + 1
    CH = 4
    NC = NT // CH
    groups = E // per_group
    K = [(q, g) for q in range(NC) for g in range(groups)]
    UB, YB, GB, LB = c.banks[0:4], c.banks[4:6], c.banks[6], c.banks[7]
    pre = f"F{L}_"
    sem = lambda n: c.sublayer_sem(pre + n)
    (stepg2, xn1_ready) = (sem("gate_zeroed"), sem("ln_xn1"))
    (wh_ready, wl_ready, xh_ready, xl_ready) = (sem(n) for n in ("w1_high", "w1_low", "x_high", "x_low"))
    (lg_ready, step, stepg, stepa, stepp, gates_ready, up_ready, h_ready, y_ready, added, gT_ready, gT_copied, bias_ready,
     bias_added, st_ready, mv_ready, rstd_ready, xn_ready, xT_ready, xnT_ready) = (sem(n) for n in (
         "logits_ready", "gate_step", "gate_pool", "gate_exp", "gate_pe", "gates_ready", "up_ready", "hidden_ready",
         "down_ready", "added", "gatesT_ready", "gatesT_copied", "bias_ready", "bias_added", "ln_stats", "ln_mv",
         "ln_rstd", "ln_xn", "ln_xT", "ln_xnT"))
    with ExitStack() as own:
        sb = lambda n, s, d=F32: own.enter_context(nc.sbuf_tensor(pre + n, s, d))
        lg = sb("lg", [P, NT, E])
        pr = sb("pr", [P, NT, E])
        m1 = sb("m1", [P, NT])
        gates = sb("gates", [P, NT, E])
        gT = sb("gT", [E, NT, P])
        ht = sb("ht", [P, HR, FT, CH * P])
        wh = sb("wh", [P, groups * FP], F32R)
        wl = sb("wl", [P, groups * FP], F32R)
        xh = sb("xh", [P, NC, CH * P], F32R)
        xl = sb("xl", [P, NC, CH * P], F32R)
        ln = layer_norm_tail(c, own, pre)
        st, mv, ve, rstd, xn = (ln[k] for k in ("st", "mv", "ve", "rstd", "xn"))
        if rule == "experts":
            pT = sb("pT", [P, P])
            msk = sb("msk", [P, P])
            eq = sb("eq", [P, P])
            cum = sb("cum", [P, P])
            zero = sb("zero", [P, P])
            cand = sb("cand", [P, 1], I32)
            low = sb("low", [P, 1], I32)
            take = sb("take", [P, 1], I32)
            cnt = sb("cnt", [P, 1])
            left = sb("left", [P, 1])
            prf = sb("prf", [P, 1])
        else:
            cmp1 = sb("cmp1", [P, NT, E, E])
            cmp2 = sb("cmp2", [P, NT, E, E])
            rank = sb("rank", [P, NT, E])

        b8 = lambda ap: ap.rearrange("p (t a) -> p t a", a=1).broadcast_to([P, NT, E])
        other = lambda ap: ap.rearrange("p t (a e) -> p t a e", a=1).broadcast_to([P, NT, E, E])
        mine = lambda ap: ap.rearrange("p t (e a) -> p t e a", a=1).broadcast_to([P, NT, E, E])
        BITS = 30

        with nc.Block() as block:
            @block.tensor
            def _(pe):
                def up(k, f):
                    q, g = K[k]
                    n = k * FT + f
                    if f == 0:
                        pe.wait_ge(wh_ready, g + 1)
                        pe.wait_ge(wl_ready, g + 1)
                        pe.wait_ge(xh_ready, q + 1)
                        pe.wait_ge(xl_ready, q + 1)
                    need(pe, h_ready, n - 3)
                    cols = slice(g * FP + f * P, g * FP + (f + 1) * P)
                    pe.matmul(UB[n % 4][:, :], wh[:, cols], xh[:, q, :], start=True, stop=False)
                    pe.matmul(UB[n % 4][:, :], wh[:, cols], xl[:, q, :], start=False, stop=False)
                    pe.matmul(UB[n % 4][:, :], wl[:, cols], xh[:, q, :], start=False, stop=True).then_inc(up_ready, 1)

                for s, all_loads in w["loaded"]:
                    pe.wait_ge(s, all_loads)
                for t in range(NT):
                    m = pe.matmul(GB[:, t * E:(t + 1) * E], c.xnT[:, t, :], w["Wr"], start=True, stop=True)
                m.then_inc(lg_ready, 1)
                if rule == "experts":
                    pe.wait_ge(step, w["steps_to_probs"])
                    pe.transpose(GB[:, 0:P], pr[:].rearrange("p t e -> p (t e)"), c.ident[:]).then_inc(stepp, 1)
                    for k in range(BITS + 1):
                        pe.wait_ge(stepg, 2 * k + 1)
                        pe.matmul(LB[:, 0:1], w["same_expert"], cnt[:], start=True, stop=True).then_inc(stepp, 1)
                        if k < AHEAD * FT:
                            up(k // FT, k % FT)
                    pe.wait_ge(stepg, 2 * BITS + 3)
                    pe.matmul(LB[:, 0:1], w["earlier_tile"], cum[:, P - 1:P], start=True, stop=True).then_inc(stepp, 1)
                    pe.wait_ge(stepg, 2 * BITS + 4)
                    pe.transpose(GB[:, 0:P], msk[:], c.ident[:]).then_inc(stepp, 1)

                def down(k, e):
                    q, g = K[k]
                    n = k * per_group + e
                    x = g * per_group + e
                    if e == 0:
                        pe.wait_ge(h_ready, (k + 1) * FT)
                    need(pe, added, 4 * (n - 1))
                    for t in range(CH):
                        for f in range(FT):
                            m = pe.matmul(YB[n % 2][:, t * D:(t + 1) * D], ht[:, k % HR, f, t * P:(t + 1) * P],
                                          w["W2"][:, (x * FT + f) * D:(x * FT + f + 1) * D],
                                          start=(f == 0), stop=(f == FT - 1))
                    m.then_inc(y_ready, 1)

                def biases(q):
                    if q == 0:
                        pe.wait_ge(gates_ready, 1)
                    for t in range(CH):
                        m = pe.transpose(GB[0:E, t * P:(t + 1) * P], gates[:, CH * q + t, :], c.ident[:])
                    m.then_inc(gT_ready, 1)
                    pe.wait_ge(gT_copied, q + 1)
                    need(pe, bias_added, q)
                    for t in range(CH):
                        m = pe.matmul(LB[:, t * D:(t + 1) * D], gT[:, CH * q + t, :], w["b2"], start=True, stop=True)
                    m.then_inc(bias_ready, 1)

                def turn_ln(q):
                    pe.wait_ge(xn_ready, CH * (q + 1))
                    if w["b2"] is not None:
                        pe.wait_ge(bias_added, NC)
                    need(pe, xnT_ready, q)
                    for t in range(CH):
                        m = pe.transpose(LB[:, t * P:(t + 1) * P], xn[:, t, :], c.ident[:])
                    m.then_inc(xT_ready, 1)

                if rule != "experts":
                    for f in range(FT):
                        up(0, f)
                for k in range(len(K)):
                    q, g = K[k]
                    if k + AHEAD < len(K):
                        for f in range(FT):
                            up(k + AHEAD, f)
                    for e in range(per_group):
                        down(k, e)
                        if (k + 1) * per_group == 2 and e == per_group - 1 and w["b2"] is not None:
                            for n in range(NC):
                                biases(n)
                    if g == groups - 2 and q > 0 and not store:
                        turn_ln(q - 1)
                if not store:
                    turn_ln(NC - 1)

            if store:
                @block.sync
                def _(sp):
                    out, stored = store
                    for q in range(NC):
                        part = slice(CH * q, CH * (q + 1))
                        sp.wait_ge(added, CH * E * (q + 1))
                        sp.dma_start(out[:, part, :], c.x[:, part, :]).then_inc(stored, 16)
                    sp.wait_ge(stored, 16 * NC)

            @block.scalar
            def _(act):
                for s, all_loads in w["loaded"]:
                    act.wait_ge(s, all_loads)
                for g in range(groups):
                    act.copy(wh[:, g * FP:(g + 1) * FP], w["W1"][:, g * FP:(g + 1) * FP]).then_inc(wh_ready, 1)
                    if g < NC:
                        act.copy(xh[:, g, :],
                                 c.xnT[:, CH * g:CH * (g + 1), :].rearrange("p t n -> p (t n)")).then_inc(xh_ready, 1)
                act.wait_ge(step, 3)
                act.activation(pr[:], pr[:], ACT.Exp).then_inc(stepa, 1)

                def hidden(k):
                    q, g = K[k]
                    need(act, y_ready, (k - HR + 1) * per_group)
                    for f in range(FT):
                        n = k * FT + f
                        act.wait_ge(up_ready, n + 1)
                        b = w["b1"][:, g * FT + f:g * FT + f + 1] if w["b1"] is not None else 0.0
                        act.activation(ht[:, k % HR, f, :], UB[n % 4][:, :], act_f, bias=b).then_inc(h_ready, 1)

                for k in range(AHEAD):
                    hidden(k)
                for k in range(len(K)):
                    q, g = K[k]
                    if k + AHEAD < len(K):
                        hidden(k + AHEAD)
                    if g == groups - 1 and q > 0 and not store:
                        copy_ln(c, act, q - 1, xT_ready, xnT_ready, LB, double)
                if not store:
                    copy_ln(c, act, NC - 1, xT_ready, xnT_ready, LB, double)

            @block.gpsimd
            def _(g):
                c.clear_spent(g)
                if rule == "experts":
                    g.memset(zero[:], 0.0).then_inc(stepg2, 1)
                    g.memset(low[:], 0).then_inc(stepg2, 1)
                for q in range(NC):
                    g.wait_ge(xh_ready, q + 1)
                    g.tensor_tensor(xl[:, q, :], c.xnT[:, CH * q:CH * (q + 1), :].rearrange("p t n -> p (t n)"),
                                    xh[:, q, :].bitcast(F32), ALU.subtract).then_inc(xl_ready, 1)
                rounds = 0 if store else 2 if double else 1
                for n in range(NC * rounds):
                    g.wait_ge(mv_ready, 4 * (n + 1))
                    g.tensor_scalar(ve[:], mv[:, :, 1], LN_EPS, None, ALU.add).then_inc(rstd_ready, 1)
                    g.wait_ge(rstd_ready, 2 * n + 1)
                    g.tensor_tensor(rstd[:], ve[:], c.mhalf[:, 0:4], ALU.pow).then_inc(rstd_ready, 1)

            @block.vector
            def _(v):
                count = [0]

                def chain(i):
                    count[0] += 1
                    i.then_inc(step, 1)
                    v.wait_ge(step, count[0])

                for s, all_loads in w["loaded"]:
                    v.wait_ge(s, all_loads)
                for g in range(groups):
                    v.wait_ge(wh_ready, g + 1)
                    v.tensor_tensor(wl[:, g * FP:(g + 1) * FP], w["W1"][:, g * FP:(g + 1) * FP],
                                    wh[:, g * FP:(g + 1) * FP].bitcast(F32), ALU.subtract).then_inc(wl_ready, 1)
                v.wait_ge(lg_ready, 1)
                l3 = GB[:, 0:NT * E].rearrange("p (t e) -> p t e", e=E)
                if w["br"] is not None:
                    chain(v.tensor_tensor(lg[:], l3, w["br"].rearrange("p (a e) -> p a e", a=1).broadcast_to([P, NT, E]),
                                          ALU.add))
                else:
                    chain(v.tensor_copy(lg[:], l3))
                chain(v.tensor_reduce(m1[:], lg[:], AX.X, ALU.max))
                chain(v.tensor_tensor(pr[:], lg[:], b8(m1[:]), ALU.subtract))
                v.wait_ge(stepa, 1)
                chain(v.tensor_reduce(m1[:], pr[:], AX.X, ALU.add))
                chain(v.reciprocal(m1[:], m1[:]))
                chain(v.tensor_tensor(pr[:], pr[:], b8(m1[:]), ALU.mult))
                if rule == "experts":
                    assert count[0] == w["steps_to_probs"]
                    v.wait_ge(stepp, 1)
                    chain(v.tensor_copy(pT[:], GB[:, 0:P]))
                    v.wait_ge(stepg2, 2)
                    chain(v.tensor_single_scalar(cand[:], low[:], 1 << (BITS - 1), ALU.bitwise_or))
                    for k in range(BITS):
                        v.tensor_scalar(msk[:], pT[:], cand[:].bitcast(F32), 0.0, ALU.is_ge, ALU.add,
                                        accum_out=cnt[:]).then_inc(stepg, 1)
                        v.wait_ge(stepp, k + 2)
                        chain(v.tensor_scalar(take[:], LB[:, 0:1], float(w["capacity"]), float(1 << (BITS - 1 - k)),
                                              ALU.is_ge, ALU.mult))
                        if k + 1 < BITS:
                            v.scalar_tensor_tensor(cand[:], take[:], 1 << (BITS - 2 - k), low[:], ALU.bitwise_or,
                                                   ALU.bitwise_or).then_inc(step, 1)
                            count[0] += 1
                        v.tensor_tensor(low[:], take[:], low[:], ALU.bitwise_or).then_inc(stepg, 1)
                        if k + 1 < BITS:
                            v.wait_ge(step, count[0])
                        v.wait_ge(stepg, 2 * k + 2)
                    v.tensor_scalar(msk[:], pT[:], low[:].bitcast(F32), 0.0, ALU.is_gt, ALU.add,
                                    accum_out=cnt[:]).then_inc(stepg, 1)
                    v.wait_ge(stepg, 2 * BITS + 1)
                    v.tensor_scalar(eq[:], pT[:], low[:].bitcast(F32), None, ALU.is_equal).then_inc(stepg, 1)
                    v.wait_ge(stepg, 2 * BITS + 2)
                    v.tensor_tensor_scan(cum[:], eq[:], zero[:], 0.0, ALU.add, ALU.add)
                    v.wait_ge(stepp, BITS + 2)
                    chain(v.tensor_scalar(left[:], LB[:, 0:1], -1.0, float(w["capacity"]), ALU.mult, ALU.add))
                    v.drain().then_inc(stepg, 1)
                    v.wait_ge(stepp, BITS + 3)
                    chain(v.tensor_copy(prf[:], LB[:, 0:1]))
                    chain(v.tensor_scalar(cum[:], cum[:], prf[:], left[:], ALU.add, ALU.is_le))
                    chain(v.tensor_tensor(eq[:], eq[:], cum[:], ALU.mult))
                    chain(v.tensor_tensor(msk[:], msk[:], eq[:], ALU.add))
                    v.tensor_tensor(msk[:], msk[:], pT[:], ALU.mult).then_inc(stepg, 1)
                    v.wait_ge(stepp, BITS + 4)
                    v.tensor_scalar(gates[:].rearrange("p t e -> p (t e)"), GB[:, 0:P], tgate, None,
                                    ALU.mult).then_inc(gates_ready, 1)
                else:
                    of = lg if rule == "first" else pr
                    v.tensor_tensor(cmp1[:], other(of[:]), mine(of[:]), ALU.is_gt)
                    chain(v.tensor_tensor(cmp2[:], other(of[:]), mine(of[:]), ALU.is_equal))
                    chain(v.tensor_tensor(cmp2[:].rearrange("p t e f -> p t (e f)"),
                                          cmp2[:].rearrange("p t e f -> p t (e f)"),
                                          w["before"].rearrange("p (a n) -> p a n", a=1).broadcast_to([P, NT, E * E]), ALU.mult))
                    chain(v.tensor_tensor(cmp1[:], cmp1[:], cmp2[:], ALU.add))
                    chain(v.tensor_reduce(rank[:], cmp1[:], AX.X, ALU.add))
                    top = 1.0 if rule == "first" else 4.0
                    chain(v.tensor_single_scalar(rank[:], rank[:], top, ALU.is_lt))
                    chain(v.tensor_tensor(pr[:], pr[:], rank[:], ALU.mult))
                    if rule == "four":
                        chain(v.tensor_reduce(m1[:], pr[:], AX.X, ALU.add))
                        chain(v.reciprocal(m1[:], m1[:]))
                        chain(v.tensor_tensor(pr[:], pr[:], b8(m1[:]), ALU.mult))
                    v.tensor_scalar(gates[:], pr[:], tgate, None, ALU.mult).then_inc(gates_ready, 1)
                v.wait_ge(gates_ready, 1)

                def biases(q):
                    v.wait_ge(gT_ready, q + 1)
                    v.tensor_copy(gT[:, CH * q:CH * (q + 1), :].rearrange("p t n -> p (t n)"),
                                  GB[0:E, :]).then_inc(gT_copied, 1)
                    v.wait_ge(bias_ready, q + 1)
                    xs = c.x[:, CH * q:CH * (q + 1), :].rearrange("p t n -> p (t n)")
                    v.tensor_tensor(xs, LB[:, :], xs, ALU.add).then_inc(bias_added, 1)
                    v.wait_ge(bias_added, q + 1)

                def stats(q, n, src):
                    for t in range(CH):
                        v.bn_stats(st[:, t, :], src(t)).then_inc(st_ready, 1)
                    v.wait_ge(st_ready, CH * (n + 1))
                    for t in range(CH):
                        v.bn_aggr(mv[:, t, :], st[:, t, :]).then_inc(mv_ready, 1)

                def normalise(q, n, src):
                    v.wait_ge(mv_ready, CH * (n + 1))
                    v.wait_ge(rstd_ready, 2 * (n + 1))
                    need(v, xT_ready, q)
                    for t in range(CH):
                        v.tensor_scalar(xn[:, t, :], src(t), mv[:, t, 0:1], rstd[:, t:t + 1], ALU.subtract,
                                        ALU.mult).then_inc(norm_sem(n), 1)

                def norm_sem(n):
                    return xn_ready if not double or n % 2 else xn1_ready

                def ln_step(q, i):
                    x1 = lambda t: c.x[:, CH * q + t, :]
                    x2 = lambda t: xn[:, t, :]
                    n = 2 * q if double else q
                    if i == 0:
                        stats(q, n, x1)
                    elif i == 1:
                        normalise(q, n, x1)
                        if double:
                            v.wait_ge(xn1_ready, CH * (q + 1))
                            stats(q, n + 1, x2)
                    elif double:
                        normalise(q, n + 1, x2)

                if w["b2"] is not None:
                    for q in range(NC):
                        biases(q)
                for k in range(len(K)):
                    q, g = K[k]
                    for e in range(per_group):
                        n = k * per_group + e
                        x = g * per_group + e
                        v.wait_ge(y_ready, n + 1)
                        if g == 0 and e == 0:
                            need(v, st_ready, 0)
                        need(v, added, 4 * n)
                        for t in range(CH):
                            xt = c.x[:, CH * q + t, :]
                            v.scalar_tensor_tensor(xt, YB[n % 2][:, t * D:(t + 1) * D], gates[:, CH * q + t, x:x + 1],
                                                   xt, ALU.mult, ALU.add).then_inc(added, 1)
                    if store:
                        continue
                    if g == groups - 1:
                        v.wait_ge(added, 4 * (k + 1) * per_group)
                        ln_step(q, 0)
                    elif g < 2 and q > 0:
                        ln_step(q - 1, g + 1)
                if not store:
                    ln_step(NC - 1, 1)
                    ln_step(NC - 1, 2)


def copy_ln(c, act, q, xT_ready, xnT_ready, bank, double):
    act.wait_ge(xT_ready, q + 1)
    dst = c.xnT[:, 4 * q:4 * (q + 1), :].rearrange("p t n -> p (t n)")
    if double:
        act.activation(dst, bank[:, :], ACT.Identity, bias=double[1], scale=double[0]).then_inc(xnT_ready, 1)
    else:
        act.copy(dst, bank[:, :]).then_inc(xnT_ready, 1)


def ternary_ffn(c, w, tgate):
    nc = c.nc
    F = 512
    FT = F // P
    CH = 4
    NC = NT // CH
    eps = 1e-6
    pre = "F1_"
    sem = lambda n: c.sublayer_sem(pre + n)
    xh_all, bias_ready = sem("x_high"), sem("bias_ready")
    (prep, prep_pe, xs_ready, up_ready, g_ready, st_ready, mv_ready, rs_ready, hn_ready, hT_ready, hh_ready, hl_ready,
     y_ready, y_copied, yT_ready, added, st2_ready, mv2_ready, rs2_ready, xn_ready, xT_ready, xnT_ready) = (
        sem(n) for n in (
            "weights_step", "weights_sums", "x_split", "up_ready", "gelu_ready", "h_stats", "h_mv", "h_rstd", "h_normed",
            "hT_ready", "h_high", "h_low", "down_ready", "down_copied", "down_turned", "added", "ln_stats", "ln_mv",
            "ln_rstd", "ln_xn", "ln_xT", "ln_xnT"))
    UB, HB, YB, TB, LB = c.banks[0:2], c.banks[2:4], c.banks[4], c.banks[5], c.banks[6]
    with ExitStack() as own:
        sb = lambda n, s, d=F32: own.enter_context(nc.sbuf_tensor(pre + n, s, d))
        tmp = sb("tmp", [P, 2, F])
        wf = sb("wf", [P, F], F32R)
        wp = sb("wp", [P, FT, D], F32R)
        sums = sb("sums", [P, 2])
        thr = sb("thr", [P, 2, 2])
        bias = sb("bias", [P, 1])
        xh = sb("xh", [P, NT, P], F32R)
        xl = sb("xl", [P, NT, P], F32R)
        hg = sb("hg", [P, 2, F])
        hn = sb("hn", [P, 2, F])
        hh = sb("hh", [P, 2, FT, CH, P], F32R)
        hl = sb("hl", [P, 2, FT, CH, P], F32R)
        yT = sb("yT", [P, F])
        st1 = sb("st1", [P, 6])
        mv1 = sb("mv1", [P, 2, 2])
        ve1 = sb("ve1", [P, 1])
        rs1 = sb("rs1", [P, 2, 1])
        ln = layer_norm_tail(c, own, pre)
        st, mv, ve, rstd, xn = (ln[k] for k in ("st", "mv", "ve", "rstd", "xn"))
        WF, WP = w["WfT"], w["WpT"].rearrange("p (j d) -> p j d", j=FT)

        with nc.Block() as block:
            @block.tensor
            def _(pe):
                for s, all_loads in w["loaded"]:
                    pe.wait_ge(s, all_loads)
                pe.wait_ge(prep, 2)
                pe.matmul(LB[:, 0:2], c.ones[:], sums[:], start=True, stop=True).then_inc(prep_pe, 1)
                pe.wait_ge(prep, 8)
                for j in range(FT):
                    m = pe.matmul(TB[:, 0:1], wp[:, j, :].bitcast(F32), w["lnb"][:, j:j + 1],
                                  start=(j == 0), stop=(j == FT - 1))
                m.then_inc(prep_pe, 1)

                def up(t):
                    if t % CH == 0:
                        pe.wait_ge(xs_ready, t // CH + 1)
                    need(pe, g_ready, t - 1)
                    pe.matmul(UB[t % 2][:, :], xh[:, t, :], wf[:], start=True, stop=False)
                    pe.matmul(UB[t % 2][:, :], xl[:, t, :], wf[:], start=False, stop=True).then_inc(up_ready, 1)

                def turn(t):
                    pe.wait_ge(hn_ready, t + 1)
                    need(pe, hl_ready, t - 1)
                    for j in range(FT):
                        m = pe.transpose(HB[t % 2][:, j * P:(j + 1) * P], hn[:, t % 2, j * P:(j + 1) * P], c.ident[:])
                    m.then_inc(hT_ready, 1)

                def down(q):
                    pe.wait_ge(hl_ready, CH * (q + 1))
                    need(pe, y_copied, q)
                    n = 0
                    for part in (hh, hl):
                        for j in range(FT):
                            m = pe.matmul(YB[:, :], wp[:, j, :], part[:, q % 2, j].rearrange("p t n -> p (t n)"),
                                          start=(n == 0), stop=(n == 2 * FT - 1))
                            n += 1
                    m.then_inc(y_ready, 1)

                def turn_y(q):
                    pe.wait_ge(y_copied, q + 1)
                    need(pe, added, q)
                    if q == 0:
                        pe.wait_ge(bias_ready, 1)
                    for t in range(CH):
                        m = pe.transpose(TB[:, t * P:(t + 1) * P], yT[:, t * P:(t + 1) * P], c.ident[:])
                    m.then_inc(yT_ready, 1)

                def turn_ln(q):
                    pe.wait_ge(xn_ready, CH * (q + 1))
                    need(pe, xnT_ready, q)
                    for t in range(CH):
                        m = pe.transpose(LB[:, t * P:(t + 1) * P], xn[:, t, :], c.ident[:])
                    m.then_inc(xT_ready, 1)

                LAG = 2
                for t in range(NT + 15):
                    if t < NT:
                        up(t)
                    if 0 <= t - LAG < NT:
                        turn(t - LAG)
                    if t - 4 >= 0 and (t - 4) % CH == CH - 1 and (t - 4) // CH < NC:
                        down((t - 4) // CH)
                    if t - 7 >= 0 and (t - 7) % CH == CH - 1 and (t - 7) // CH < NC:
                        turn_y((t - 7) // CH)
                    if t - 11 >= 0 and (t - 11) % CH == CH - 1 and (t - 11) // CH < NC:
                        turn_ln((t - 11) // CH)

            @block.scalar
            def _(act):
                for s, all_loads in w["loaded"]:
                    act.wait_ge(s, all_loads)
                act.copy(xh[:], c.xnT[:]).then_inc(xh_all, 1)
                act.wait_ge(prep_pe, 2)
                act.copy(bias[:], TB[:, 0:1]).then_inc(bias_ready, 1)
                for t in range(NT + 15):
                    if t < NT:
                        act.wait_ge(up_ready, t + 1)
                        need(act, hn_ready, t - 1)
                        act.activation(hg[:, t % 2, :], UB[t % 2][:, :], ACT.Gelu).then_inc(g_ready, 1)
                    if 0 <= t - 2 < NT:
                        n = t - 2
                        act.wait_ge(hT_ready, n + 1)
                        need(act, y_ready, n // CH - 1)
                        for j in range(FT):
                            i = act.activation(hh[:, n // CH % 2, j, n % CH, :], HB[n % 2][:, j * P:(j + 1) * P],
                                               ACT.Copy, scale=w["lnw"][:, j:j + 1])
                        i.then_inc(hh_ready, 1)
                    if t - 5 >= 0 and (t - 5) % CH == CH - 1 and (t - 5) // CH < NC:
                        q = (t - 5) // CH
                        act.wait_ge(y_ready, q + 1)
                        need(act, yT_ready, q)
                        if q == 0:
                            act.wait_ge(bias_ready, 1)
                        act.activation(yT[:], YB[:, :], ACT.Identity, bias=bias[:]).then_inc(y_copied, 1)
                    if t - 11 >= 0 and (t - 11) % CH == CH - 1 and (t - 11) // CH < NC:
                        copy_ln(c, act, (t - 11) // CH, xT_ready, xnT_ready, LB, None)

            @block.gpsimd
            def _(g):
                c.clear_spent(g)
                g.wait_ge(xh_all, 1)
                for q in range(NC):
                    s = slice(CH * q, CH * (q + 1))
                    g.tensor_tensor(xl[:, s, :], c.xnT[:, s, :], xh[:, s, :].bitcast(F32),
                                    ALU.subtract).then_inc(xs_ready, 1)
                for t in range(NT + 15):
                    if t < NT:
                        g.wait_ge(mv_ready, t + 1)
                        need(g, rs_ready, 2 * t)
                        g.tensor_scalar(ve1[:], mv1[:, t % 2, 1:2], LN_EPS, None, ALU.add).then_inc(rs_ready, 1)
                        g.wait_ge(rs_ready, 2 * t + 1)
                        g.tensor_tensor(rs1[:, t % 2], ve1[:], c.mhalf[:, 0:1], ALU.pow).then_inc(rs_ready, 1)
                    if t - 9 >= 0 and (t - 9) % CH == CH - 1 and (t - 9) // CH < NC:
                        q = (t - 9) // CH
                        g.wait_ge(mv2_ready, CH * (q + 1))
                        g.tensor_scalar(ve[:], mv[:, :, 1], LN_EPS, None, ALU.add).then_inc(rs2_ready, 1)
                        g.wait_ge(rs2_ready, 2 * q + 1)
                        g.tensor_tensor(rstd[:], ve[:], c.mhalf[:, 0:4], ALU.pow).then_inc(rs2_ready, 1)

            @block.vector
            def _(v):
                count = [0]

                def chain(i):
                    count[0] += 1
                    i.then_inc(prep, 1)
                    v.wait_ge(prep, count[0])

                for s, all_loads in w["loaded"]:
                    v.wait_ge(s, all_loads)
                chain(v.tensor_reduce(sums[:, 0:1], WF, AX.X, ALU.add, apply_absolute_value=True))
                chain(v.tensor_reduce(sums[:, 1:2], w["WpT"], AX.X, ALU.add, apply_absolute_value=True))
                v.wait_ge(prep_pe, 1)
                half = 0.5 / (D * F)
                chain(v.tensor_scalar(thr[:, 0], LB[:, 0:2], half, 0.5 * eps, ALU.mult, ALU.add))
                chain(v.tensor_scalar(thr[:, 1], thr[:, 0], -1.0, None, ALU.mult))
                chain(v.tensor_scalar(tmp[:, 0, :], WF, thr[:, 1, 0:1], None, ALU.is_lt))
                chain(v.scalar_tensor_tensor(wf[:], WF, thr[:, 0, 0:1], tmp[:, 0, :], ALU.is_gt, ALU.subtract))
                chain(v.tensor_scalar(tmp[:, 1, :], w["WpT"], thr[:, 1, 1:2], None, ALU.is_lt))
                chain(v.scalar_tensor_tensor(wp[:].rearrange("p j d -> p (j d)"), w["WpT"], thr[:, 0, 1:2], tmp[:, 1, :],
                                             ALU.is_gt, ALU.subtract))

                def low(n):
                    v.wait_ge(hh_ready, n + 1)
                    for j in range(FT):
                        i = v.scalar_tensor_tensor(hl[:, n // CH % 2, j, n % CH, :], HB[n % 2][:, j * P:(j + 1) * P],
                                                   w["lnw"][:, j:j + 1], hh[:, n // CH % 2, j, n % CH, :].bitcast(F32),
                                                   ALU.mult, ALU.subtract)
                    i.then_inc(hl_ready, 1)

                for t in range(NT + 15):
                    if t < NT:
                        v.wait_ge(g_ready, t + 1)
                        need(v, mv_ready, t)
                        v.bn_stats(st1[:], hg[:, t % 2, :]).then_inc(st_ready, 1)
                        v.wait_ge(st_ready, t + 1)
                        need(v, rs_ready, 2 * (t - 1) + 1)
                        v.bn_aggr(mv1[:, t % 2, :], st1[:]).then_inc(mv_ready, 1)
                    if 0 <= t - 1 < NT:
                        n = t - 1
                        v.wait_ge(rs_ready, 2 * n + 2)
                        need(v, hT_ready, n - 1)
                        v.tensor_scalar(hn[:, n % 2, :], hg[:, n % 2, :], mv1[:, n % 2, 0:1], rs1[:, n % 2, 0:1],
                                        ALU.subtract, ALU.mult).then_inc(hn_ready, 1)
                    if 0 <= t - 2 < NT:
                        low(t - 2)
                    if t - 7 >= 0 and (t - 7) % CH == CH - 1 and (t - 7) // CH < NC:
                        q = (t - 7) // CH
                        v.wait_ge(yT_ready, q + 1)
                        xs = c.x[:, CH * q:CH * (q + 1), :].rearrange("p t n -> p (t n)")
                        v.scalar_tensor_tensor(xs, TB[:, :], tgate, xs, ALU.mult, ALU.add).then_inc(added, 1)
                        v.wait_ge(added, q + 1)
                        for k in range(CH):
                            v.bn_stats(st[:, k, :], c.x[:, CH * q + k, :]).then_inc(st2_ready, 1)
                        v.wait_ge(st2_ready, CH * (q + 1))
                        for k in range(CH):
                            v.bn_aggr(mv[:, k, :], st[:, k, :]).then_inc(mv2_ready, 1)
                    if t - 10 >= 0 and (t - 10) % CH == CH - 1 and (t - 10) // CH < NC:
                        q = (t - 10) // CH
                        v.wait_ge(mv2_ready, CH * (q + 1))
                        v.wait_ge(rs2_ready, 2 * (q + 1))
                        need(v, xT_ready, q)
                        for k in range(CH):
                            v.tensor_scalar(xn[:, k, :], c.x[:, CH * q + k, :], mv[:, k, 0:1], rstd[:, k:k + 1],
                                            ALU.subtract, ALU.mult).then_inc(xn_ready, 1)


def wide_attention(c, w, next_loads, gate):
    nc = c.nc
    W64 = 64
    NP = H // 2
    M = B * NP
    SC = 0.125
    NPS, TRS, QKB, VB, OB, MISC = c.banks[0:2], c.banks[2:4], c.banks[4], c.banks[5], c.banks[6], c.banks[7]
    pre = "L1_"
    sem = lambda n: c.sublayer_sem(pre + n)
    (ct0, ct1, zeroed, gate_ready, qk_ready, hi_ready, lo_ready, n_ready, max_ready, p_ready, rc_ready, norm0_ready, norm1_ready,
     tr_ready, pt_even, pt_odd, pv_ready, o_ready, vp_ready, v_ready, po_ready, resid, st_ready, mv_ready, rstd_ready,
     xn_ready, xT_ready, xnT_ready) = (sem(n) for n in (
         "ctx_loaded0", "ctx_loaded1", "zeroed", "gate_ready", "qk_projected", "split_high", "split_low",
         "scores_ready", "max_ready", "exp_ready", "recip_ready", "probs_normed0", "probs_normed1", "probs_turned", "probsT_even", "probsT_odd",
         "pv_ready", "ctx_copied", "v_projected", "v_ready", "out_ready", "resid_ready", "ln_stats", "ln_mv",
         "ln_rstd", "ln_xn", "ln_xT", "ln_xnT"))
    ct_in = [ct0, ct1]
    wh_ready, wl_ready, th_ready, tl_ready = (sem(n) for n in ("weights_high", "weights_low", "tokens_high", "tokens_low"))
    CHUNKS = [("Wq", 0), ("Wk", 0), ("Wv", 0), ("Wv", 1), ("Wq", 1), ("Wk", 1)]
    with ExitStack() as own:
        sb = lambda n, s, d=F32: own.enter_context(nc.sbuf_tensor(pre + n, s, d))
        ct = sb("ct", [P, 2, S])
        qh = sb("qh", [P, 2, 2, S], F32R)
        ql = sb("ql", [P, 2, 2, S], F32R)
        kh = sb("kh", [P, 2, S], F32R)
        kl = sb("kl", [P, 2, S], F32R)
        split_w = {k: [sb(k + n, [P, H * W64], F32R) for n in ("h", "l")] for k in ("Wq", "Wk", "Wv")}
        tok = [sb("tokens_" + n, [P, 2, 2, S], F32R) for n in ("h", "l")]
        nm = sb("nm", [P, 4, TPB])
        sm = sb("sm", [P, 4, TPB])
        rs = sb("rs", [P, 4, TPB])
        pn = sb("pn", [P, 4, TPB, S])
        pt = sb("pt", [P, 4, TPB, S])
        vv = sb("vv", [P, 2, TPB, H * W64])
        oT = sb("oT", [P, 2, NP, S])
        g2 = sb("g2", [P, 1])
        st = sb("st", [P, TPB, 6])
        mv = sb("mv", [P, TPB, 2])
        ve = sb("ve", [P, TPB])
        rstd = sb("rstd", [P, TPB])
        xn = sb("xn", [P, TPB, D])

        with nc.Block() as block:
            @block.sync
            def _(sp):
                for b in range(B):
                    if b >= 2:
                        sp.wait_ge(tl_ready, 2 * (b - 1))
                    sp.dma_start(ct[:, b % 2, :], c.a["ctxT"][:, b * S:(b + 1) * S]).then_inc(ct_in[b % 2], 16)
                    if b == 1:
                        for s, dst, src in next_loads:
                            sp.dma_start(dst, src).then_inc(s, 16)

            @block.tensor
            def _(pe):
                def split_product(o, left, right):
                    pe.matmul(o, left[0], right[0], start=True, stop=False)
                    pe.matmul(o, left[0], right[1], start=False, stop=False)
                    return pe.matmul(o, left[1], right[0], start=False, stop=True)

                def wait_split(b, chunks):
                    pe.wait_ge(wh_ready, chunks)
                    pe.wait_ge(wl_ready, chunks)
                    pe.wait_ge(th_ready, 2 * (b + 1))
                    pe.wait_ge(tl_ready, 2 * (b + 1))

                def project(m):
                    b, p = divmod(m, NP)
                    need(pe, lo_ready, 3 * m)
                    wait_split(b, 2 if p < NP // 2 and b == 0 else len(CHUNKS))
                    part = lambda k: [x[:, p * P:(p + 1) * P] for x in split_w[k]]
                    split_product(QKB[:, 0:S], part("Wq"), [x[:, b % 2, 0, :] for x in tok])
                    split_product(QKB[:, S:2 * S], part("Wk"), [x[:, b % 2, 1, :] for x in tok]).then_inc(qk_ready, 1)

                def project_v(b, i):
                    t, half = divmod(i, 2)
                    need(pe, v_ready, 4 * b + i)
                    wait_split(b, 4)
                    split_product(VB[:, :], [x[:, b % 2, 1, t * P:(t + 1) * P] for x in tok],
                                  [x[:, half * 512:(half + 1) * 512] for x in split_w["Wv"]]).then_inc(vp_ready, 1)

                def scores(n):
                    m, s = divmod(n, 2)
                    if s == 0:
                        pe.wait_ge(lo_ready, 3 * (m + 1))
                    need(pe, p_ready, 2 * (n - 1))
                    for t in range(TPB):
                        o = NPS[n % 2][:, t * S:(t + 1) * S]
                        q = slice(t * P, (t + 1) * P)
                        pe.matmul(o, qh[:, m % 2, s, q], kh[:, m % 2, :], start=True, stop=False)
                        pe.matmul(o, qh[:, m % 2, s, q], kl[:, m % 2, :], start=False, stop=False)
                        i = pe.matmul(o, ql[:, m % 2, s, q], kh[:, m % 2, :], start=False, stop=True)
                    i.then_inc(n_ready, 1)

                def turn(n):
                    pe.wait_ge(norm0_ready, n + 1)
                    pe.wait_ge(norm1_ready, n + 1)
                    need(pe, (pt_even, pt_odd)[n % 2], n // 2)
                    for k in range(TPB):
                        for t in range(TPB):
                            i = pe.transpose(TRS[n % 2][:, k * S + t * P:k * S + (t + 1) * P],
                                             pn[:, n % 4, t, k * P:(k + 1) * P], c.ident[:])
                    i.then_inc(tr_ready, 1)

                def pv(m):
                    b, p = divmod(m, NP)
                    pe.wait_ge(pt_even, m + 1)
                    pe.wait_ge(pt_odd, m + 1)
                    need(pe, o_ready, m)
                    pe.wait_ge(v_ready, 4 * (b + 1))
                    for k in range(TPB):
                        for s in range(2):
                            h = 2 * p + s
                            i = pe.matmul(OB[W64 * s:W64 * (s + 1), 0:S], vv[:, b % 2, k, h * W64:(h + 1) * W64],
                                          pt[:, (2 * m + s) % 4, k, :], start=(k == 0), stop=(k == 1))
                    i.then_inc(pv_ready, 1)

                def out(b):
                    pe.wait_ge(o_ready, NP * (b + 1))
                    need(pe, xnT_ready, b)
                    for t in range(TPB):
                        o = MISC[:, t * D:(t + 1) * D]
                        for p in range(NP):
                            pe.matmul(o, oT[:, b % 2, p, t * P:(t + 1) * P], w["Wo"][:, p * D:(p + 1) * D],
                                      start=(p == 0), stop=False)
                        i = pe.matmul(o, c.ones[0:1, :], w["bo"], start=False, stop=True)
                    i.then_inc(po_ready, 1)

                def turn_ln(b):
                    pe.wait_ge(xn_ready, 2 * (b + 1))
                    for t in range(TPB):
                        i = pe.transpose(MISC[:, t * P:(t + 1) * P], xn[:, t, :], c.ident[:])
                    i.then_inc(xT_ready, 1)

                for s, all_loads in w["loaded"]:
                    pe.wait_ge(s, all_loads)
                project(0)
                for m in range(M + 8):
                    b, p = divmod(m, NP)
                    for s in range(2):
                        n = 2 * m + s
                        if m < M:
                            scores(n)
                        if s == 0 and m + 1 < M:
                            project(m + 1)
                        if m == 0 and s == 0:
                            for i in range(4):
                                project_v(0, i)
                        if 0 <= n - 3 < 2 * M:
                            turn(n - 3)
                        if s == 0 and 0 <= m - 3 < M:
                            pv(m - 3)
                    if 3 <= p < 7 and b + 1 < B:
                        project_v(b + 1, p - 3)
                    if m >= 12 and (m - 12) % NP == 0 and (m - 12) // NP < B:
                        out((m - 12) // NP)
                    if m >= 15 and (m - 15) % NP == 0 and (m - 15) // NP < B:
                        turn_ln((m - 15) // NP)

            @block.scalar
            def _(act):
                def split(m):
                    act.wait_ge(qk_ready, m + 1)
                    need(act, n_ready, 2 * (m - 1))
                    for s in range(2):
                        r = slice(W64 * s, W64 * (s + 1))
                        act.activation(qh[r, m % 2, s, :], QKB[r, 0:S], ACT.Copy, scale=SC).then_inc(hi_ready, 1)
                    act.copy(kh[:, m % 2, :], QKB[:, S:2 * S]).then_inc(hi_ready, 1)

                def copy_v(b, i):
                    t, half = divmod(i, 2)
                    act.wait_ge(vp_ready, 4 * b + i + 1)
                    need(act, pv_ready, NP * (b - 1))
                    act.copy(vv[:, b % 2, t, half * 512:(half + 1) * 512], VB[:, :]).then_inc(v_ready, 1)

                for s, all_loads in w["loaded"]:
                    act.wait_ge(s, all_loads)
                def token_high(b):
                    act.wait_ge(ct_in[b % 2], 16 * (b // 2 + 1))
                    need(act, qk_ready, NP * (b - 1))
                    need(act, vp_ready, 4 * (b - 1))
                    act.copy(tok[0][:, b % 2, 0, :],
                             c.xnT[:, TPB * b:TPB * (b + 1), :].rearrange("p t n -> p (t n)")).then_inc(th_ready, 1)
                    act.copy(tok[0][:, b % 2, 1, :], ct[:, b % 2, :]).then_inc(th_ready, 1)

                def weight_high(n):
                    k, half = CHUNKS[n]
                    cols = slice(half * 512, (half + 1) * 512)
                    act.copy(split_w[k][0][:, cols], w[k][:, cols]).then_inc(wh_ready, 1)

                weight_high(0)
                weight_high(1)
                token_high(0)
                act.activation(g2[:], w["gate"], ACT.Tanh).then_inc(gate_ready, 1)
                act.wait_ge(gate_ready, 1)
                act.activation(g2[:], g2[:], ACT.Copy, scale=gate).then_inc(gate_ready, 1)
                act.wait_ge(zeroed, 2)
                split(0)
                for n in range(2, len(CHUNKS)):
                    weight_high(n)
                for m in range(M + 8):
                    b, p = divmod(m, NP)
                    for s in range(2):
                        n = 2 * m + s
                        if s == 0 and m + 1 < M:
                            split(m + 1)
                        if s == 1 and 0 <= n - 4 < 2 * M:
                            k = n - 4
                            act.wait_ge(tr_ready, k + 1)
                            need(act, pv_ready, k // 2 - 1)
                            act.copy(pt[:, k % 4].rearrange("p t n -> p (t n)"), TRS[k % 2][:, :]).then_inc(pt_odd, 1)
                        if m < M:
                            act.wait_ge(max_ready, n + 1)
                            need(act, tr_ready, n - 3)
                            for t in range(TPB):
                                act.activation(pn[:, n % 4, t, :], NPS[n % 2][:, t * S:(t + 1) * S], ACT.Exp,
                                               bias=nm[:, n % 4, t:t + 1],
                                               accum_out=sm[:, n % 4, t:t + 1]).then_inc(p_ready, 1)
                        if m == 0 and s == 0:
                            for i in range(4):
                                copy_v(0, i)
                        if s == 0 and 0 <= m - 3 < M:
                            k = m - 3
                            act.wait_ge(pv_ready, k + 1)
                            if k % NP == 0:
                                need(act, po_ready, k // NP - 1)
                            act.copy(oT[:, k // NP % 2, k % NP, :], OB[:, 0:S]).then_inc(o_ready, 1)
                    if p == 1 and b + 1 < B:
                        token_high(b + 1)
                    if 3 <= p < 7 and b + 1 < B:
                        copy_v(b + 1, p - 3)
                    if m >= 15 and (m - 15) % NP == 0 and (m - 15) // NP < B:
                        k = (m - 15) // NP
                        act.wait_ge(xT_ready, k + 1)
                        act.copy(c.xnT[:, TPB * k:TPB * (k + 1), :].rearrange("p t n -> p (t n)"),
                                 MISC[:, 0:S]).then_inc(xnT_ready, 1)

            @block.gpsimd
            def _(g):
                c.clear_spent(g)
                def token_low(b):
                    g.wait_ge(th_ready, 2 * (b + 1))
                    need(g, qk_ready, NP * (b - 1))
                    need(g, vp_ready, 4 * (b - 1))
                    g.tensor_tensor(tok[1][:, b % 2, 0, :],
                                    c.xnT[:, TPB * b:TPB * (b + 1), :].rearrange("p t n -> p (t n)"),
                                    tok[0][:, b % 2, 0, :].bitcast(F32), ALU.subtract).then_inc(tl_ready, 1)
                    g.tensor_tensor(tok[1][:, b % 2, 1, :], ct[:, b % 2, :], tok[0][:, b % 2, 1, :].bitcast(F32),
                                    ALU.subtract).then_inc(tl_ready, 1)

                g.memset(ql[:].bitcast(F32), 0.0).then_inc(zeroed, 1)
                token_low(0)
                for m in range(M + 8):
                    if m % NP == 2 and m // NP + 1 < B:
                        token_low(m // NP + 1)
                    for s in range(2):
                        n = 2 * m + s
                        if m < M:
                            g.wait_ge(rc_ready, n + 1)
                            g.tensor_scalar(pn[:, n % 4, 0, :], pn[:, n % 4, 0, :], rs[:, n % 4, 0:1], None,
                                            ALU.mult).then_inc(norm0_ready, 1)
                    if m >= 13 and (m - 13) % NP == 0 and (m - 13) // NP < B:
                        k = (m - 13) // NP
                        g.wait_ge(mv_ready, 2 * (k + 1))
                        g.tensor_scalar(ve[:], mv[:, :, 1], LN_EPS, None, ALU.add).then_inc(rstd_ready, 1)
                        g.wait_ge(rstd_ready, 2 * k + 1)
                        g.tensor_tensor(rstd[:], ve[:], c.mhalf[:, 0:TPB], ALU.pow).then_inc(rstd_ready, 1)

            @block.vector
            def _(v):
                def split(m):
                    v.wait_ge(hi_ready, 3 * (m + 1))
                    for s in range(2):
                        r = slice(W64 * s, W64 * (s + 1))
                        v.scalar_tensor_tensor(ql[r, m % 2, s, :], QKB[r, 0:S], SC, qh[r, m % 2, s, :].bitcast(F32),
                                               ALU.mult, ALU.subtract).then_inc(lo_ready, 1)
                    v.tensor_tensor(kl[:, m % 2, :], QKB[:, S:2 * S], kh[:, m % 2, :].bitcast(F32),
                                    ALU.subtract).then_inc(lo_ready, 1)

                def recip(n):
                    v.wait_ge(p_ready, 2 * (n + 1))
                    v.reciprocal(rs[:, n % 4, :], sm[:, n % 4, :]).then_inc(rc_ready, 1)

                v.memset(qh[:].bitcast(F32), 0.0).then_inc(zeroed, 1)
                for s, all_loads in w["loaded"]:
                    v.wait_ge(s, all_loads)
                def weight_low(n):
                    k, half = CHUNKS[n]
                    cols = slice(half * 512, (half + 1) * 512)
                    v.wait_ge(wh_ready, n + 1)
                    v.tensor_tensor(split_w[k][1][:, cols], w[k][:, cols], split_w[k][0][:, cols].bitcast(F32),
                                    ALU.subtract).then_inc(wl_ready, 1)

                weight_low(0)
                weight_low(1)
                v.wait_ge(zeroed, 2)
                split(0)
                for n in range(2, len(CHUNKS)):
                    weight_low(n)
                for m in range(M + 8):
                    for s in range(2):
                        n = 2 * m + s
                        if m < M:
                            v.wait_ge(n_ready, n + 1)
                            v.tensor_reduce(nm[:, n % 4, :], NPS[n % 2][:, :].rearrange("p (t n) -> p t n", t=TPB),
                                            AX.X, ALU.max, negate=True).then_inc(max_ready, 1)
                        if 0 <= n - 1 < 2 * M:
                            recip(n - 1)
                        if 0 <= n - 1 < 2 * M:
                            k = n - 1
                            v.wait_ge(rc_ready, k + 1)
                            v.tensor_scalar(pn[:, k % 4, 1, :], pn[:, k % 4, 1, :], rs[:, k % 4, 1:2], None,
                                            ALU.mult).then_inc(norm1_ready, 1)
                        if s == 0 and 0 <= n - 4 < 2 * M:
                            k = n - 4
                            v.wait_ge(tr_ready, k + 1)
                            need(v, pv_ready, k // 2 - 1)
                            v.tensor_copy(pt[:, k % 4].rearrange("p t n -> p (t n)"), TRS[k % 2][:, :]).then_inc(pt_even, 1)
                        if s == 0 and m + 1 < M:
                            split(m + 1)
                    if m >= 12 and (m - 12) % NP == 0 and (m - 12) // NP < B:
                        k = (m - 12) // NP
                        v.wait_ge(po_ready, k + 1)
                        if k == 0:
                            v.wait_ge(gate_ready, 2)
                        xs = c.x[:, TPB * k:TPB * (k + 1), :].rearrange("p t n -> p (t n)")
                        v.scalar_tensor_tensor(xs, MISC[:, 0:S], g2[:, 0:1], xs, ALU.mult, ALU.add).then_inc(resid, 1)
                        v.wait_ge(resid, k + 1)
                        for t in range(TPB):
                            v.bn_stats(st[:, t, :], c.x[:, TPB * k + t, :]).then_inc(st_ready, 1)
                        v.wait_ge(st_ready, 2 * (k + 1))
                        for t in range(TPB):
                            v.bn_aggr(mv[:, t, :], st[:, t, :]).then_inc(mv_ready, 1)
                    if m >= 14 and (m - 14) % NP == 0 and (m - 14) // NP < B:
                        k = (m - 14) // NP
                        v.wait_ge(mv_ready, 2 * (k + 1))
                        v.wait_ge(rstd_ready, 2 * (k + 1))
                        need(v, xT_ready, k)
                        for t in range(TPB):
                            v.tensor_scalar(xn[:, t, :], c.x[:, TPB * k + t, :], mv[:, t, 0:1], rstd[:, t:t + 1],
                                            ALU.subtract, ALU.mult).then_inc(xn_ready, 1)


def window_mask(c, name, window):
    W = P + window
    m = c.sb(name, [P, TPB, W], BF16)
    return m, window


def draw_masks(g, masks, made):
    n = 0
    for m, window in masks:
        W = P + window
        g.memset(m[:], 0.0).then_inc(made, 1)
        n += 1
        g.wait_ge(made, n)
        for t in range(TPB):
            off = window * t
            g.affine_select(out=m[:, t, :], in_=m[:, t, :], compare_op=ALU.is_ge, fill=NEG,
                            base=off + window, pattern=[[-1, W]], channel_multiplier=1).then_inc(made, 1)
            n += 1
            g.wait_ge(made, n)
            g.affine_select(out=m[:, t, :], in_=m[:, t, :], compare_op=ALU.is_ge, fill=NEG,
                            base=window - off, pattern=[[1, W]], channel_multiplier=-1).then_inc(made, 1)
            n += 1
            g.wait_ge(made, n)


def program(nc, a, out, stages=range(8)):
    with ExitStack() as ctx:
        c = Chip(nc, ctx, a)
        stored = c.sem("stored")
        weights = []

        def load(name, shape, src, sems, place=None, after=None):
            t = c.sb("w_" + name, shape, F32)[:] if place is None else place
            if not sems:
                sems.append([c.sem("ld_" + name), 0])
            sems[0][1] += 16
            (weights if after is None or after + 1 not in stages else late[after]).append((sems[0][0], t, src))
            return t

        late = {1: [], 3: []}
        early, middle = c.sb("place_early", [P, 8192], F32), c.sb("place_middle", [P, 8192], F32)

        masks = []
        W = {}
        if 0 in stages:
            l = []
            w = {k: load("L0" + k, [P, P], a["L0_" + k], l) for k in ("WqT", "WkT", "WvT", "WoT")}
            w["bq"] = load("L0bq", [P, 1], col(a["L0_bq"]), l)
            w["bk"] = load("L0bk", [P, 1], col(a["L0_bk"]), l)
            w["bv"] = load("L0bv", [P, D], a["L0_bv"].partition_broadcast(P), l)
            w["bo"] = load("L0bo", [1, D], row(a["L0_bo"]), l)
            m = window_mask(c, "mask64", 64)
            masks.append(m)
            w["mask"] = m[0]
            w["loaded"] = l
            W[0] = w
        def cst(key, shape, l):
            return load(key, shape, a[key], l)

        if 1 in stages:
            l = []
            w = dict(F=341, capacity=256, steps_to_probs=6)
            w["Wr"] = load("F0Wr", [P, 8], a["F0_Wr"], l)
            w["br"] = load("F0br", [P, 8], a["F0_br"].partition_broadcast(P), l)
            w["W1"] = load("F0W1", None, a["F0_W1"], l, early[:, 0:1536])
            w["b1"] = load("F0b1", [P, 12], a["F0_b1"], l)
            w["W2"] = load("F0W2", None, a["F0_W2"], l, early[:, 1536:1536 + 24 * D])
            w["b2"] = load("F0b2", [8, D], a["F0_b2"], l)
            w["same_expert"] = cst("same_expert", [P, P], l)
            w["earlier_tile"] = cst("earlier_tile", [P, P], l)
            w["ln1"] = load("ln1", [P, 2], a["L1_ln"], l)
            w["loaded"] = l
            W[1] = w
        if 2 in stages:
            l = []
            W[2] = dict(Wq=load("L1Wq", None, a["L1_Wq"], l, middle[:, 0:1024]), Wk=load("L1Wk", None, a["L1_Wkv"][:, 0:1024], l, middle[:, 1024:2048]),
                        Wv=load("L1Wv", None, a["L1_Wkv"][:, 1024:2048], l, middle[:, 2048:3072]), Wo=load("L1Wo", None, a["L1_Wo"], l, middle[:, 3072:4096]),
                        bo=load("L1bo", [1, D], row(a["L1_bo"]), l),
                        gate=load("L1gate", [P, 1], a["L1_gate"].partition_broadcast(P), l), loaded=l)
        if 3 in stages:
            l = []
            W[3] = dict(WfT=load("F1Wf", None, a["F1_WfT"], l, middle[:, 4096:4608]), WpT=load("F1Wp", None, a["F1_WpT"], l, middle[:, 4608:5120]),
                        lnw=load("F1lnw", [P, 4], a["F1_lnw"], l), lnb=load("F1lnb", [P, 4], a["F1_lnb"], l), loaded=l)
        if 4 in stages:
            l = []
            w = {k: load("L2" + k, [P, P], a["L2_" + k], l) for k in ("WqT", "WkT", "WkTs", "WoT", "WvT", "WvTs")}
            w["bo"] = load("L2bo", [1, D], row(a["L2_bo"]), l)
            w["cosT"] = load("cosT", [P, S], a["rope_cosT"], l)
            w["sinT"] = load("sinT", [P, S], a["rope_sinT"], l)
            w["cs"] = load("rope_cs", [P, 2, TPB, D], a["rope_cs"], l)
            w["bq"] = 0.0
            w["loaded"] = l
            W[4] = w
        if 6 in stages:
            l = []
            w = {k: load("L3" + k, [P, P], a["L3_" + k], l) for k in ("WqT", "WvT", "WoT")}
            w["WkT"] = w["WqT"]
            w["bo"] = load("L3bo", [1, D], row(a["L3_bo"]), l)
            w["bq"] = w["bk"] = 0.0
            w["bv"] = None
            m = window_mask(c, "mask64b", 64) if 0 not in stages else (W[0]["mask"],)
            if 0 not in stages:
                masks.append(m)
            w["mask"] = m[0]
            w["loaded"] = l
            W[6] = w
        before_l = []
        if 5 in stages or 7 in stages:
            before = load("before", [P, 64], a["before"].partition_broadcast(P), before_l)

        if 5 in stages:
            l = []
            w = dict(F=512, before=before)
            w["Wr"] = load("F2Wr", [P, 8], a["F2_Wr"], l)
            w["br"] = load("F2br", [P, 8], a["F2_br"].partition_broadcast(P), l)
            w["W1"] = load("F2W1", None, a["F2_W1"], l, middle[:, 0:4096], 3)
            w["b1"] = load("F2b1", [P, 32], a["F2_b1"], l)
            w["W2"] = load("F2W2", None, a["F2_W2"], l, middle[:, 4096:8192], 3)
            w["b2"] = load("F2b2", [8, D], a["F2_b2"], l)
            w["loaded"] = l + before_l
            W[5] = w
        if 7 in stages:
            l = []
            w = dict(F=512, before=before, br=None, b1=None, b2=None)
            w["Wr"] = load("F3Wr", [P, 8], a["F3_Wr"], l)
            w["W1"] = load("F3W1", None, a["F3_W1"], l, early[:, 0:4096], 1)
            w["W2"] = load("F3W2", None, a["F3_W2"], l, early[:, 4096:8192], 1)
            w["loaded"] = l + before_l
            W[7] = w
        start_block(c, weights, masks)
        if 0 in stages:
            attention(c, 0, W[0], c.gates_t[:, 0:1], window=64)
            c.end_sublayer()
        if 1 in stages:
            w = W[1]
            ffn(c, 0, w, c.gates_t[:, 4:5], 8, 2, ACT.Silu, "experts", double=(w["ln1"][:, 0:1], w["ln1"][:, 1:2]))
            c.end_sublayer()
        if 2 in stages:
            wide_attention(c, W[2], late[1], c.gates_t[:, 1:2])
            c.end_sublayer()
        if 3 in stages:
            ternary_ffn(c, W[3], c.gates_t[:, 5:6])
            c.end_sublayer()
        if 4 in stages:
            attention(c, 2, W[4], c.gates_t[:, 2:3], rope=True, next_loads=late[3])
            c.end_sublayer()
        if 5 in stages:
            ffn(c, 2, W[5], c.gates_t[:, 6:7], 8, 1, ACT.Gelu, "first")
            c.end_sublayer()
        if 6 in stages:
            attention(c, 3, W[6], c.gates_t[:, 3:4], window=64)
            c.end_sublayer()
        if 7 in stages:
            ffn(c, 3, W[7], c.gates_t[:, 7:8], 8, 1, ACT.Gelu_apprx_tanh, "four", store=(out, stored))


def feature_first(w):
    return w.reshape(*w.shape[:-1], 2, HU, DH).swapaxes(-1, -2).reshape(w.shape)


def layout(i):
    o = {}
    tiles = lambda x: np.ascontiguousarray(x.reshape(NT, P, D).transpose(1, 0, 2))
    o["x"] = tiles(i["x"])
    o["ctxT"] = i["ctx_1024"].reshape(B * S, D).T
    o["g_xattn"], o["g_ffn"] = i["g_xattn"], i["g_ffn"]
    o["L0_WqT"] = feature_first(i["L0_xattn_Wq"].T)
    o["L0_WkT"] = feature_first(i["L0_xattn_Wk"].T)
    o["L0_WvT"] = i["L0_xattn_Wv"].T
    o["L0_WoT"] = i["L0_xattn_Wo"].T
    o["L0_bq"] = feature_first(i["L0_xattn_bq"])
    o["L0_bk"] = feature_first(i["L0_xattn_bk"])
    o["L0_bv"], o["L0_bo"] = i["L0_xattn_bv"], i["L0_xattn_bo"]
    f_tiles = lambda v, F: np.pad(v, [(0, 0), (0, -F % P)] + [(0, 0)] * (v.ndim - 2))
    for L, p, F in ((0, "L0_ffn_", 341), (2, "L2_ffn_", 512), (3, "L3_ffn_", 512)):
        n = {0: ("Wr", "W_up", "W_down"), 2: ("Wr", "W1", "W2"), 3: ("router_w", "up_w", "down_w")}[L]
        wr, w1, w2 = (i[p + k] for k in n)
        o[f"F{L}_Wr"] = wr
        o[f"F{L}_W1"] = np.pad(w1.transpose(1, 0, 2), [(0, 0), (0, 0), (0, -F % P)]).reshape(D, -1)
        w2 = f_tiles(w2, F)
        o[f"F{L}_W2"] = w2.reshape(8, -1, P, D).transpose(2, 0, 1, 3).reshape(P, -1)
    for L, p, F, br, b1, b2 in ((0, "L0_ffn_", 341, "br", "b_up", "b_down"), (2, "L2_ffn_", 512, "br", "b1", "b2")):
        o[f"F{L}_br"] = i[p + br]
        o[f"F{L}_b1"] = f_tiles(i[p + b1], F).reshape(-1, P).T
        o[f"F{L}_b2"] = i[p + b2]
    o["L1_Wq"], o["L1_Wkv"] = i["L1_xattn_w_q"], i["L1_xattn_w_kv"]
    o["L1_Wo"] = i["L1_xattn_w_out"].reshape(8, P, D).transpose(1, 0, 2).reshape(P, -1)
    o["L1_bo"], o["L1_gate"] = i["L1_xattn_b_out"], i["L1_xattn_gate"]
    o["F1_WfT"] = i["L1_ffn_W_fc"].T
    o["F1_WpT"] = i["L1_ffn_W_proj"].T.reshape(4, P, D).transpose(1, 0, 2).reshape(P, -1)
    o["F1_lnw"] = i["L1_ffn_ln_w"].reshape(4, P).T
    o["F1_lnb"] = i["L1_ffn_ln_b"].reshape(4, P).T
    turned = lambda w: np.stack([w[..., 1::2], w[..., 0::2]], -1).reshape(w.shape)
    o["L2_WqT"] = feature_first(i["L2_xattn_Wq"].T)
    o["L2_WkT"] = feature_first(i["L2_xattn_Wk"].T)
    o["L2_WkTs"] = feature_first(turned(i["L2_xattn_Wk"].T))
    o["L2_WvT"] = i["L2_xattn_Wv"].T
    o["L2_WvTs"] = turned(i["L2_xattn_Wv"].T)
    o["L2_WoT"], o["L2_bo"] = i["L2_xattn_Wp"].T, i["L2_xattn_bp"]
    half = D // 2
    theta = (1.0 / np.float32(10000.0) ** (np.float32(2.0) * np.arange(half, dtype=np.float32) / np.float32(D))).astype(np.float32)
    ang = np.arange(S, dtype=np.float32)[:, None] * theta[None, :]
    cos, sin = (np.repeat(f(ang), 2, axis=1).astype(np.float32) for f in (np.cos, np.sin))
    sin[:, 0::2] *= np.float32(-1.0)
    o["rope_cosT"], o["rope_sinT"] = feature_first(cos).T, feature_first(sin).T
    o["rope_cs"] = np.stack([cos, sin]).reshape(2, TPB, P, D).transpose(2, 0, 1, 3)
    eye = np.eye(P, dtype=np.float32)
    o["L3_WqT"], o["L3_WvT"] = feature_first(eye), eye
    o["L3_WoT"], o["L3_bo"] = i["L3_xattn_W_proj"].T, i["L3_xattn_b_proj"]
    e = np.arange(P) % 8
    t = np.arange(P) // 8
    o["same_expert"] = (e[:, None] == e[None, :]).astype(np.float32)
    o["earlier_tile"] = ((e[:, None] == e[None, :]) & (t[:, None] < t[None, :])).astype(np.float32)
    o["before"] = (np.arange(8)[None, :] < np.arange(8)[:, None]).astype(np.float32).reshape(-1)
    o["L1_ln"] = np.stack([i["L1_xattn_ln_gamma"], i["L1_xattn_ln_beta"]], 1)
    return {k: np.ascontiguousarray(v) for k, v in o.items()}


def kernel(**inputs):
    import concourse.bacc as bacc
    from concourse.bass_utils import run_bass_kernel_spmd

    arrays = layout({k: np.asarray(v) for k, v in inputs.items()})
    nc = bacc.Bacc("TRN2", target_bir_lowering=False, num_devices=1)
    aps = {k: nc.dram_tensor("in_" + k, v.shape, F32, kind="ExternalInput").ap() for k, v in arrays.items()}
    out = nc.dram_tensor("out", (P, NT, D), F32, kind="ExternalOutput").ap()
    program(nc, aps, out)
    r = run_bass_kernel_spmd(nc, [{"in_" + k: v for k, v in arrays.items()}], core_ids=[0])
    y = r.results[0]["out"]
    return np.ascontiguousarray(y.transpose(1, 0, 2)).reshape(B, S, D)
```

```python
import numpy as np
import concourse.bass as bass
from concourse import mybir
from contextlib import ExitStack

F32 = mybir.dt.float32
F32R = mybir.dt.float32r
BF16 = mybir.dt.bfloat16
I32 = mybir.dt.int32
ALU = mybir.AluOpType
ACT = mybir.ActivationFunctionType
AX = mybir.AxisListType

P = 128
B, S, D = 8, 256, 128
TPB = S // P
NT = B * TPB
H = 16
DH = D // H
HU = H // 2
WINDOW = 64
INNER = 1024
E = 8
F = 512
F0 = 8 * D // 3
GROUP0 = 2
CAPACITY = B * S // E
RING = 4
PROBS = 6
NEG = -1e30
LN_EPS = 1e-5


class Chip:

    def __init__(self, nc, ctx, arrays):
        self.nc, self.ctx, self.a = nc, ctx, arrays
        self.sublayer_sems, self.spent_sems = [], []
        sb = self.sb
        self.x = sb("x_res", [P, NT, D])
        self.xnT = sb("xnT", [P, NT, P])
        self.ident = sb("ident", [P, P])
        self.identb = sb("identb", [P, P], BF16)
        self.ones = sb("ones", [P, P])
        self.zrow = sb("zrow", [2, S])
        self.mhalf = sb("mhalf", [P, NT])
        self.gates_t = sb("gates_t", [P, 8])
        self.banks = [ctx.enter_context(nc.psum_tensor(f"bank{i}", [P, 512], F32)) for i in range(8)]

    def sb(self, name, shape, dt=F32):
        return self.ctx.enter_context(self.nc.sbuf_tensor(name, shape, dt))

    def sem(self, name):
        return self.ctx.enter_context(self.nc.semaphore(name))

    def sublayer_sem(self, name):
        s = self.nc.alloc_semaphore(name)
        self.sublayer_sems.append(s)
        return s

    def end_sublayer(self):
        for s in self.spent_sems:
            self.nc.release_semaphore(s)
        self.spent_sems, self.sublayer_sems = self.sublayer_sems, []

    def clear_spent(self, g):
        for s in self.spent_sems:
            g.sem_clear(s)


def need(eng, sem, value):
    if value > 0:
        eng.wait_ge(sem, value)


def row(v):
    return v.rearrange("(a n) -> a n", a=1)


def col(v):
    return v.rearrange("(n a) -> n a", a=1)


def start_block(c, weights, mask):
    nc, a = c.nc, c.a
    CH = 4
    NC = NT // CH
    x_in = [c.sem(f"x_loaded{q}") for q in range(NC)]
    const, gate_in, gate_t, made = (c.sem(s) for s in ("consts_ready", "gates_loaded", "gates_ready", "mask_made"))
    stats, rstd_ready, xn_ready, xT_ready, xnT_ready = (
        c.sem(s) for s in ("ln0_stats", "ln0_rstd", "ln0_xn", "ln0_xT", "ln0_xnT"))
    with ExitStack() as own:
        sb = lambda n, s: own.enter_context(nc.sbuf_tensor(n, s, F32))
        st = sb("ln0_st", [P, NT, 6])
        mv = sb("ln0_mv", [P, NT, 2])
        rstd = sb("ln0_rstd_t", [P, NT])
        ve = sb("ln0_ve", [P, NT])
        xn = sb("ln0_xn_t", [P, 2, 4, D])
        with nc.Block() as block:
            @block.sync
            def _(sp):
                for q in range(NC):
                    sp.dma_start(c.x[:, CH * q:CH * (q + 1), :], a["x"][:, CH * q:CH * (q + 1), :]).then_inc(x_in[q], 16)
                sp.dma_start(c.gates_t[:, 0:4], a["g_xattn"].partition_broadcast(P)).then_inc(gate_in, 16)
                sp.dma_start(c.gates_t[:, 4:8], a["g_ffn"].partition_broadcast(P)).then_inc(gate_in, 16)
                for sem, dst, src in weights:
                    sp.dma_start(dst, src).then_inc(sem, 16)

            @block.gpsimd
            def _(g):
                g.memset(c.ones[:], 1.0).then_inc(const, 1)
                g.memset(c.mhalf[:], -0.5).then_inc(const, 1)
                g.memset(c.zrow[:], 0.0).then_inc(const, 1)
                g.wait_ge(const, 3)
                g.affine_select(out=c.ident[:], in_=c.ones[:], compare_op=ALU.is_equal, fill=0.0, base=0,
                                pattern=[[-1, P]], channel_multiplier=1).then_inc(const, 1)
                g.wait_ge(const, 4)
                g.tensor_copy(c.identb[:], c.ident[:]).then_inc(const, 1)
                for q in range(NC):
                    part = slice(CH * q, CH * (q + 1))
                    g.wait_ge(stats, 2 * CH * (q + 1))
                    g.tensor_scalar(ve[:, part], mv[:, part, 1], LN_EPS, None, ALU.add).then_inc(rstd_ready, 1)
                    g.wait_ge(rstd_ready, 2 * q + 1)
                    g.tensor_tensor(rstd[:, part], ve[:, part], c.mhalf[:, part], ALU.pow).then_inc(rstd_ready, 1)
                    if q == 1:
                        draw_mask(g, mask, WINDOW, made)

            @block.scalar
            def _(act):
                act.wait_ge(gate_in, 32)
                act.activation(c.gates_t[:], c.gates_t[:], ACT.Tanh).then_inc(gate_t, 1)
                for q in range(4):
                    act.wait_ge(xT_ready, q + 1)
                    act.copy(c.xnT[:, 4 * q:4 * q + 4, :], c.banks[q][:, :]).then_inc(xnT_ready, 1)

            @block.vector
            def _(v):
                def statistics(q):
                    v.wait_ge(x_in[q], 16)
                    for t in range(CH * q, CH * (q + 1)):
                        v.bn_stats(st[:, t, :], c.x[:, t, :]).then_inc(stats, 1)
                    v.wait_ge(stats, CH * (2 * q + 1))
                    for t in range(CH * q, CH * (q + 1)):
                        v.bn_aggr(mv[:, t, :], st[:, t, :]).then_inc(stats, 1)

                def normalise(q):
                    v.wait_ge(stats, 2 * CH * (q + 1))
                    v.wait_ge(rstd_ready, 2 * (q + 1))
                    if q >= 2:
                        v.wait_ge(xT_ready, q - 1)
                    for t in range(CH * q, CH * (q + 1)):
                        v.tensor_scalar(xn[:, q % 2, t % CH, :], c.x[:, t, :], mv[:, t, 0:1], rstd[:, t:t + 1],
                                        ALU.subtract, ALU.mult).then_inc(xn_ready, 1)

                for q in range(NC + 1):
                    if q < NC:
                        statistics(q)
                    if q >= 1:
                        normalise(q - 1)

            @block.tensor
            def _(pe):
                pe.wait_ge(const, 4)
                for q in range(4):
                    pe.wait_ge(xn_ready, 4 * q + 4)
                    for t in range(4):
                        m = pe.transpose(c.banks[q][:, t * P:(t + 1) * P], xn[:, q % 2, t, :], c.ident[:])
                    m.then_inc(xT_ready, 1)


def attention(c, L, w, gate, window=0, rope=False, next_loads=()):
    nc = c.nc
    W = P + window if window else S
    lo = [0, S - W]
    scale = float(1.0 / np.sqrt(DH))
    NPS, TPS, PA, PB, OPB, MISC = c.banks[0:2], c.banks[2:4], c.banks[4], c.banks[5], c.banks[6], c.banks[7]
    U = 2 * B
    SHIFT_ROW = 3 * DH
    stack_loads = lambda u: 16 * (7 * (u // 2 + 1) - min(u // 2 + 1, RING // 2))
    pre = f"L{L}_"
    sem = lambda n: c.sublayer_sem(pre + n)
    (ct_in0, ct_in1, proj_q, proj_v, split_q, va_ready, stacked0, stacked1, n_ready, max_ready, shT_ready, sh_ready,
     shifted, t_ready, p_ready, pv_ready, o_ready, trT_ready, rc_ready, cn_ready, cnT_ready, cnT_copied,
     po_ready, resid, st_ready, mv_ready, rstd_ready, xn_ready, xT_ready, xnT_ready, zeroed, kf_ready, k_turned,
     v_turned) = (
        sem(n) for n in (
            "ctx_loaded0", "ctx_loaded1", "qk_projected", "v_projected", "qk_split", "v_ready", "stacked0",
            "stacked1", "scores_ready", "max_ready", "maxT_ready", "shift_ready", "shift_stacked",
            "scoresT_ready", "probs_ready", "pv_ready", "ctx_copied", "ctx_turned", "recip_ready", "ctx_normed",
            "ctxT_ready", "ctxT_copied", "out_ready", "resid_ready", "ln_stats", "ln_mv", "ln_rstd", "ln_xn",
            "ln_xT", "ln_xnT", "zeroed", "k_roped", "k_turned", "v_turned"))
    ct_in, stacked = [ct_in0, ct_in1], [stacked0, stacked1]
    with ExitStack() as own:
        sb = lambda n, s, d=F32: own.enter_context(nc.sbuf_tensor(pre + n, s, d))
        ct = sb("ct", [P, 2, S])
        parts = sb("parts", [P, 4, S], F32R)
        kf = sb("kf", [P, 3, S]) if rope else None
        vt = sb("vt", [P, 2, TPB, D]) if rope else None
        QS = sb("q_stack", [P, RING, HU, S], F32R)
        KS = sb("k_stack", [P, RING, HU, S], F32R)
        q_cleared, k_cleared = sem("q_stack_cleared"), sem("k_stack_cleared")
        va = sb("va", [P, 3, TPB, H, 32])
        mx = sb("mx", [P, 2, HU, TPB])
        sh = sb("sh", [HU, 2, 2, S], F32R)
        pt = sb("pt", [P, PROBS, TPB, S])
        os_ = sb("os", [P, 2, S])
        rc = sb("rc", [P, 2, TPB, 4])
        cn = sb("cn", [P, TPB, D])
        cnT = sb("cnT", [P, S])
        st = sb("st", [P, TPB, 6])
        mv = sb("mv", [P, TPB, 2])
        ve = sb("ve", [P, TPB])
        rstd = sb("rstd", [P, TPB])
        xn = sb("xn", [P, TPB, D])

        with nc.Block() as block:
            @block.sync
            def _(sp):
                def load_ctx(b):
                    if b >= 2:
                        sp.wait_ge(proj_v, b - 1)
                    sp.dma_start(ct[:, b % 2, :], c.a["ctxT"][:, b * S:(b + 1) * S]).then_inc(ct_in[b % 2], 16)

                def stack(u):
                    b, hf, r = u // 2, u % 2, u % RING
                    sp.wait_ge(split_q, 4 * (b + 1))
                    need(sp, t_ready, (u - RING + 1) * HU)
                    if u < RING:
                        sp.wait_ge(q_cleared, u + 1)
                        sp.wait_ge(k_cleared, u + 1)
                    for term, (qp, kp) in enumerate(((0, 2), (1, 2), (0, 3))):
                        for dst, part in ((QS, qp), (KS, kp)):
                            src = parts[hf * 64:hf * 64 + 64, part, :].bitcast(F32)
                            sp.dma_start(dst[DH * term:DH * (term + 1), r, :, :].bitcast(F32),
                                         src).then_inc(stacked[u % 2], 16)
                    if u >= RING:
                        sp.dma_start(QS[SHIFT_ROW:SHIFT_ROW + 2, r, :, :].bitcast(F32),
                                     c.zrow[:].unsqueeze(1).broadcast_to([2, HU, S])).then_inc(stacked[u % 2], 16)

                def shift(u):
                    sp.wait_ge(sh_ready, 2 * (u + 1))
                    sp.wait_ge(n_ready, (u + 1) * HU)
                    for k in range(2):
                        sp.dma_start(QS[SHIFT_ROW + k:SHIFT_ROW + k + 1, u % RING, :, :].bitcast(F32),
                                     sh[:, u % 2, k, :].bitcast(F32)).then_inc(shifted, 16)

                load_ctx(0)
                load_ctx(1)
                stack(0)
                stack(1)
                for t in range(U + 2):
                    if t % 2 == 0 and t // 2 + 2 < B:
                        load_ctx(t // 2 + 2)
                    if t == 0:
                        for s, dst, src in next_loads:
                            sp.dma_start(dst, src).then_inc(s, 16)
                    if t >= 1 and t + 1 < U:
                        stack(t + 1)
                    if t >= 1 and t - 1 < U:
                        shift(t - 1)

            @block.tensor
            def _(pe):
                def project_qk(b):
                    xs = c.xnT[:, TPB * b:TPB * (b + 1), :].rearrange("p t n -> p (t n)")
                    need(pe, split_q, 4 * b)
                    need(pe, sh_ready, 4 * (b - 1))
                    if b >= 1:
                        pe.wait_ge(va_ready, b)
                    pe.wait_ge(ct_in[b % 2], 16 * (b // 2 + 1))
                    pe.matmul(PA[:, 0:S], w["WqT"], xs, start=True, stop=True)
                    m = pe.matmul(PA[:, S:2 * S], w["WkT"], ct[:, b % 2, :], start=True, stop=True)
                    if rope:
                        m = pe.matmul(PB[:, 0:S], w["WkTs"], ct[:, b % 2, :], start=True, stop=True)
                    m.then_inc(proj_q, 1)

                def project_v(b):
                    if rope:
                        pe.wait_ge(k_turned, 2 * b + 2)
                    for t in range(TPB):
                        tok = ct[:, b % 2, t * P:(t + 1) * P]
                        m = pe.matmul(PB[:, t * D:(t + 1) * D], tok, w["WvT"], start=True, stop=True)
                        if rope:
                            m = pe.matmul(PB[:, (2 + t) * D:(3 + t) * D], tok, w["WvTs"], start=True, stop=True)
                    m.then_inc(proj_v, 1)

                def put_mask(bank):
                    pe.matmul(bank[:, 0:TPB * W], c.identb[:], w["mask"][:].rearrange("p t n -> p (t n)"),
                              start=True, stop=False, skip_group_check=True)

                def scores(u, h):
                    n, r = u * HU + h, u % RING
                    need(pe, max_ready, n - 1)
                    if h == 0:
                        pe.wait_ge(stacked[u % 2], stack_loads(u))
                    if window:
                        put_mask(NPS[n % 2])
                    for t in range(TPB):
                        m = pe.matmul(NPS[n % 2][:, t * W:(t + 1) * W], QS[:, r, h, t * P:(t + 1) * P],
                                      KS[:, r, h, lo[t]:lo[t] + W], start=not window, stop=True,
                                      skip_group_check=bool(window))
                    m.then_inc(n_ready, 1)

                def scores_t(u, h):
                    n, r = u * HU + h, u % RING
                    need(pe, p_ready, n - 1)
                    if h == 0:
                        pe.wait_ge(shifted, 32 * (u + 1))
                    if window:
                        put_mask(TPS[n % 2])
                    for t in range(TPB):
                        m = pe.matmul(TPS[n % 2][:, t * W:(t + 1) * W], KS[:, r, h, t * P:(t + 1) * P],
                                      QS[:, r, h, lo[t]:lo[t] + W], start=not window, stop=True,
                                      skip_group_check=bool(window))
                    m.then_inc(t_ready, 1)

                def pv(u, g):
                    G = 2 * u + g
                    pe.wait_ge(p_ready, 4 * (G + 1))
                    need(pe, o_ready, G)
                    pe.wait_ge(va_ready, u // 2 + 1)
                    for t in range(TPB):
                        for j in range(4):
                            n = 4 * G + j
                            h = n % H
                            m = pe.matmul(OPB[32 * j:32 * j + 32, lo[t]:lo[t] + W], va[:, u // 2 % 3, t, h, :],
                                          pt[:, n % PROBS, t, 0:W], start=(t == 0), stop=(t == 1),
                                          skip_group_check=bool(window))
                    m.then_inc(pv_ready, 1)

                def turn_max(u):
                    pe.wait_ge(max_ready, (u + 1) * HU)
                    pe.wait_ge(va_ready, min(B, (u + 1) // 2 + 1 + (u + 1) % 2))
                    for t in range(TPB):
                        m = pe.transpose(PB[0:HU, t * P:(t + 1) * P], mx[:, u % 2, :, t], c.ident[:])
                    m.then_inc(shT_ready, 1)

                def turn_ctx(u, g):
                    G = 2 * u + g
                    pe.wait_ge(o_ready, G + 1)
                    need(pe, cn_ready, G)
                    for t in range(TPB):
                        m = pe.transpose(MISC[:, t * P:(t + 1) * P], os_[:, G % 2, t * P:(t + 1) * P], c.ident[:])
                    m.then_inc(trT_ready, 1)

                def turn_normed(b):
                    pe.wait_ge(cn_ready, 4 * (b + 1))
                    for t in range(TPB):
                        m = pe.transpose(MISC[:, t * P:(t + 1) * P], cn[:, t, :], c.ident[:])
                    m.then_inc(cnT_ready, 1)

                def out(b):
                    pe.wait_ge(cnT_copied, b + 1)
                    for t in range(TPB):
                        pe.matmul(MISC[:, t * D:(t + 1) * D], cnT[:, t * P:(t + 1) * P], w["WoT"],
                                  start=True, stop=False)
                        m = pe.matmul(MISC[:, t * D:(t + 1) * D], c.ones[0:1, :], w["bo"], start=False, stop=True)
                    m.then_inc(po_ready, 1)

                def turn_ln(b):
                    pe.wait_ge(xn_ready, 2 * (b + 1))
                    for t in range(TPB):
                        m = pe.transpose(MISC[:, t * P:(t + 1) * P], xn[:, t, :], c.ident[:])
                    m.then_inc(xT_ready, 1)

                for s, all_loads in w["loaded"]:
                    pe.wait_ge(s, all_loads)
                project_qk(0)
                project_v(0)
                for t in range(U + 6):
                    N, T, T3 = t < U, 0 <= t - 2 < U, 0 <= t - 3 < U
                    b4, b5 = (t - 4) // 2, (t - 5) // 2
                    for h in range(HU):
                        if N:
                            scores(t, h)
                        if T:
                            scores_t(t - 2, h)
                        if h == 1:
                            if 0 <= t - 1 < U:
                                turn_max(t - 1)
                            if T3:
                                pv(t - 3, 1)
                        if h == 2 and t % 2 == 1 and 0 <= b5 < B:
                            pe.wait_ge(cn_ready, min(2 * t - 5, 2 * U))
                            turn_ln(b5)
                        if h == 3 and T3:
                            if t % 2 == 1 and b5 >= 0:
                                pe.wait_ge(xnT_ready, b5 + 1)
                            turn_ctx(t - 3, 1)
                        if h == 4 and t % 2 == 0 and 0 <= b4 < B:
                            turn_normed(b4)
                        if h == 5 and T:
                            pv(t - 2, 0)
                        if h == 5 and t % 2 == 0 and t // 2 + 1 < B:
                            project_qk(t // 2 + 1)
                        if h == 6 and t % 2 == 0 and 0 <= b4 < B:
                            out(b4)
                        if h == 7 and t % 2 == 0 and t // 2 + 1 < B:
                            project_v(t // 2 + 1)
                        if h == 7 and T:
                            if t % 2 == 0 and b4 >= 0:
                                pe.wait_ge(resid, b4 + 1)
                            if t % 2 == 1:
                                need(pe, cn_ready, 2 * (t - 3) + 2)
                            turn_ctx(t - 2, 0)

            @block.scalar
            def _(act):
                def split_q_high(b):
                    act.wait_ge(proj_q, b + 1)
                    if b >= 1:
                        act.wait_ge(stacked[0], stack_loads(2 * b - 2))
                        act.wait_ge(stacked[1], stack_loads(2 * b - 1))
                    act.activation(parts[:, 0, :], PA[:, 0:S], ACT.Identity, bias=w["bq"]).then_inc(split_q, 1)

                def split_k_high(b):
                    if rope:
                        act.wait_ge(kf_ready, b + 1)
                        act.copy(parts[:, 2, :], kf[:, 2, :]).then_inc(split_q, 1)
                    else:
                        act.activation(parts[:, 2, :], PA[:, S:2 * S], ACT.Identity, bias=w["bk"]).then_inc(split_q, 1)

                def exps(u, h):
                    n = u * HU + h
                    act.wait_ge(t_ready, n + 1)
                    need(act, pv_ready, (n - PROBS) // 4 + 1)
                    src = TPS[n % 2][:, 0:TPB * W]
                    if window:
                        src = src.rearrange("p (t n) -> p t n", t=TPB)
                    else:
                        src = src.rearrange("p (t n) -> p t n", t=TPB)
                    act.activation(pt[:, n % PROBS, :, 0:W], src, ACT.Exp, scale=scale).then_inc(p_ready, 1)

                def copy_ctx(u, g):
                    G = 2 * u + g
                    act.wait_ge(pv_ready, G + 1)
                    need(act, trT_ready, G - 1)
                    act.copy(os_[:, G % 2, :], OPB[:, 0:S]).then_inc(o_ready, 1)

                def copy_normed(b):
                    act.wait_ge(cnT_ready, b + 1)
                    need(act, po_ready, b)
                    act.copy(cnT[:], MISC[:, 0:S]).then_inc(cnT_copied, 1)

                def copy_ln(b):
                    act.wait_ge(xT_ready, b + 1)
                    act.copy(c.xnT[:, TPB * b:TPB * (b + 1), :].rearrange("p t n -> p (t n)"),
                             MISC[:, 0:S]).then_inc(xnT_ready, 1)

                for s, all_loads in w["loaded"]:
                    act.wait_ge(s, all_loads)
                split_q_high(0)
                split_k_high(0)
                for t in range(U + 6):
                    T, T3 = 0 <= t - 2 < U, 0 <= t - 3 < U
                    b4, b5 = (t - 4) // 2, (t - 5) // 2
                    for h in range(HU):
                        if T:
                            exps(t - 2, h)
                        if h == 1 and T3:
                            copy_ctx(t - 3, 1)
                        if h == 2 and t % 2 == 1 and 0 <= b5 < B:
                            copy_ln(b5)
                        if h == 4 and t % 2 == 0 and 0 <= b4 < B:
                            copy_normed(b4)
                        if h == 5 and t % 2 == 0 and t // 2 + 1 < B:
                            split_q_high(t // 2 + 1)
                        if h == 6 and t % 2 == 0 and t // 2 + 1 < B:
                            split_k_high(t // 2 + 1)
                        if h == 5 and T:
                            copy_ctx(t - 2, 0)

            @block.gpsimd
            def _(g):
                c.clear_spent(g)
                g.memset(QS[:, 0].bitcast(F32), 0.0).then_inc(q_cleared, 1)
                g.memset(va[:], 1.0).then_inc(zeroed, 1)
                for r in range(1, RING):
                    g.memset(QS[:, r].bitcast(F32), 0.0).then_inc(q_cleared, 1)
                for b in range(B):
                    g.wait_ge(mv_ready, 2 * (b + 1))
                    g.tensor_scalar(ve[:], mv[:, :, 1], LN_EPS, None, ALU.add).then_inc(rstd_ready, 1)
                    g.wait_ge(rstd_ready, 2 * b + 1)
                    g.tensor_tensor(rstd[:], ve[:], c.mhalf[:, 0:TPB], ALU.pow).then_inc(rstd_ready, 1)

            @block.vector
            def _(v):
                v3 = lambda ap: ap.rearrange("p (t h d) -> p t h d", t=TPB, h=H)

                def split_low(b):
                    v.wait_ge(proj_q, b + 1)
                    if rope:
                        v.wait_ge(split_q, 4 * b + 1)
                        v.tensor_tensor(kf[:, 0, :], PA[:, S:2 * S], w["cosT"], ALU.mult).then_inc(k_turned, 1)
                        v.tensor_tensor(kf[:, 1, :], PB[:, 0:S], w["sinT"], ALU.mult).then_inc(k_turned, 1)
                        v.wait_ge(k_turned, 2 * b + 2)
                        if b >= 1:
                            v.wait_ge(split_q, 4 * b)
                        v.tensor_tensor(kf[:, 2, :], kf[:, 0, :], kf[:, 1, :], ALU.add).then_inc(kf_ready, 1)
                    v.wait_ge(split_q, 4 * b + 2)
                    v.scalar_tensor_tensor(parts[:, 1, :], PA[:, 0:S], w["bq"], parts[:, 0, :].bitcast(F32),
                                           ALU.add, ALU.subtract).then_inc(split_q, 1)
                    if rope:
                        v.wait_ge(kf_ready, b + 1)
                        v.tensor_tensor(parts[:, 3, :], kf[:, 2, :], parts[:, 2, :].bitcast(F32),
                                        ALU.subtract).then_inc(split_q, 1)
                    else:
                        v.scalar_tensor_tensor(parts[:, 3, :], PA[:, S:2 * S], w["bk"],
                                               parts[:, 2, :].bitcast(F32), ALU.add, ALU.subtract).then_inc(split_q, 1)

                def place_v(b):
                    v.wait_ge(proj_v, b + 1)
                    if b == 0:
                        v.wait_ge(zeroed, 1)
                    need(v, pv_ready, 4 * (b - 2))
                    dst = va[:, b % 3, :, :, 0:DH]
                    if rope:
                        src = PB[:, :].rearrange("p (s t d) -> p s t d", s=2, t=TPB)
                        for s in range(2):
                            v.tensor_tensor(vt[:, s], src[:, s], w["cs"][:, s], ALU.mult).then_inc(v_turned, 1)
                        v.wait_ge(v_turned, 2 * b + 2)
                        x3 = lambda s: vt[:, s].rearrange("p t (h d) -> p t h d", h=H)
                        for t in range(TPB):
                            i = v.tensor_tensor(dst[:, t], x3(0)[:, t], x3(1)[:, t], ALU.add)
                        i.then_inc(va_ready, 1)
                    else:
                        for t in range(TPB):
                            if w["bv"] is None:
                                i = v.tensor_copy(dst[:, t], v3(PB[:, 0:S])[:, t])
                            else:
                                i = v.tensor_tensor(dst[:, t], v3(PB[:, 0:S])[:, t],
                                                    w["bv"].rearrange("p (h d) -> p h d", h=H), ALU.add)
                        i.then_inc(va_ready, 1)

                def maxima(u, h):
                    n = u * HU + h
                    v.wait_ge(n_ready, n + 1)
                    if h == 0:
                        need(v, shT_ready, u - 1)
                    v.tensor_reduce(mx[:, u % 2, h, :], NPS[n % 2][:, 0:TPB * W].rearrange("p (t n) -> p t n", t=TPB),
                                    AX.X, ALU.max).then_inc(max_ready, 1)

                def shift(u):
                    v.wait_ge(shT_ready, u + 1)
                    need(v, shifted, 32 * (u - 1))
                    v.tensor_scalar(sh[:, u % 2, 0, :], PB[0:HU, 0:S], -1.0, None, ALU.mult).then_inc(sh_ready, 1)
                    v.wait_ge(sh_ready, 2 * u + 1)
                    v.scalar_tensor_tensor(sh[:, u % 2, 1, :], PB[0:HU, 0:S], -1.0,
                                           sh[:, u % 2, 0, :].bitcast(F32), ALU.mult, ALU.subtract).then_inc(sh_ready, 1)

                def norm_ctx(u, g):
                    G = 2 * u + g
                    v.wait_ge(trT_ready, G + 1)
                    o4 = MISC[:, 0:S].rearrange("p (t j k) -> p t j k", t=TPB, j=4)
                    need(v, cn_ready, G - 1)
                    v.reciprocal(rc[:, G % 2], o4[:, :, :, DH]).then_inc(rc_ready, 1)
                    v.wait_ge(rc_ready, G + 1)
                    if G % 4 == 0:
                        need(v, cnT_ready, G // 4)
                    h0 = 4 * G % H
                    for t in range(TPB):
                        i = v.tensor_tensor(cn[:, t, h0 * DH:(h0 + 4) * DH].rearrange("p (j d) -> p j d", j=4),
                                            o4[:, t, :, 0:DH],
                                            rc[:, G % 2, t, :].rearrange("p (j a) -> p j a", a=1).broadcast_to([P, 4, DH]),
                                            ALU.mult)
                    i.then_inc(cn_ready, 1)

                def finish(b):
                    v.wait_ge(po_ready, b + 1)
                    xs = c.x[:, TPB * b:TPB * (b + 1), :].rearrange("p t n -> p (t n)")
                    v.scalar_tensor_tensor(xs, MISC[:, 0:S], gate, xs, ALU.mult, ALU.add).then_inc(resid, 1)
                    v.wait_ge(resid, b + 1)
                    for t in range(TPB):
                        v.bn_stats(st[:, t, :], c.x[:, TPB * b + t, :]).then_inc(st_ready, 1)
                    v.wait_ge(st_ready, 2 * (b + 1))
                    for t in range(TPB):
                        v.bn_aggr(mv[:, t, :], st[:, t, :]).then_inc(mv_ready, 1)

                def normalise(b):
                    v.wait_ge(mv_ready, 2 * (b + 1))
                    v.wait_ge(rstd_ready, 2 * (b + 1))
                    need(v, xT_ready, b)
                    for t in range(TPB):
                        v.tensor_scalar(xn[:, t, :], c.x[:, TPB * b + t, :], mv[:, t, 0:1], rstd[:, t:t + 1],
                                        ALU.subtract, ALU.mult).then_inc(xn_ready, 1)

                v.memset(KS[:, 0].bitcast(F32), 1.0).then_inc(k_cleared, 1)
                for s, all_loads in w["loaded"]:
                    v.wait_ge(s, all_loads)
                split_low(0)
                place_v(0)
                for r in range(1, RING):
                    v.memset(KS[:, r].bitcast(F32), 1.0).then_inc(k_cleared, 1)
                for t in range(U + 6):
                    N, T, T3 = t < U, 0 <= t - 2 < U, 0 <= t - 3 < U
                    b4, b5 = (t - 4) // 2, (t - 5) // 2
                    for h in range(HU):
                        if h == 0 and t % 2 == 1 and 0 <= b5 < B:
                            normalise(b5)
                        if N:
                            maxima(t, h)
                        if h == 1 and 0 <= t - 1 < U:
                            shift(t - 1)
                        if h == 3 and T3:
                            norm_ctx(t - 3, 1)
                        if h == 6 and t % 2 == 0 and t // 2 + 1 < B:
                            split_low(t // 2 + 1)
                        if h == 7 and t % 2 == 0 and t // 2 + 1 < B:
                            place_v(t // 2 + 1)
                        if h == 6 and t % 2 == 0 and 0 <= b4 < B:
                            finish(b4)
                        if h == 7 and T:
                            norm_ctx(t - 2, 0)


def layer_norm_tail(c, own, pre):
    nc = c.nc
    sb = lambda n, s, d=F32: own.enter_context(nc.sbuf_tensor(pre + n, s, d))
    return dict(st=sb("st", [P, 4, 6]), mv=sb("mv", [P, 4, 2]), ve=sb("ve", [P, 4]), rstd=sb("rstd", [P, 4]),
                xn=sb("xn", [P, 4, D]))


def ffn(c, L, w, F, tgate, per_group, act_f, rule, double=None, store=None):
    nc = c.nc
    FT = (F + P - 1) // P
    FP = FT * P
    AHEAD = 10 if rule == "experts" else 1
    HR = AHEAD + 1
    CH = 4
    NC = NT // CH
    groups = E // per_group
    K = [(q, g) for q in range(NC) for g in range(groups)]
    UB, YB, GB, LB = c.banks[0:4], c.banks[4:6], c.banks[6], c.banks[7]
    pre = f"F{L}_"
    sem = lambda n: c.sublayer_sem(pre + n)
    (cleared, xn1_ready) = (sem("search_cleared"), sem("ln_xn1"))
    (wh_ready, wl_ready, xh_ready, xl_ready) = (sem(n) for n in ("w1_high", "w1_low", "x_high", "x_low"))
    (lg_ready, step, search_step, exp_done, pe_step, gates_ready, up_ready, h_ready, y_ready, added, gT_ready,
     gT_copied, bias_ready, bias_added, st_ready, mv_ready, rstd_ready, xn_ready, xT_ready, xnT_ready) = (sem(n) for n in (
         "logits_ready", "gate_step", "search_step", "gate_exp", "search_pe", "gates_ready", "up_ready", "hidden_ready",
         "down_ready", "added", "gatesT_ready", "gatesT_copied", "bias_ready", "bias_added", "ln_stats", "ln_mv",
         "ln_rstd", "ln_xn", "ln_xT", "ln_xnT"))
    with ExitStack() as own:
        sb = lambda n, s, d=F32: own.enter_context(nc.sbuf_tensor(pre + n, s, d))
        lg = sb("lg", [P, NT, E])
        pr = sb("pr", [P, NT, E])
        m1 = sb("m1", [P, NT])
        gates = sb("gates", [P, NT, E])
        gT = sb("gT", [E, NT, P])
        ht = sb("ht", [P, HR, FT, CH * P])
        wh = sb("wh", [P, groups * FP], F32R)
        wl = sb("wl", [P, groups * FP], F32R)
        xh = sb("xh", [P, NC, CH * P], F32R)
        xl = sb("xl", [P, NC, CH * P], F32R)
        ln = layer_norm_tail(c, own, pre)
        st, mv, ve, rstd, xn = (ln[k] for k in ("st", "mv", "ve", "rstd", "xn"))
        if rule == "experts":
            pT = sb("pT", [P, P])
            msk = sb("msk", [P, P])
            eq = sb("eq", [P, P])
            cum = sb("cum", [P, P])
            zero = sb("zero", [P, P])
            cand = sb("cand", [P, 1], I32)
            low = sb("low", [P, 1], I32)
            take = sb("take", [P, 1], I32)
            cnt = sb("cnt", [P, 1])
            left = sb("left", [P, 1])
            prf = sb("prf", [P, 1])
        else:
            cmp1 = sb("cmp1", [P, NT, E, E])
            cmp2 = sb("cmp2", [P, NT, E, E])
            rank = sb("rank", [P, NT, E])

        b8 = lambda ap: ap.rearrange("p (t a) -> p t a", a=1).broadcast_to([P, NT, E])
        other = lambda ap: ap.rearrange("p t (a e) -> p t a e", a=1).broadcast_to([P, NT, E, E])
        mine = lambda ap: ap.rearrange("p t (e a) -> p t e a", a=1).broadcast_to([P, NT, E, E])
        BITS = 30
        STEPS_TO_PROBS = 6

        with nc.Block() as block:
            @block.tensor
            def _(pe):
                def up(k, f):
                    q, g = K[k]
                    n = k * FT + f
                    if f == 0:
                        pe.wait_ge(wh_ready, g + 1)
                        pe.wait_ge(wl_ready, g + 1)
                        pe.wait_ge(xh_ready, q + 1)
                        pe.wait_ge(xl_ready, q + 1)
                    need(pe, h_ready, n - 3)
                    cols = slice(g * FP + f * P, g * FP + (f + 1) * P)
                    pe.matmul(UB[n % 4][:, :], wh[:, cols], xh[:, q, :], start=True, stop=False)
                    pe.matmul(UB[n % 4][:, :], wh[:, cols], xl[:, q, :], start=False, stop=False)
                    pe.matmul(UB[n % 4][:, :], wl[:, cols], xh[:, q, :], start=False, stop=True).then_inc(up_ready, 1)

                for s, all_loads in w["loaded"]:
                    pe.wait_ge(s, all_loads)
                for t in range(NT):
                    m = pe.matmul(GB[:, t * E:(t + 1) * E], c.xnT[:, t, :], w["Wr"], start=True, stop=True)
                m.then_inc(lg_ready, 1)
                if rule == "experts":
                    pe.wait_ge(step, STEPS_TO_PROBS)
                    pe.transpose(GB[:, 0:P], pr[:].rearrange("p t e -> p (t e)"), c.ident[:]).then_inc(pe_step, 1)
                    for k in range(BITS + 1):
                        pe.wait_ge(search_step, 2 * k + 1)
                        pe.matmul(LB[:, 0:1], w["same_expert"], cnt[:], start=True, stop=True).then_inc(pe_step, 1)
                        if k < AHEAD * FT:
                            up(k // FT, k % FT)
                    pe.wait_ge(search_step, 2 * BITS + 3)
                    pe.matmul(LB[:, 0:1], w["earlier_tile"], cum[:, P - 1:P], start=True, stop=True).then_inc(pe_step, 1)
                    pe.wait_ge(search_step, 2 * BITS + 4)
                    pe.transpose(GB[:, 0:P], msk[:], c.ident[:]).then_inc(pe_step, 1)

                def down(k, e):
                    q, g = K[k]
                    n = k * per_group + e
                    x = g * per_group + e
                    if e == 0:
                        pe.wait_ge(h_ready, (k + 1) * FT)
                    need(pe, added, 4 * (n - 1))
                    for t in range(CH):
                        for f in range(FT):
                            m = pe.matmul(YB[n % 2][:, t * D:(t + 1) * D], ht[:, k % HR, f, t * P:(t + 1) * P],
                                          w["W2"][:, (x * FT + f) * D:(x * FT + f + 1) * D],
                                          start=(f == 0), stop=(f == FT - 1))
                    m.then_inc(y_ready, 1)

                def biases(q):
                    if q == 0:
                        pe.wait_ge(gates_ready, 1)
                    for t in range(CH):
                        m = pe.transpose(GB[0:E, t * P:(t + 1) * P], gates[:, CH * q + t, :], c.ident[:])
                    m.then_inc(gT_ready, 1)
                    pe.wait_ge(gT_copied, q + 1)
                    need(pe, bias_added, q)
                    for t in range(CH):
                        m = pe.matmul(LB[:, t * D:(t + 1) * D], gT[:, CH * q + t, :], w["b2"], start=True, stop=True)
                    m.then_inc(bias_ready, 1)

                def turn_ln(q):
                    pe.wait_ge(xn_ready, CH * (q + 1))
                    if w["b2"] is not None:
                        pe.wait_ge(bias_added, NC)
                    need(pe, xnT_ready, q)
                    for t in range(CH):
                        m = pe.transpose(LB[:, t * P:(t + 1) * P], xn[:, t, :], c.ident[:])
                    m.then_inc(xT_ready, 1)

                if rule != "experts":
                    for f in range(FT):
                        up(0, f)
                for k in range(len(K)):
                    q, g = K[k]
                    if k + AHEAD < len(K):
                        for f in range(FT):
                            up(k + AHEAD, f)
                    for e in range(per_group):
                        down(k, e)
                        if (k + 1) * per_group == 2 and e == per_group - 1 and w["b2"] is not None:
                            for n in range(NC):
                                biases(n)
                    if g == groups - 2 and q > 0 and not store:
                        turn_ln(q - 1)
                if not store:
                    turn_ln(NC - 1)

            if store:
                @block.sync
                def _(sp):
                    out, stored = store
                    for q in range(NC):
                        part = slice(CH * q, CH * (q + 1))
                        sp.wait_ge(added, CH * E * (q + 1))
                        sp.dma_start(out[:, part, :], c.x[:, part, :]).then_inc(stored, 16)
                    sp.wait_ge(stored, 16 * NC)

            @block.scalar
            def _(act):
                for s, all_loads in w["loaded"]:
                    act.wait_ge(s, all_loads)
                for g in range(groups):
                    act.copy(wh[:, g * FP:(g + 1) * FP], w["W1"][:, g * FP:(g + 1) * FP]).then_inc(wh_ready, 1)
                    if g < NC:
                        act.copy(xh[:, g, :],
                                 c.xnT[:, CH * g:CH * (g + 1), :].rearrange("p t n -> p (t n)")).then_inc(xh_ready, 1)
                act.wait_ge(step, 3)
                act.activation(pr[:], pr[:], ACT.Exp).then_inc(exp_done, 1)

                def hidden(k):
                    q, g = K[k]
                    need(act, y_ready, (k - HR + 1) * per_group)
                    for f in range(FT):
                        n = k * FT + f
                        act.wait_ge(up_ready, n + 1)
                        b = w["b1"][:, g * FT + f:g * FT + f + 1] if w["b1"] is not None else 0.0
                        act.activation(ht[:, k % HR, f, :], UB[n % 4][:, :], act_f, bias=b).then_inc(h_ready, 1)

                for k in range(AHEAD):
                    hidden(k)
                for k in range(len(K)):
                    q, g = K[k]
                    if k + AHEAD < len(K):
                        hidden(k + AHEAD)
                    if g == groups - 1 and q > 0 and not store:
                        copy_ln(c, act, q - 1, xT_ready, xnT_ready, LB, double)
                if not store:
                    copy_ln(c, act, NC - 1, xT_ready, xnT_ready, LB, double)

            @block.gpsimd
            def _(g):
                c.clear_spent(g)
                if rule == "experts":
                    g.memset(zero[:], 0.0).then_inc(cleared, 1)
                    g.memset(low[:], 0).then_inc(cleared, 1)
                for q in range(NC):
                    g.wait_ge(xh_ready, q + 1)
                    g.tensor_tensor(xl[:, q, :], c.xnT[:, CH * q:CH * (q + 1), :].rearrange("p t n -> p (t n)"),
                                    xh[:, q, :].bitcast(F32), ALU.subtract).then_inc(xl_ready, 1)
                rounds = 0 if store else 2 if double else 1
                for n in range(NC * rounds):
                    g.wait_ge(mv_ready, 4 * (n + 1))
                    g.tensor_scalar(ve[:], mv[:, :, 1], LN_EPS, None, ALU.add).then_inc(rstd_ready, 1)
                    g.wait_ge(rstd_ready, 2 * n + 1)
                    g.tensor_tensor(rstd[:], ve[:], c.mhalf[:, 0:4], ALU.pow).then_inc(rstd_ready, 1)

            @block.vector
            def _(v):
                count = [0]

                def chain(i):
                    count[0] += 1
                    i.then_inc(step, 1)
                    v.wait_ge(step, count[0])

                for s, all_loads in w["loaded"]:
                    v.wait_ge(s, all_loads)
                for g in range(groups):
                    v.wait_ge(wh_ready, g + 1)
                    v.tensor_tensor(wl[:, g * FP:(g + 1) * FP], w["W1"][:, g * FP:(g + 1) * FP],
                                    wh[:, g * FP:(g + 1) * FP].bitcast(F32), ALU.subtract).then_inc(wl_ready, 1)
                v.wait_ge(lg_ready, 1)
                l3 = GB[:, 0:NT * E].rearrange("p (t e) -> p t e", e=E)
                if w["br"] is not None:
                    chain(v.tensor_tensor(lg[:], l3, w["br"].rearrange("p (a e) -> p a e", a=1).broadcast_to([P, NT, E]),
                                          ALU.add))
                else:
                    chain(v.tensor_copy(lg[:], l3))
                chain(v.tensor_reduce(m1[:], lg[:], AX.X, ALU.max))
                chain(v.tensor_tensor(pr[:], lg[:], b8(m1[:]), ALU.subtract))
                v.wait_ge(exp_done, 1)
                chain(v.tensor_reduce(m1[:], pr[:], AX.X, ALU.add))
                chain(v.reciprocal(m1[:], m1[:]))
                chain(v.tensor_tensor(pr[:], pr[:], b8(m1[:]), ALU.mult))
                if rule == "experts":
                    assert count[0] == STEPS_TO_PROBS
                    v.wait_ge(pe_step, 1)
                    chain(v.tensor_copy(pT[:], GB[:, 0:P]))
                    v.wait_ge(cleared, 2)
                    chain(v.tensor_single_scalar(cand[:], low[:], 1 << (BITS - 1), ALU.bitwise_or))
                    for k in range(BITS):
                        v.tensor_scalar(msk[:], pT[:], cand[:].bitcast(F32), 0.0, ALU.is_ge, ALU.add,
                                        accum_out=cnt[:]).then_inc(search_step, 1)
                        v.wait_ge(pe_step, k + 2)
                        chain(v.tensor_scalar(take[:], LB[:, 0:1], float(CAPACITY), float(1 << (BITS - 1 - k)),
                                              ALU.is_ge, ALU.mult))
                        if k + 1 < BITS:
                            v.scalar_tensor_tensor(cand[:], take[:], 1 << (BITS - 2 - k), low[:], ALU.bitwise_or,
                                                   ALU.bitwise_or).then_inc(step, 1)
                            count[0] += 1
                        v.tensor_tensor(low[:], take[:], low[:], ALU.bitwise_or).then_inc(search_step, 1)
                        if k + 1 < BITS:
                            v.wait_ge(step, count[0])
                        v.wait_ge(search_step, 2 * k + 2)
                    v.tensor_scalar(msk[:], pT[:], low[:].bitcast(F32), 0.0, ALU.is_gt, ALU.add,
                                    accum_out=cnt[:]).then_inc(search_step, 1)
                    v.wait_ge(search_step, 2 * BITS + 1)
                    v.tensor_scalar(eq[:], pT[:], low[:].bitcast(F32), None, ALU.is_equal).then_inc(search_step, 1)
                    v.wait_ge(search_step, 2 * BITS + 2)
                    v.tensor_tensor_scan(cum[:], eq[:], zero[:], 0.0, ALU.add, ALU.add)
                    v.wait_ge(pe_step, BITS + 2)
                    chain(v.tensor_scalar(left[:], LB[:, 0:1], -1.0, float(CAPACITY), ALU.mult, ALU.add))
                    v.drain().then_inc(search_step, 1)
                    v.wait_ge(pe_step, BITS + 3)
                    chain(v.tensor_copy(prf[:], LB[:, 0:1]))
                    chain(v.tensor_scalar(cum[:], cum[:], prf[:], left[:], ALU.add, ALU.is_le))
                    chain(v.tensor_tensor(eq[:], eq[:], cum[:], ALU.mult))
                    chain(v.tensor_tensor(msk[:], msk[:], eq[:], ALU.add))
                    v.tensor_tensor(msk[:], msk[:], pT[:], ALU.mult).then_inc(search_step, 1)
                    v.wait_ge(pe_step, BITS + 4)
                    v.tensor_scalar(gates[:].rearrange("p t e -> p (t e)"), GB[:, 0:P], tgate, None,
                                    ALU.mult).then_inc(gates_ready, 1)
                else:
                    of = lg if rule == "first" else pr
                    v.tensor_tensor(cmp1[:], other(of[:]), mine(of[:]), ALU.is_gt)
                    chain(v.tensor_tensor(cmp2[:], other(of[:]), mine(of[:]), ALU.is_equal))
                    chain(v.tensor_tensor(cmp2[:].rearrange("p t e f -> p t (e f)"),
                                          cmp2[:].rearrange("p t e f -> p t (e f)"),
                                          w["before"].rearrange("p (a n) -> p a n", a=1).broadcast_to([P, NT, E * E]), ALU.mult))
                    chain(v.tensor_tensor(cmp1[:], cmp1[:], cmp2[:], ALU.add))
                    chain(v.tensor_reduce(rank[:], cmp1[:], AX.X, ALU.add))
                    top = 1.0 if rule == "first" else 4.0
                    chain(v.tensor_single_scalar(rank[:], rank[:], top, ALU.is_lt))
                    chain(v.tensor_tensor(pr[:], pr[:], rank[:], ALU.mult))
                    if rule == "four":
                        chain(v.tensor_reduce(m1[:], pr[:], AX.X, ALU.add))
                        chain(v.reciprocal(m1[:], m1[:]))
                        chain(v.tensor_tensor(pr[:], pr[:], b8(m1[:]), ALU.mult))
                    v.tensor_scalar(gates[:], pr[:], tgate, None, ALU.mult).then_inc(gates_ready, 1)
                v.wait_ge(gates_ready, 1)

                def biases(q):
                    v.wait_ge(gT_ready, q + 1)
                    v.tensor_copy(gT[:, CH * q:CH * (q + 1), :].rearrange("p t n -> p (t n)"),
                                  GB[0:E, :]).then_inc(gT_copied, 1)
                    v.wait_ge(bias_ready, q + 1)
                    xs = c.x[:, CH * q:CH * (q + 1), :].rearrange("p t n -> p (t n)")
                    v.tensor_tensor(xs, LB[:, :], xs, ALU.add).then_inc(bias_added, 1)
                    v.wait_ge(bias_added, q + 1)

                def stats(q, n, src):
                    for t in range(CH):
                        v.bn_stats(st[:, t, :], src(t)).then_inc(st_ready, 1)
                    v.wait_ge(st_ready, CH * (n + 1))
                    for t in range(CH):
                        v.bn_aggr(mv[:, t, :], st[:, t, :]).then_inc(mv_ready, 1)

                def normalise(q, n, src):
                    v.wait_ge(mv_ready, CH * (n + 1))
                    v.wait_ge(rstd_ready, 2 * (n + 1))
                    need(v, xT_ready, q)
                    for t in range(CH):
                        v.tensor_scalar(xn[:, t, :], src(t), mv[:, t, 0:1], rstd[:, t:t + 1], ALU.subtract,
                                        ALU.mult).then_inc(norm_sem(n), 1)

                def norm_sem(n):
                    return xn_ready if not double or n % 2 else xn1_ready

                def ln_step(q, i):
                    x1 = lambda t: c.x[:, CH * q + t, :]
                    x2 = lambda t: xn[:, t, :]
                    n = 2 * q if double else q
                    if i == 0:
                        stats(q, n, x1)
                    elif i == 1:
                        normalise(q, n, x1)
                        if double:
                            v.wait_ge(xn1_ready, CH * (q + 1))
                            stats(q, n + 1, x2)
                    elif double:
                        normalise(q, n + 1, x2)

                if w["b2"] is not None:
                    for q in range(NC):
                        biases(q)
                for k in range(len(K)):
                    q, g = K[k]
                    for e in range(per_group):
                        n = k * per_group + e
                        x = g * per_group + e
                        v.wait_ge(y_ready, n + 1)
                        need(v, added, 4 * n)
                        for t in range(CH):
                            xt = c.x[:, CH * q + t, :]
                            v.scalar_tensor_tensor(xt, YB[n % 2][:, t * D:(t + 1) * D], gates[:, CH * q + t, x:x + 1],
                                                   xt, ALU.mult, ALU.add).then_inc(added, 1)
                    if store:
                        continue
                    if g == groups - 1:
                        v.wait_ge(added, 4 * (k + 1) * per_group)
                        ln_step(q, 0)
                    elif g < 2 and q > 0:
                        ln_step(q - 1, g + 1)
                if not store:
                    ln_step(NC - 1, 1)
                    ln_step(NC - 1, 2)


def copy_ln(c, act, q, xT_ready, xnT_ready, bank, double):
    act.wait_ge(xT_ready, q + 1)
    dst = c.xnT[:, 4 * q:4 * (q + 1), :].rearrange("p t n -> p (t n)")
    if double:
        act.activation(dst, bank[:, :], ACT.Identity, bias=double[1], scale=double[0]).then_inc(xnT_ready, 1)
    else:
        act.copy(dst, bank[:, :]).then_inc(xnT_ready, 1)


def ternary_ffn(c, w, tgate):
    nc = c.nc
    FT = F // P
    CH = 4
    NC = NT // CH
    eps = 1e-6
    pre = "F1_"
    sem = lambda n: c.sublayer_sem(pre + n)
    xh_all, bias_ready = sem("x_high"), sem("bias_ready")
    (prep, prep_pe, xs_ready, up_ready, g_ready, st_ready, mv_ready, rs_ready, hn_ready, hT_ready, hh_ready, hl_ready,
     y_ready, y_copied, yT_ready, added, st2_ready, mv2_ready, rs2_ready, xn_ready, xT_ready, xnT_ready) = (
        sem(n) for n in (
            "weights_step", "weights_sums", "x_split", "up_ready", "gelu_ready", "h_stats", "h_mv", "h_rstd", "h_normed",
            "hT_ready", "h_high", "h_low", "down_ready", "down_copied", "down_turned", "added", "ln_stats", "ln_mv",
            "ln_rstd", "ln_xn", "ln_xT", "ln_xnT"))
    UB, HB, YB, TB, LB = c.banks[0:2], c.banks[2:4], c.banks[4], c.banks[5], c.banks[6]
    with ExitStack() as own:
        sb = lambda n, s, d=F32: own.enter_context(nc.sbuf_tensor(pre + n, s, d))
        tmp = sb("tmp", [P, 2, F])
        wf = sb("wf", [P, F], F32R)
        wp = sb("wp", [P, FT, D], F32R)
        sums = sb("sums", [P, 2])
        thr = sb("thr", [P, 2, 2])
        bias = sb("bias", [P, 1])
        xh = sb("xh", [P, NT, P], F32R)
        xl = sb("xl", [P, NT, P], F32R)
        hg = sb("hg", [P, 2, F])
        hn = sb("hn", [P, 2, F])
        hh = sb("hh", [P, 2, FT, CH, P], F32R)
        hl = sb("hl", [P, 2, FT, CH, P], F32R)
        yT = sb("yT", [P, F])
        st1 = sb("st1", [P, 6])
        mv1 = sb("mv1", [P, 2, 2])
        ve1 = sb("ve1", [P, 1])
        rs1 = sb("rs1", [P, 2, 1])
        ln = layer_norm_tail(c, own, pre)
        st, mv, ve, rstd, xn = (ln[k] for k in ("st", "mv", "ve", "rstd", "xn"))
        WF = w["WfT"]

        with nc.Block() as block:
            @block.tensor
            def _(pe):
                for s, all_loads in w["loaded"]:
                    pe.wait_ge(s, all_loads)
                pe.wait_ge(prep, 2)
                pe.matmul(LB[:, 0:2], c.ones[:], sums[:], start=True, stop=True).then_inc(prep_pe, 1)
                pe.wait_ge(prep, 8)
                for j in range(FT):
                    m = pe.matmul(TB[:, 0:1], wp[:, j, :].bitcast(F32), w["lnb"][:, j:j + 1],
                                  start=(j == 0), stop=(j == FT - 1))
                m.then_inc(prep_pe, 1)

                def up(t):
                    if t % CH == 0:
                        pe.wait_ge(xs_ready, t // CH + 1)
                    need(pe, g_ready, t - 1)
                    pe.matmul(UB[t % 2][:, :], xh[:, t, :], wf[:], start=True, stop=False)
                    pe.matmul(UB[t % 2][:, :], xl[:, t, :], wf[:], start=False, stop=True).then_inc(up_ready, 1)

                def turn(t):
                    pe.wait_ge(hn_ready, t + 1)
                    need(pe, hl_ready, t - 1)
                    for j in range(FT):
                        m = pe.transpose(HB[t % 2][:, j * P:(j + 1) * P], hn[:, t % 2, j * P:(j + 1) * P], c.ident[:])
                    m.then_inc(hT_ready, 1)

                def down(q):
                    pe.wait_ge(hl_ready, CH * (q + 1))
                    need(pe, y_copied, q)
                    n = 0
                    for part in (hh, hl):
                        for j in range(FT):
                            m = pe.matmul(YB[:, :], wp[:, j, :], part[:, q % 2, j].rearrange("p t n -> p (t n)"),
                                          start=(n == 0), stop=(n == 2 * FT - 1))
                            n += 1
                    m.then_inc(y_ready, 1)

                def turn_y(q):
                    pe.wait_ge(y_copied, q + 1)
                    need(pe, added, q)
                    if q == 0:
                        pe.wait_ge(bias_ready, 1)
                    for t in range(CH):
                        m = pe.transpose(TB[:, t * P:(t + 1) * P], yT[:, t * P:(t + 1) * P], c.ident[:])
                    m.then_inc(yT_ready, 1)

                def turn_ln(q):
                    pe.wait_ge(xn_ready, CH * (q + 1))
                    need(pe, xnT_ready, q)
                    for t in range(CH):
                        m = pe.transpose(LB[:, t * P:(t + 1) * P], xn[:, t, :], c.ident[:])
                    m.then_inc(xT_ready, 1)

                for t in range(NT + 15):
                    if t < NT:
                        up(t)
                    if 0 <= t - 2 < NT:
                        turn(t - 2)
                    if t - 4 >= 0 and (t - 4) % CH == CH - 1 and (t - 4) // CH < NC:
                        down((t - 4) // CH)
                    if t - 7 >= 0 and (t - 7) % CH == CH - 1 and (t - 7) // CH < NC:
                        turn_y((t - 7) // CH)
                    if t - 11 >= 0 and (t - 11) % CH == CH - 1 and (t - 11) // CH < NC:
                        turn_ln((t - 11) // CH)

            @block.scalar
            def _(act):
                for s, all_loads in w["loaded"]:
                    act.wait_ge(s, all_loads)
                act.copy(xh[:], c.xnT[:]).then_inc(xh_all, 1)
                act.wait_ge(prep_pe, 2)
                act.copy(bias[:], TB[:, 0:1]).then_inc(bias_ready, 1)
                for t in range(NT + 15):
                    if t < NT:
                        act.wait_ge(up_ready, t + 1)
                        need(act, hn_ready, t - 1)
                        act.activation(hg[:, t % 2, :], UB[t % 2][:, :], ACT.Gelu).then_inc(g_ready, 1)
                    if 0 <= t - 2 < NT:
                        n = t - 2
                        act.wait_ge(hT_ready, n + 1)
                        need(act, y_ready, n // CH - 1)
                        for j in range(FT):
                            i = act.activation(hh[:, n // CH % 2, j, n % CH, :], HB[n % 2][:, j * P:(j + 1) * P],
                                               ACT.Copy, scale=w["lnw"][:, j:j + 1])
                        i.then_inc(hh_ready, 1)
                    if t - 5 >= 0 and (t - 5) % CH == CH - 1 and (t - 5) // CH < NC:
                        q = (t - 5) // CH
                        act.wait_ge(y_ready, q + 1)
                        need(act, yT_ready, q)
                        if q == 0:
                            act.wait_ge(bias_ready, 1)
                        act.activation(yT[:], YB[:, :], ACT.Identity, bias=bias[:]).then_inc(y_copied, 1)
                    if t - 11 >= 0 and (t - 11) % CH == CH - 1 and (t - 11) // CH < NC:
                        copy_ln(c, act, (t - 11) // CH, xT_ready, xnT_ready, LB, None)

            @block.gpsimd
            def _(g):
                c.clear_spent(g)
                g.wait_ge(xh_all, 1)
                for q in range(NC):
                    s = slice(CH * q, CH * (q + 1))
                    g.tensor_tensor(xl[:, s, :], c.xnT[:, s, :], xh[:, s, :].bitcast(F32),
                                    ALU.subtract).then_inc(xs_ready, 1)
                for t in range(NT + 15):
                    if t < NT:
                        g.wait_ge(mv_ready, t + 1)
                        need(g, rs_ready, 2 * t)
                        g.tensor_scalar(ve1[:], mv1[:, t % 2, 1:2], LN_EPS, None, ALU.add).then_inc(rs_ready, 1)
                        g.wait_ge(rs_ready, 2 * t + 1)
                        g.tensor_tensor(rs1[:, t % 2], ve1[:], c.mhalf[:, 0:1], ALU.pow).then_inc(rs_ready, 1)
                    if t - 9 >= 0 and (t - 9) % CH == CH - 1 and (t - 9) // CH < NC:
                        q = (t - 9) // CH
                        g.wait_ge(mv2_ready, CH * (q + 1))
                        g.tensor_scalar(ve[:], mv[:, :, 1], LN_EPS, None, ALU.add).then_inc(rs2_ready, 1)
                        g.wait_ge(rs2_ready, 2 * q + 1)
                        g.tensor_tensor(rstd[:], ve[:], c.mhalf[:, 0:4], ALU.pow).then_inc(rs2_ready, 1)

            @block.vector
            def _(v):
                count = [0]

                def chain(i):
                    count[0] += 1
                    i.then_inc(prep, 1)
                    v.wait_ge(prep, count[0])

                for s, all_loads in w["loaded"]:
                    v.wait_ge(s, all_loads)
                chain(v.tensor_reduce(sums[:, 0:1], WF, AX.X, ALU.add, apply_absolute_value=True))
                chain(v.tensor_reduce(sums[:, 1:2], w["WpT"], AX.X, ALU.add, apply_absolute_value=True))
                v.wait_ge(prep_pe, 1)
                half = 0.5 / (D * F)
                chain(v.tensor_scalar(thr[:, 0], LB[:, 0:2], half, 0.5 * eps, ALU.mult, ALU.add))
                chain(v.tensor_scalar(thr[:, 1], thr[:, 0], -1.0, None, ALU.mult))
                chain(v.tensor_scalar(tmp[:, 0, :], WF, thr[:, 1, 0:1], None, ALU.is_lt))
                chain(v.scalar_tensor_tensor(wf[:], WF, thr[:, 0, 0:1], tmp[:, 0, :], ALU.is_gt, ALU.subtract))
                chain(v.tensor_scalar(tmp[:, 1, :], w["WpT"], thr[:, 1, 1:2], None, ALU.is_lt))
                chain(v.scalar_tensor_tensor(wp[:].rearrange("p j d -> p (j d)"), w["WpT"], thr[:, 0, 1:2], tmp[:, 1, :],
                                             ALU.is_gt, ALU.subtract))

                def low(n):
                    v.wait_ge(hh_ready, n + 1)
                    for j in range(FT):
                        i = v.scalar_tensor_tensor(hl[:, n // CH % 2, j, n % CH, :], HB[n % 2][:, j * P:(j + 1) * P],
                                                   w["lnw"][:, j:j + 1], hh[:, n // CH % 2, j, n % CH, :].bitcast(F32),
                                                   ALU.mult, ALU.subtract)
                    i.then_inc(hl_ready, 1)

                for t in range(NT + 15):
                    if t < NT:
                        v.wait_ge(g_ready, t + 1)
                        need(v, mv_ready, t)
                        v.bn_stats(st1[:], hg[:, t % 2, :]).then_inc(st_ready, 1)
                        v.wait_ge(st_ready, t + 1)
                        need(v, rs_ready, 2 * (t - 1) + 1)
                        v.bn_aggr(mv1[:, t % 2, :], st1[:]).then_inc(mv_ready, 1)
                    if 0 <= t - 1 < NT:
                        n = t - 1
                        v.wait_ge(rs_ready, 2 * n + 2)
                        need(v, hT_ready, n - 1)
                        v.tensor_scalar(hn[:, n % 2, :], hg[:, n % 2, :], mv1[:, n % 2, 0:1], rs1[:, n % 2, 0:1],
                                        ALU.subtract, ALU.mult).then_inc(hn_ready, 1)
                    if 0 <= t - 2 < NT:
                        low(t - 2)
                    if t - 7 >= 0 and (t - 7) % CH == CH - 1 and (t - 7) // CH < NC:
                        q = (t - 7) // CH
                        v.wait_ge(yT_ready, q + 1)
                        xs = c.x[:, CH * q:CH * (q + 1), :].rearrange("p t n -> p (t n)")
                        v.scalar_tensor_tensor(xs, TB[:, :], tgate, xs, ALU.mult, ALU.add).then_inc(added, 1)
                        v.wait_ge(added, q + 1)
                        for k in range(CH):
                            v.bn_stats(st[:, k, :], c.x[:, CH * q + k, :]).then_inc(st2_ready, 1)
                        v.wait_ge(st2_ready, CH * (q + 1))
                        for k in range(CH):
                            v.bn_aggr(mv[:, k, :], st[:, k, :]).then_inc(mv2_ready, 1)
                    if t - 10 >= 0 and (t - 10) % CH == CH - 1 and (t - 10) // CH < NC:
                        q = (t - 10) // CH
                        v.wait_ge(mv2_ready, CH * (q + 1))
                        v.wait_ge(rs2_ready, 2 * (q + 1))
                        need(v, xT_ready, q)
                        for k in range(CH):
                            v.tensor_scalar(xn[:, k, :], c.x[:, CH * q + k, :], mv[:, k, 0:1], rstd[:, k:k + 1],
                                            ALU.subtract, ALU.mult).then_inc(xn_ready, 1)


def wide_attention(c, w, gate, next_loads):
    nc = c.nc
    W64 = 64
    NP = H // 2
    M = B * NP
    SC = 0.125
    NPS, TRS, QKB, VB, OB, MISC = c.banks[0:2], c.banks[2:4], c.banks[4], c.banks[5], c.banks[6], c.banks[7]
    pre = "L1_"
    sem = lambda n: c.sublayer_sem(pre + n)
    (ct0, ct1, zeroed, gate_ready, qk_ready, hi_ready, lo_ready, n_ready, max_ready, p_ready, rc_ready, norm0_ready, norm1_ready,
     tr_ready, pt_even, pt_odd, pv_ready, o_ready, vp_ready, v_ready, po_ready, resid, st_ready, mv_ready, rstd_ready,
     xn_ready, xT_ready, xnT_ready) = (sem(n) for n in (
         "ctx_loaded0", "ctx_loaded1", "zeroed", "gate_ready", "qk_projected", "split_high", "split_low",
         "scores_ready", "max_ready", "exp_ready", "recip_ready", "probs_normed0", "probs_normed1", "probs_turned", "probsT_even", "probsT_odd",
         "pv_ready", "ctx_copied", "v_projected", "v_ready", "out_ready", "resid_ready", "ln_stats", "ln_mv",
         "ln_rstd", "ln_xn", "ln_xT", "ln_xnT"))
    ct_in = [ct0, ct1]
    wh_ready, wl_ready, th_ready, tl_ready = (sem(n) for n in ("weights_high", "weights_low", "tokens_high", "tokens_low"))
    CHUNKS = [("Wq", 0), ("Wk", 0), ("Wv", 0), ("Wv", 1), ("Wq", 1), ("Wk", 1)]
    with ExitStack() as own:
        sb = lambda n, s, d=F32: own.enter_context(nc.sbuf_tensor(pre + n, s, d))
        ct = sb("ct", [P, 2, S])
        qh = sb("qh", [P, 2, 2, S], F32R)
        ql = sb("ql", [P, 2, 2, S], F32R)
        kh = sb("kh", [P, 2, S], F32R)
        kl = sb("kl", [P, 2, S], F32R)
        split_w = {k: [sb(k + n, [P, H * W64], F32R) for n in ("h", "l")] for k in ("Wq", "Wk", "Wv")}
        tok = [sb("tokens_" + n, [P, 2, 2, S], F32R) for n in ("h", "l")]
        nm = sb("nm", [P, 4, TPB])
        sm = sb("sm", [P, 4, TPB])
        rs = sb("rs", [P, 4, TPB])
        pn = sb("pn", [P, 4, TPB, S])
        pt = sb("pt", [P, 4, TPB, S])
        vv = sb("vv", [P, 2, TPB, H * W64])
        oT = sb("oT", [P, 2, NP, S])
        g2 = sb("g2", [P, 1])
        st = sb("st", [P, TPB, 6])
        mv = sb("mv", [P, TPB, 2])
        ve = sb("ve", [P, TPB])
        rstd = sb("rstd", [P, TPB])
        xn = sb("xn", [P, TPB, D])

        with nc.Block() as block:
            @block.sync
            def _(sp):
                for b in range(B):
                    if b >= 2:
                        sp.wait_ge(tl_ready, 2 * (b - 1))
                    sp.dma_start(ct[:, b % 2, :], c.a["ctxT"][:, b * S:(b + 1) * S]).then_inc(ct_in[b % 2], 16)
                    if b == 1:
                        for s, dst, src in next_loads:
                            sp.dma_start(dst, src).then_inc(s, 16)

            @block.tensor
            def _(pe):
                def split_product(o, left, right):
                    pe.matmul(o, left[0], right[0], start=True, stop=False)
                    pe.matmul(o, left[0], right[1], start=False, stop=False)
                    return pe.matmul(o, left[1], right[0], start=False, stop=True)

                def wait_split(b, chunks):
                    pe.wait_ge(wh_ready, chunks)
                    pe.wait_ge(wl_ready, chunks)
                    pe.wait_ge(th_ready, 2 * (b + 1))
                    pe.wait_ge(tl_ready, 2 * (b + 1))

                def project(m):
                    b, p = divmod(m, NP)
                    need(pe, lo_ready, 3 * m)
                    wait_split(b, 2 if p < NP // 2 and b == 0 else len(CHUNKS))
                    part = lambda k: [x[:, p * P:(p + 1) * P] for x in split_w[k]]
                    split_product(QKB[:, 0:S], part("Wq"), [x[:, b % 2, 0, :] for x in tok])
                    split_product(QKB[:, S:2 * S], part("Wk"), [x[:, b % 2, 1, :] for x in tok]).then_inc(qk_ready, 1)

                def project_v(b, i):
                    t, half = divmod(i, 2)
                    need(pe, v_ready, 4 * b + i)
                    wait_split(b, 4)
                    split_product(VB[:, :], [x[:, b % 2, 1, t * P:(t + 1) * P] for x in tok],
                                  [x[:, half * 512:(half + 1) * 512] for x in split_w["Wv"]]).then_inc(vp_ready, 1)

                def scores(n):
                    m, s = divmod(n, 2)
                    if s == 0:
                        pe.wait_ge(lo_ready, 3 * (m + 1))
                    need(pe, p_ready, 2 * (n - 1))
                    for t in range(TPB):
                        o = NPS[n % 2][:, t * S:(t + 1) * S]
                        q = slice(t * P, (t + 1) * P)
                        pe.matmul(o, qh[:, m % 2, s, q], kh[:, m % 2, :], start=True, stop=False)
                        pe.matmul(o, qh[:, m % 2, s, q], kl[:, m % 2, :], start=False, stop=False)
                        i = pe.matmul(o, ql[:, m % 2, s, q], kh[:, m % 2, :], start=False, stop=True)
                    i.then_inc(n_ready, 1)

                def turn(n):
                    pe.wait_ge(norm0_ready, n + 1)
                    pe.wait_ge(norm1_ready, n + 1)
                    need(pe, (pt_even, pt_odd)[n % 2], n // 2)
                    for k in range(TPB):
                        for t in range(TPB):
                            i = pe.transpose(TRS[n % 2][:, k * S + t * P:k * S + (t + 1) * P],
                                             pn[:, n % 4, t, k * P:(k + 1) * P], c.ident[:])
                    i.then_inc(tr_ready, 1)

                def pv(m):
                    b, p = divmod(m, NP)
                    pe.wait_ge(pt_even, m + 1)
                    pe.wait_ge(pt_odd, m + 1)
                    need(pe, o_ready, m)
                    pe.wait_ge(v_ready, 4 * (b + 1))
                    for k in range(TPB):
                        for s in range(2):
                            h = 2 * p + s
                            i = pe.matmul(OB[W64 * s:W64 * (s + 1), 0:S], vv[:, b % 2, k, h * W64:(h + 1) * W64],
                                          pt[:, (2 * m + s) % 4, k, :], start=(k == 0), stop=(k == 1))
                    i.then_inc(pv_ready, 1)

                def out(b):
                    pe.wait_ge(o_ready, NP * (b + 1))
                    need(pe, xnT_ready, b)
                    for t in range(TPB):
                        o = MISC[:, t * D:(t + 1) * D]
                        for p in range(NP):
                            pe.matmul(o, oT[:, b % 2, p, t * P:(t + 1) * P], w["Wo"][:, p * D:(p + 1) * D],
                                      start=(p == 0), stop=False)
                        i = pe.matmul(o, c.ones[0:1, :], w["bo"], start=False, stop=True)
                    i.then_inc(po_ready, 1)

                def turn_ln(b):
                    pe.wait_ge(xn_ready, 2 * (b + 1))
                    for t in range(TPB):
                        i = pe.transpose(MISC[:, t * P:(t + 1) * P], xn[:, t, :], c.ident[:])
                    i.then_inc(xT_ready, 1)

                for s, all_loads in w["loaded"]:
                    pe.wait_ge(s, all_loads)
                project(0)
                for m in range(M + 8):
                    b, p = divmod(m, NP)
                    for s in range(2):
                        n = 2 * m + s
                        if m < M:
                            scores(n)
                        if s == 0 and m + 1 < M:
                            project(m + 1)
                        if m == 0 and s == 0:
                            for i in range(4):
                                project_v(0, i)
                        if 0 <= n - 3 < 2 * M:
                            turn(n - 3)
                        if s == 0 and 0 <= m - 3 < M:
                            pv(m - 3)
                    if 3 <= p < 7 and b + 1 < B:
                        project_v(b + 1, p - 3)
                    if m >= 12 and (m - 12) % NP == 0 and (m - 12) // NP < B:
                        out((m - 12) // NP)
                    if m >= 15 and (m - 15) % NP == 0 and (m - 15) // NP < B:
                        turn_ln((m - 15) // NP)

            @block.scalar
            def _(act):
                def split(m):
                    act.wait_ge(qk_ready, m + 1)
                    need(act, n_ready, 2 * (m - 1))
                    for s in range(2):
                        r = slice(W64 * s, W64 * (s + 1))
                        act.activation(qh[r, m % 2, s, :], QKB[r, 0:S], ACT.Copy, scale=SC).then_inc(hi_ready, 1)
                    act.copy(kh[:, m % 2, :], QKB[:, S:2 * S]).then_inc(hi_ready, 1)

                def copy_v(b, i):
                    t, half = divmod(i, 2)
                    act.wait_ge(vp_ready, 4 * b + i + 1)
                    need(act, pv_ready, NP * (b - 1))
                    act.copy(vv[:, b % 2, t, half * 512:(half + 1) * 512], VB[:, :]).then_inc(v_ready, 1)

                for s, all_loads in w["loaded"]:
                    act.wait_ge(s, all_loads)
                def token_high(b):
                    act.wait_ge(ct_in[b % 2], 16 * (b // 2 + 1))
                    need(act, qk_ready, NP * (b - 1))
                    need(act, vp_ready, 4 * (b - 1))
                    act.copy(tok[0][:, b % 2, 0, :],
                             c.xnT[:, TPB * b:TPB * (b + 1), :].rearrange("p t n -> p (t n)")).then_inc(th_ready, 1)
                    act.copy(tok[0][:, b % 2, 1, :], ct[:, b % 2, :]).then_inc(th_ready, 1)

                def weight_high(n):
                    k, half = CHUNKS[n]
                    cols = slice(half * 512, (half + 1) * 512)
                    act.copy(split_w[k][0][:, cols], w[k][:, cols]).then_inc(wh_ready, 1)

                weight_high(0)
                weight_high(1)
                token_high(0)
                act.activation(g2[:], w["gate"], ACT.Tanh).then_inc(gate_ready, 1)
                act.wait_ge(gate_ready, 1)
                act.activation(g2[:], g2[:], ACT.Copy, scale=gate).then_inc(gate_ready, 1)
                act.wait_ge(zeroed, 2)
                split(0)
                for n in range(2, len(CHUNKS)):
                    weight_high(n)
                for m in range(M + 8):
                    b, p = divmod(m, NP)
                    for s in range(2):
                        n = 2 * m + s
                        if s == 0 and m + 1 < M:
                            split(m + 1)
                        if s == 1 and 0 <= n - 4 < 2 * M:
                            k = n - 4
                            act.wait_ge(tr_ready, k + 1)
                            need(act, pv_ready, k // 2 - 1)
                            act.copy(pt[:, k % 4].rearrange("p t n -> p (t n)"), TRS[k % 2][:, :]).then_inc(pt_odd, 1)
                        if m < M:
                            act.wait_ge(max_ready, n + 1)
                            need(act, tr_ready, n - 3)
                            for t in range(TPB):
                                act.activation(pn[:, n % 4, t, :], NPS[n % 2][:, t * S:(t + 1) * S], ACT.Exp,
                                               bias=nm[:, n % 4, t:t + 1],
                                               accum_out=sm[:, n % 4, t:t + 1]).then_inc(p_ready, 1)
                        if m == 0 and s == 0:
                            for i in range(4):
                                copy_v(0, i)
                        if s == 0 and 0 <= m - 3 < M:
                            k = m - 3
                            act.wait_ge(pv_ready, k + 1)
                            if k % NP == 0:
                                need(act, po_ready, k // NP - 1)
                            act.copy(oT[:, k // NP % 2, k % NP, :], OB[:, 0:S]).then_inc(o_ready, 1)
                    if p == 1 and b + 1 < B:
                        token_high(b + 1)
                    if 3 <= p < 7 and b + 1 < B:
                        copy_v(b + 1, p - 3)
                    if m >= 15 and (m - 15) % NP == 0 and (m - 15) // NP < B:
                        k = (m - 15) // NP
                        act.wait_ge(xT_ready, k + 1)
                        act.copy(c.xnT[:, TPB * k:TPB * (k + 1), :].rearrange("p t n -> p (t n)"),
                                 MISC[:, 0:S]).then_inc(xnT_ready, 1)

            @block.gpsimd
            def _(g):
                c.clear_spent(g)
                def token_low(b):
                    g.wait_ge(th_ready, 2 * (b + 1))
                    need(g, qk_ready, NP * (b - 1))
                    need(g, vp_ready, 4 * (b - 1))
                    g.tensor_tensor(tok[1][:, b % 2, 0, :],
                                    c.xnT[:, TPB * b:TPB * (b + 1), :].rearrange("p t n -> p (t n)"),
                                    tok[0][:, b % 2, 0, :].bitcast(F32), ALU.subtract).then_inc(tl_ready, 1)
                    g.tensor_tensor(tok[1][:, b % 2, 1, :], ct[:, b % 2, :], tok[0][:, b % 2, 1, :].bitcast(F32),
                                    ALU.subtract).then_inc(tl_ready, 1)

                g.memset(ql[:].bitcast(F32), 0.0).then_inc(zeroed, 1)
                token_low(0)
                for m in range(M + 8):
                    if m % NP == 2 and m // NP + 1 < B:
                        token_low(m // NP + 1)
                    for s in range(2):
                        n = 2 * m + s
                        if m < M:
                            g.wait_ge(rc_ready, n + 1)
                            g.tensor_scalar(pn[:, n % 4, 0, :], pn[:, n % 4, 0, :], rs[:, n % 4, 0:1], None,
                                            ALU.mult).then_inc(norm0_ready, 1)
                    if m >= 13 and (m - 13) % NP == 0 and (m - 13) // NP < B:
                        k = (m - 13) // NP
                        g.wait_ge(mv_ready, 2 * (k + 1))
                        g.tensor_scalar(ve[:], mv[:, :, 1], LN_EPS, None, ALU.add).then_inc(rstd_ready, 1)
                        g.wait_ge(rstd_ready, 2 * k + 1)
                        g.tensor_tensor(rstd[:], ve[:], c.mhalf[:, 0:TPB], ALU.pow).then_inc(rstd_ready, 1)

            @block.vector
            def _(v):
                def split(m):
                    v.wait_ge(hi_ready, 3 * (m + 1))
                    for s in range(2):
                        r = slice(W64 * s, W64 * (s + 1))
                        v.scalar_tensor_tensor(ql[r, m % 2, s, :], QKB[r, 0:S], SC, qh[r, m % 2, s, :].bitcast(F32),
                                               ALU.mult, ALU.subtract).then_inc(lo_ready, 1)
                    v.tensor_tensor(kl[:, m % 2, :], QKB[:, S:2 * S], kh[:, m % 2, :].bitcast(F32),
                                    ALU.subtract).then_inc(lo_ready, 1)

                def recip(n):
                    v.wait_ge(p_ready, 2 * (n + 1))
                    v.reciprocal(rs[:, n % 4, :], sm[:, n % 4, :]).then_inc(rc_ready, 1)

                v.memset(qh[:].bitcast(F32), 0.0).then_inc(zeroed, 1)
                for s, all_loads in w["loaded"]:
                    v.wait_ge(s, all_loads)
                def weight_low(n):
                    k, half = CHUNKS[n]
                    cols = slice(half * 512, (half + 1) * 512)
                    v.wait_ge(wh_ready, n + 1)
                    v.tensor_tensor(split_w[k][1][:, cols], w[k][:, cols], split_w[k][0][:, cols].bitcast(F32),
                                    ALU.subtract).then_inc(wl_ready, 1)

                weight_low(0)
                weight_low(1)
                v.wait_ge(zeroed, 2)
                split(0)
                for n in range(2, len(CHUNKS)):
                    weight_low(n)
                for m in range(M + 8):
                    for s in range(2):
                        n = 2 * m + s
                        if m < M:
                            v.wait_ge(n_ready, n + 1)
                            v.tensor_reduce(nm[:, n % 4, :], NPS[n % 2][:, :].rearrange("p (t n) -> p t n", t=TPB),
                                            AX.X, ALU.max, negate=True).then_inc(max_ready, 1)
                        if 0 <= n - 1 < 2 * M:
                            recip(n - 1)
                        if 0 <= n - 1 < 2 * M:
                            k = n - 1
                            v.wait_ge(rc_ready, k + 1)
                            v.tensor_scalar(pn[:, k % 4, 1, :], pn[:, k % 4, 1, :], rs[:, k % 4, 1:2], None,
                                            ALU.mult).then_inc(norm1_ready, 1)
                        if s == 0 and 0 <= n - 4 < 2 * M:
                            k = n - 4
                            v.wait_ge(tr_ready, k + 1)
                            need(v, pv_ready, k // 2 - 1)
                            v.tensor_copy(pt[:, k % 4].rearrange("p t n -> p (t n)"), TRS[k % 2][:, :]).then_inc(pt_even, 1)
                        if s == 0 and m + 1 < M:
                            split(m + 1)
                    if m >= 12 and (m - 12) % NP == 0 and (m - 12) // NP < B:
                        k = (m - 12) // NP
                        v.wait_ge(po_ready, k + 1)
                        if k == 0:
                            v.wait_ge(gate_ready, 2)
                        xs = c.x[:, TPB * k:TPB * (k + 1), :].rearrange("p t n -> p (t n)")
                        v.scalar_tensor_tensor(xs, MISC[:, 0:S], g2[:, 0:1], xs, ALU.mult, ALU.add).then_inc(resid, 1)
                        v.wait_ge(resid, k + 1)
                        for t in range(TPB):
                            v.bn_stats(st[:, t, :], c.x[:, TPB * k + t, :]).then_inc(st_ready, 1)
                        v.wait_ge(st_ready, 2 * (k + 1))
                        for t in range(TPB):
                            v.bn_aggr(mv[:, t, :], st[:, t, :]).then_inc(mv_ready, 1)
                    if m >= 14 and (m - 14) % NP == 0 and (m - 14) // NP < B:
                        k = (m - 14) // NP
                        v.wait_ge(mv_ready, 2 * (k + 1))
                        v.wait_ge(rstd_ready, 2 * (k + 1))
                        need(v, xT_ready, k)
                        for t in range(TPB):
                            v.tensor_scalar(xn[:, t, :], c.x[:, TPB * k + t, :], mv[:, t, 0:1], rstd[:, t:t + 1],
                                            ALU.subtract, ALU.mult).then_inc(xn_ready, 1)


def draw_mask(g, mask, window, made):
    W = P + window
    g.memset(mask[:], 0.0).then_inc(made, 1)
    n = 1
    for t in range(TPB):
        off = window * t
        for base, sign in ((window + off, -1), (window - off, 1)):
            g.wait_ge(made, n)
            g.affine_select(out=mask[:, t, :], in_=mask[:, t, :], compare_op=ALU.is_ge, fill=NEG, base=base,
                            pattern=[[sign, W]], channel_multiplier=-sign).then_inc(made, 1)
            n += 1


def program(nc, a, out):
    with ExitStack() as ctx:
        c = Chip(nc, ctx, a)
        stored = c.sem("stored")
        at_start, after_experts0, after_ternary = [], [], []
        FT0, FT = -(-F0 // P), F // P
        early, middle = (c.sb("place_" + n, [P, 2 * E * F], F32) for n in ("early", "middle"))

        class Weights(dict):

            def __init__(self, name):
                super().__init__()
                self.name, self.sem, self.count = name, c.sem(name + "_loaded"), 0

            def load(self, key, shape, src, place=None, when=at_start):
                self[key] = c.sb(f"{self.name}_{key}", shape, F32)[:] if place is None else place
                self.count += 16
                when.append((self.sem, self[key], src))
                self["loaded"] = [(self.sem, self.count)]

            def load_all(self, prefix, shapes):
                for key, shape in shapes.items():
                    self.load(key, shape, a[prefix + key])

        wide = lambda name: a[name].partition_broadcast(P)
        square = lambda *keys: {k: [P, P] for k in keys}

        mask = c.sb("window_mask", [P, TPB, P + WINDOW], BF16)
        att0 = Weights("att0")
        att0.load_all("L0_", square("WqT", "WkT", "WvT", "WoT"))
        att0.load("bq", [P, 1], col(a["L0_bq"]))
        att0.load("bk", [P, 1], col(a["L0_bk"]))
        att0.load("bv", [P, D], wide("L0_bv"))
        att0.load("bo", [1, D], row(a["L0_bo"]))
        att0["mask"] = mask

        experts0 = Weights("experts0")
        experts0.load("Wr", [P, E], a["F0_Wr"])
        experts0.load("br", [P, E], wide("F0_br"))
        n = E // GROUP0 * FT0 * P
        experts0.load("W1", None, a["F0_W1"], early[:, 0:n])
        experts0.load("W2", None, a["F0_W2"], early[:, n:n + E * FT0 * D])
        experts0.load("b1", [P, E // GROUP0 * FT0], a["F0_b1"])
        experts0.load("b2", [E, D], a["F0_b2"])
        experts0.load_all("", square("same_expert", "earlier_tile"))
        experts0.load("ln", [P, 2], a["L1_ln"])

        att1 = Weights("att1")
        for k, (key, src) in enumerate((("Wq", a["L1_Wq"]), ("Wk", a["L1_Wkv"][:, 0:INNER]),
                                        ("Wv", a["L1_Wkv"][:, INNER:2 * INNER]), ("Wo", a["L1_Wo"]))):
            att1.load(key, None, src, middle[:, k * INNER:(k + 1) * INNER])
        att1.load("bo", [1, D], row(a["L1_bo"]))
        att1.load("gate", [P, 1], wide("L1_gate"))

        ternary = Weights("ternary")
        for k, key in enumerate(("WfT", "WpT")):
            ternary.load(key, None, a["F1_" + key], middle[:, 4 * INNER + k * F:4 * INNER + (k + 1) * F])
        ternary.load_all("F1_", {"lnw": [P, FT], "lnb": [P, FT]})

        att2 = Weights("att2")
        att2.load_all("L2_", square("WqT", "WkT", "WkTs", "WoT", "WvT", "WvTs"))
        att2.load("bo", [1, D], row(a["L2_bo"]))
        att2.load("cosT", [P, S], a["rope_cosT"])
        att2.load("sinT", [P, S], a["rope_sinT"])
        att2.load("cs", [P, 2, TPB, D], a["rope_cs"])
        att2["bq"] = 0.0

        experts2, experts3 = Weights("experts2"), Weights("experts3")
        for w, p, place, when in ((experts2, "F2_", middle, after_ternary), (experts3, "F3_", early, after_experts0)):
            w.load("Wr", [P, E], a[p + "Wr"])
            w.load("before", [P, E * E], wide("before"))
            w.load("W1", None, a[p + "W1"], place[:, 0:E * F], when)
            w.load("W2", None, a[p + "W2"], place[:, E * F:2 * E * F], when)
        experts2.load("br", [P, E], wide("F2_br"))
        experts2.load("b1", [P, E * FT], a["F2_b1"])
        experts2.load("b2", [E, D], a["F2_b2"])
        experts3.update(br=None, b1=None, b2=None)

        att3 = Weights("att3")
        att3.load_all("L3_", square("WqT", "WvT", "WoT"))
        att3.load("bo", [1, D], row(a["L3_bo"]))
        att3.update(WkT=att3["WqT"], bq=0.0, bk=0.0, bv=None, mask=mask)

        gate_att = lambda layer: c.gates_t[:, layer:layer + 1]
        gate_ffn = lambda layer: c.gates_t[:, 4 + layer:5 + layer]
        start_block(c, at_start, mask)
        attention(c, 0, att0, gate_att(0), window=WINDOW)
        c.end_sublayer()
        ffn(c, 0, experts0, F0, gate_ffn(0), GROUP0, ACT.Silu, "experts",
            double=(experts0["ln"][:, 0:1], experts0["ln"][:, 1:2]))
        c.end_sublayer()
        wide_attention(c, att1, gate_att(1), after_experts0)
        c.end_sublayer()
        ternary_ffn(c, ternary, gate_ffn(1))
        c.end_sublayer()
        attention(c, 2, att2, gate_att(2), rope=True, next_loads=after_ternary)
        c.end_sublayer()
        ffn(c, 2, experts2, F, gate_ffn(2), 1, ACT.Gelu, "first")
        c.end_sublayer()
        attention(c, 3, att3, gate_att(3), window=WINDOW)
        c.end_sublayer()
        ffn(c, 3, experts3, F, gate_ffn(3), 1, ACT.Gelu_apprx_tanh, "four", store=(out, stored))


def feature_first(w):
    return w.reshape(*w.shape[:-1], 2, HU, DH).swapaxes(-1, -2).reshape(w.shape)


def layout(i):
    o = {}
    tiles = lambda x: np.ascontiguousarray(x.reshape(NT, P, D).transpose(1, 0, 2))
    o["x"] = tiles(i["x"])
    o["ctxT"] = i["ctx_1024"].reshape(B * S, D).T
    o["g_xattn"], o["g_ffn"] = i["g_xattn"], i["g_ffn"]
    o["L0_WqT"] = feature_first(i["L0_xattn_Wq"].T)
    o["L0_WkT"] = feature_first(i["L0_xattn_Wk"].T)
    o["L0_WvT"] = i["L0_xattn_Wv"].T
    o["L0_WoT"] = i["L0_xattn_Wo"].T
    o["L0_bq"] = feature_first(i["L0_xattn_bq"])
    o["L0_bk"] = feature_first(i["L0_xattn_bk"])
    o["L0_bv"], o["L0_bo"] = i["L0_xattn_bv"], i["L0_xattn_bo"]
    f_tiles = lambda v, n: np.pad(v, [(0, 0), (0, -n % P)] + [(0, 0)] * (v.ndim - 2))
    for L, p, hidden in ((0, "L0_ffn_", F0), (2, "L2_ffn_", F), (3, "L3_ffn_", F)):
        n = {0: ("Wr", "W_up", "W_down"), 2: ("Wr", "W1", "W2"), 3: ("router_w", "up_w", "down_w")}[L]
        wr, w1, w2 = (i[p + k] for k in n)
        o[f"F{L}_Wr"] = wr
        o[f"F{L}_W1"] = np.pad(w1.transpose(1, 0, 2), [(0, 0), (0, 0), (0, -hidden % P)]).reshape(D, -1)
        w2 = f_tiles(w2, hidden)
        o[f"F{L}_W2"] = w2.reshape(8, -1, P, D).transpose(2, 0, 1, 3).reshape(P, -1)
    for L, p, hidden, br, b1, b2 in ((0, "L0_ffn_", F0, "br", "b_up", "b_down"), (2, "L2_ffn_", F, "br", "b1", "b2")):
        o[f"F{L}_br"] = i[p + br]
        o[f"F{L}_b1"] = f_tiles(i[p + b1], hidden).reshape(-1, P).T
        o[f"F{L}_b2"] = i[p + b2]
    o["L1_Wq"], o["L1_Wkv"] = i["L1_xattn_w_q"], i["L1_xattn_w_kv"]
    o["L1_Wo"] = i["L1_xattn_w_out"].reshape(8, P, D).transpose(1, 0, 2).reshape(P, -1)
    o["L1_bo"], o["L1_gate"] = i["L1_xattn_b_out"], i["L1_xattn_gate"]
    o["F1_WfT"] = i["L1_ffn_W_fc"].T
    o["F1_WpT"] = i["L1_ffn_W_proj"].T.reshape(4, P, D).transpose(1, 0, 2).reshape(P, -1)
    o["F1_lnw"] = i["L1_ffn_ln_w"].reshape(4, P).T
    o["F1_lnb"] = i["L1_ffn_ln_b"].reshape(4, P).T
    turned = lambda w: np.stack([w[..., 1::2], w[..., 0::2]], -1).reshape(w.shape)
    o["L2_WqT"] = feature_first(i["L2_xattn_Wq"].T)
    o["L2_WkT"] = feature_first(i["L2_xattn_Wk"].T)
    o["L2_WkTs"] = feature_first(turned(i["L2_xattn_Wk"].T))
    o["L2_WvT"] = i["L2_xattn_Wv"].T
    o["L2_WvTs"] = turned(i["L2_xattn_Wv"].T)
    o["L2_WoT"], o["L2_bo"] = i["L2_xattn_Wp"].T, i["L2_xattn_bp"]
    half = D // 2
    theta = (1.0 / np.float32(10000.0) ** (np.float32(2.0) * np.arange(half, dtype=np.float32) / np.float32(D))).astype(np.float32)
    ang = np.arange(S, dtype=np.float32)[:, None] * theta[None, :]
    cos, sin = (np.repeat(f(ang), 2, axis=1).astype(np.float32) for f in (np.cos, np.sin))
    sin[:, 0::2] *= np.float32(-1.0)
    o["rope_cosT"], o["rope_sinT"] = feature_first(cos).T, feature_first(sin).T
    o["rope_cs"] = np.stack([cos, sin]).reshape(2, TPB, P, D).transpose(2, 0, 1, 3)
    eye = np.eye(P, dtype=np.float32)
    o["L3_WqT"], o["L3_WvT"] = feature_first(eye), eye
    o["L3_WoT"], o["L3_bo"] = i["L3_xattn_W_proj"].T, i["L3_xattn_b_proj"]
    e = np.arange(P) % 8
    t = np.arange(P) // 8
    o["same_expert"] = (e[:, None] == e[None, :]).astype(np.float32)
    o["earlier_tile"] = ((e[:, None] == e[None, :]) & (t[:, None] < t[None, :])).astype(np.float32)
    o["before"] = (np.arange(8)[None, :] < np.arange(8)[:, None]).astype(np.float32).reshape(-1)
    o["L1_ln"] = np.stack([i["L1_xattn_ln_gamma"], i["L1_xattn_ln_beta"]], 1)
    return {k: np.ascontiguousarray(v) for k, v in o.items()}


def kernel(**inputs):
    import concourse.bacc as bacc
    from concourse.bass_utils import run_bass_kernel_spmd

    arrays = layout({k: np.asarray(v) for k, v in inputs.items()})
    nc = bacc.Bacc("TRN2", target_bir_lowering=False, num_devices=1)
    aps = {k: nc.dram_tensor("in_" + k, v.shape, F32, kind="ExternalInput").ap() for k, v in arrays.items()}
    out = nc.dram_tensor("out", (P, NT, D), F32, kind="ExternalOutput").ap()
    program(nc, aps, out)
    r = run_bass_kernel_spmd(nc, [{"in_" + k: v for k, v in arrays.items()}], core_ids=[0])
    y = r.results[0]["out"]
    return np.ascontiguousarray(y.transpose(1, 0, 2)).reshape(B, S, D)
```
